# Optimizing a Trainium2 kernel written in Bass

```python
import numpy as np
import jax
import jax.numpy as jnp

def _softmax(x, axis=-1):
    return jax.nn.softmax(x, axis=axis)

def _gelu(x):
    return jax.nn.gelu(x, approximate=True)

def _silu(x):
    return jax.nn.silu(x)

def _sigmoid(x):
    return jax.nn.sigmoid(x)

def _layernorm(x, axis=-1, eps=1e-05):
    m = jnp.mean(x, axis=axis, keepdims=True)
    v = jnp.var(x, axis=axis, keepdims=True)
    return (x - m) / jnp.sqrt(v + eps)

def _scatter_add(tgt, idx, src, axis=0):
    return tgt.at[idx].add(src)

def _segment_sum(src, seg, n):
    return jax.ops.segment_sum(src, seg, n)
kernel_name = 'mk_early_fusion_embed_d2_tok_img768_r4_eb89cf'

def setup_inputs(seed: int=0):
    np.random.seed(seed)
    _w = jnp.asarray

    def _rec_inputs():
        import jax
        import jax.numpy as jnp
        _rk = jax.random.key(seed)
        x = -0.000356955 + 1 * jax.random.normal(jax.random.fold_in(_rk, 1), (8, 3, 128, 128), jnp.float32)
        x_txt = jax.random.randint(jax.random.fold_in(_rk, 51), (8, 77), 0, 12564, jnp.int32)
        return (x, x_txt)
    x, x_txt = _rec_inputs()

    def _L0_tok_setup():
        import jax, jax.numpy as jnp
        import numpy as np
        PATCH = 16
        EMBED = 192
        IN_DIM = PATCH * PATCH * 3

        def extract_patches(x, p):
            B, C, H, Wd = x.shape
            h, w = (H // p, Wd // p)
            xr = x.reshape(B, C, h, p, w, p)
            xr = xr.transpose(0, 2, 4, 3, 5, 1)
            return xr.reshape(B, h * w, p * p * C)
        key = jax.random.key(seed)
        kx, kw, kb = jax.random.split(key, 3)
        x = jax.random.normal(kx, (128, 3, 224, 224), dtype=jnp.float32)
        bound = 1.0 / np.sqrt(IN_DIM)
        W = jax.random.uniform(kw, (EMBED, IN_DIM), jnp.float32, -bound, bound)
        b = jax.random.uniform(kb, (EMBED,), jnp.float32, -bound, bound)
        return {'x': x, 'W': W, 'b': b}
    _L0_tok_all = _L0_tok_setup()
    _L0_tok_in = {k: v for k, v in _L0_tok_all.items() if k in ('W', 'b')}
    del _L0_tok_all

    def _L0_txt_setup():
        import jax, jax.numpy as jnp
        import numpy as np
        B, T, V, C = (8, 512, 50257, 192)

        def _rosa(x):
            Bx, Tx = x.shape
            eq = (x[:, :, None] == x[:, None, :]).astype(jnp.int32)

            def step(prev, eq_row):
                cur = (jnp.pad(prev[:, :-1], ((0, 0), (1, 0))) + 1) * eq_row
                return (cur, cur)
            init = jnp.zeros((Bx, Tx), jnp.int32)
            _, rows = jax.lax.scan(step, init, jnp.swapaxes(eq, 0, 1)[1:])
            L = jnp.swapaxes(jnp.concatenate([init[None], rows], axis=0), 0, 1)
            mask = jnp.tril(jnp.ones((Tx, Tx), dtype=bool), -1)
            j = jnp.arange(Tx, dtype=jnp.float32)
            TIE = 1e-05
            scored = jnp.where(mask[None], L.astype(jnp.float32) + j[None, None, :] * TIE, -1.0)
            best_j = jnp.argmax(scored, axis=2)
            pred_idx = jnp.minimum(best_j + 1, Tx - 1)
            preds = jnp.take_along_axis(x, pred_idx, axis=1)
            no_match = jnp.max(jnp.where(mask[None], L, 0), axis=2) == 0
            return jnp.where(no_match, -1, preds)
        key = jax.random.key(seed)
        k1, k2 = jax.random.split(key)
        idx = jax.random.randint(k1, (B, T), 0, V)
        emb = jax.random.normal(k2, (V, C), dtype=jnp.float32)
        return {'idx': idx, 'emb': emb}
    _L0_txt_all = _L0_txt_setup()
    _L0_txt_in = {k: v for k, v in _L0_txt_all.items() if k in ('emb',)}
    del _L0_txt_all

    def _L0_attn_setup():
        import jax, jax.numpy as jnp
        import numpy as np
        D_MODEL = 192
        D_STATE = 16
        D_CONV = 4
        EXPAND = 2
        HEADDIM = 64
        D_INNER = EXPAND * D_MODEL
        NHEADS = D_INNER // HEADDIM
        CONV_DIM = D_INNER + 2 * D_STATE
        D_IN_PROJ = 2 * D_INNER + 2 * D_STATE + NHEADS
        BATCH, SEQ = (4, 512)

        def _mamba_params(key, scale=0.02):
            ks = jax.random.split(key, 5)
            return dict(in_w=jax.random.normal(ks[0], (D_MODEL, D_IN_PROJ), jnp.float32) * scale, conv_w=jax.random.normal(ks[1], (CONV_DIM, D_CONV), jnp.float32) * scale, conv_b=jnp.zeros((CONV_DIM,), jnp.float32), dt_bias=jax.random.normal(ks[2], (NHEADS,), jnp.float32) * 0.1, A_log=jnp.log(jax.random.uniform(ks[3], (NHEADS,), jnp.float32, 1.0, 16.0)), D=jnp.ones((NHEADS,), jnp.float32), norm_w=jnp.ones((D_INNER,), jnp.float32), out_w=jax.random.normal(ks[4], (D_INNER, D_MODEL), jnp.float32) * scale)

        def _layernorm(x, w, b, eps=1e-05):
            m = jnp.mean(x, -1, keepdims=True)
            v = jnp.mean((x - m) ** 2, -1, keepdims=True)
            return (x - m) * jax.lax.rsqrt(v + eps) * w + b

        def _mamba2(u, in_w, conv_w, conv_b, dt_bias, A_log, D, norm_w, out_w):
            b, l, _ = u.shape
            zxbcdt = u @ in_w
            z = zxbcdt[..., :D_INNER]
            xBC = zxbcdt[..., D_INNER:D_INNER + CONV_DIM]
            dt = jax.nn.softplus(zxbcdt[..., -NHEADS:] + dt_bias)
            xpad = jnp.pad(xBC, ((0, 0), (D_CONV - 1, 0), (0, 0)))
            xc = sum((conv_w[:, k] * xpad[:, k:k + l, :] for k in range(D_CONV))) + conv_b
            xc = jax.nn.silu(xc)
            xh = xc[..., :D_INNER].reshape(b, l, NHEADS, HEADDIM)
            Bm = xc[..., D_INNER:D_INNER + D_STATE]
            Cm = xc[..., D_INNER + D_STATE:]
            A = -jnp.exp(A_log)
            dA = jnp.exp(dt * A)

            def step(h, inp):
                dA_t, dt_t, B_t, C_t, x_t = inp
                h = h * dA_t[:, :, None, None] + (dt_t[:, :, None] * x_t)[..., None] * B_t[:, None, None, :]
                y = jnp.einsum('bhpn,bn->bhp', h, C_t)
                return (h, y)
            h0 = jnp.zeros((b, NHEADS, HEADDIM, D_STATE), u.dtype)
            xs = (dA.transpose(1, 0, 2), dt.transpose(1, 0, 2), Bm.transpose(1, 0, 2), Cm.transpose(1, 0, 2), xh.transpose(1, 0, 2, 3))
            _, ys = jax.lax.scan(step, h0, xs)
            y = ys.transpose(1, 0, 2, 3) + D[None, None, :, None] * xh
            y = y.reshape(b, l, D_INNER)
            yz = y * jax.nn.silu(z)
            yz = yz * jax.lax.rsqrt(jnp.mean(yz * yz, -1, keepdims=True) + 1e-05) * norm_w
            return yz @ out_w
        key = jax.random.key(seed)
        kx, kf, kb, k1, k2 = jax.random.split(key, 5)
        f = _mamba_params(kf)
        b = _mamba_params(kb)
        k1a, k1b = jax.random.split(k1)
        inp = {'x': jax.random.normal(kx, (BATCH, SEQ, D_MODEL), jnp.float32), 'ln1_w': jnp.ones((D_MODEL,), jnp.float32), 'ln1_b': jnp.zeros((D_MODEL,), jnp.float32), 'ln2_w': jnp.ones((D_MODEL,), jnp.float32), 'ln2_b': jnp.zeros((D_MODEL,), jnp.float32), 'ffn_w1': jax.random.normal(k1a, (2 * D_MODEL, 4 * D_MODEL), jnp.float32) * 0.02, 'ffn_b1': jnp.zeros((4 * D_MODEL,), jnp.float32), 'ffn_w2': jax.random.normal(k1b, (4 * D_MODEL, D_MODEL), jnp.float32) * 0.02, 'ffn_b2': jnp.zeros((D_MODEL,), jnp.float32)}
        for name, p in (('f', f), ('b', b)):
            for k, v in p.items():
                inp[name + '_' + k] = v
        return inp
    _L0_attn_all = _L0_attn_setup()
    _L0_attn_in = {k: v for k, v in _L0_attn_all.items() if k in ('ln1_w', 'ln1_b', 'ln2_w', 'ln2_b', 'f_in_w', 'f_conv_w', 'f_conv_b', 'f_dt_bias', 'f_A_log', 'f_D', 'f_norm_w', 'f_out_w', 'b_in_w', 'b_conv_w', 'b_conv_b', 'b_dt_bias', 'b_A_log', 'b_D', 'b_norm_w', 'b_out_w', 'ffn_w1', 'ffn_b1', 'ffn_w2', 'ffn_b2')}
    del _L0_attn_all

    def _L0_ffn_setup():
        import jax, jax.numpy as jnp
        import numpy as np
        LN2 = jnp.log(jnp.float32(2.0))
        ALPHA = 0.5
        A_BITS = 8
        W_BITS = 8
        EPS = 1e-08

        def round_ln(x):
            y = jnp.floor(jnp.log(x) / LN2)
            up = x - 2.0 ** y > 2.0 ** (y + 1.0) - x
            return y + up.astype(x.dtype)

        def fq_act_asym(x, bits=A_BITS):
            qmax = 2 ** bits - 1
            xmin = jnp.minimum(x.min(), 0.0)
            xmax = jnp.maximum(x.max(), 0.0)
            scale = jnp.maximum((xmax - xmin) / qmax, EPS)
            zp = jnp.round(-xmin / scale)
            q = jnp.clip(jnp.round(x / scale) + zp, 0, qmax)
            return (q - zp) * scale

        def fq_act_sym(x, bits=A_BITS):
            qmax = 2 ** (bits - 1) - 1
            scale = jnp.maximum(jnp.abs(x).max() / qmax, EPS)
            q = jnp.clip(jnp.round(x / scale), -qmax - 1, qmax)
            return q * scale

        def fq_weight(w, bits=W_BITS):
            qmax = 2 ** (bits - 1) - 1
            scale = jnp.maximum(jnp.abs(w).max(axis=1, keepdims=True) / qmax, EPS)
            q = jnp.clip(jnp.round(w / scale), -qmax - 1, qmax)
            return q * scale
        key = jax.random.key(seed)
        ks = jax.random.split(key, 5)
        B, N, C, H = (64, 197, 192, 768)
        x = jax.random.normal(ks[0], (B, N, C), dtype=jnp.float32)
        w1 = jax.random.normal(ks[1], (H, C), dtype=jnp.float32) * 0.02
        b1 = jax.random.normal(ks[2], (H,), dtype=jnp.float32) * 0.02
        w2 = jax.random.normal(ks[3], (C, H), dtype=jnp.float32) * 0.02
        b2 = jax.random.normal(ks[4], (C,), dtype=jnp.float32) * 0.02
        return {'x': x, 'w1': w1, 'b1': b1, 'w2': w2, 'b2': b2}
    _L0_ffn_all = _L0_ffn_setup()
    _L0_ffn_in = {k: v for k, v in _L0_ffn_all.items() if k in ('w1', 'b1', 'w2', 'b2')}
    del _L0_ffn_all

    def _L1_attn_setup():
        import jax, jax.numpy as jnp
        import numpy as np
        import math
        B, N, DIM = (4, 512, 192)
        HEADS, DIM_HEAD = (12, 64)
        SCALE = math.sqrt(DIM_HEAD)

        def _split_heads(t):
            b, n, _ = t.shape
            return t.reshape(b, n, HEADS, DIM_HEAD).transpose(0, 2, 1, 3)
        key = jax.random.key(seed)
        ks = jax.random.split(key, 5)
        inner = HEADS * DIM_HEAD
        x = jax.random.normal(ks[0], (B, N, DIM), dtype=jnp.float32)
        w_q = jax.random.normal(ks[1], (DIM, inner), dtype=jnp.float32) * 0.02
        w_k = jax.random.normal(ks[2], (DIM, inner), dtype=jnp.float32) * 0.02
        w_v = jax.random.normal(ks[3], (DIM, inner), dtype=jnp.float32) * 0.02
        w_o = jax.random.normal(ks[4], (inner, DIM), dtype=jnp.float32) * 0.02
        b_o = jnp.zeros((DIM,), dtype=jnp.float32)
        return {'x': x, 'w_q': w_q, 'w_k': w_k, 'w_v': w_v, 'w_o': w_o, 'b_o': b_o}
    _L1_attn_all = _L1_attn_setup()
    _L1_attn_in = {k: v for k, v in _L1_attn_all.items() if k in ('w_q', 'w_k', 'w_v', 'w_o', 'b_o')}
    del _L1_attn_all

    def _L1_ffn_setup():
        import jax, jax.numpy as jnp
        import numpy as np
        D = 192
        I = 768
        E = 8
        K = 2
        LIMIT = 10.0
        VOCAB = 8192

        def _expert(xf, W1, W2, W3):
            gate = jnp.minimum(xf @ W1, LIMIT)
            up = jnp.clip(xf @ W3, -LIMIT, LIMIT)
            return jax.nn.silu(gate) * up @ W2
        key = jax.random.key(seed)
        ks = jax.random.split(key, 10)
        s = 0.02
        return {'x': jax.random.normal(ks[0], (1, 512, D), dtype=jnp.float32), 'input_ids': jax.random.randint(ks[1], (1, 512), 0, VOCAB, dtype=jnp.int64), 'gate_w': jax.random.normal(ks[2], (D, E), dtype=jnp.float32) * s, 'gate_bias': jnp.zeros((E,), dtype=jnp.float32), 'w1': jax.random.normal(ks[3], (E, D, I), dtype=jnp.float32) * s, 'w2': jax.random.normal(ks[4], (E, I, D), dtype=jnp.float32) * s, 'w3': jax.random.normal(ks[5], (E, D, I), dtype=jnp.float32) * s, 'w1s': jax.random.normal(ks[6], (D, I), dtype=jnp.float32) * s, 'w2s': jax.random.normal(ks[7], (I, D), dtype=jnp.float32) * s, 'w3s': jax.random.normal(ks[8], (D, I), dtype=jnp.float32) * s}
    _L1_ffn_all = _L1_ffn_setup()
    _L1_ffn_in = {k: v for k, v in _L1_ffn_all.items() if k in ('input_ids', 'gate_w', 'gate_bias', 'w1', 'w2', 'w3', 'w1s', 'w2s', 'w3s')}
    del _L1_ffn_all
    return {'x': x, 'x_txt': x_txt, 'L0_tok_W': _L0_tok_in['W'], 'L0_tok_b': _L0_tok_in['b'], 'L0_txt_emb': _L0_txt_in['emb'], 'L0_attn_ln1_w': _L0_attn_in['ln1_w'], 'L0_attn_ln1_b': _L0_attn_in['ln1_b'], 'L0_attn_ln2_w': _L0_attn_in['ln2_w'], 'L0_attn_ln2_b': _L0_attn_in['ln2_b'], 'L0_attn_f_in_w': _L0_attn_in['f_in_w'], 'L0_attn_f_conv_w': _L0_attn_in['f_conv_w'], 'L0_attn_f_conv_b': _L0_attn_in['f_conv_b'], 'L0_attn_f_dt_bias': _L0_attn_in['f_dt_bias'], 'L0_attn_f_A_log': _L0_attn_in['f_A_log'], 'L0_attn_f_D': _L0_attn_in['f_D'], 'L0_attn_f_norm_w': _L0_attn_in['f_norm_w'], 'L0_attn_f_out_w': _L0_attn_in['f_out_w'], 'L0_attn_b_in_w': _L0_attn_in['b_in_w'], 'L0_attn_b_conv_w': _L0_attn_in['b_conv_w'], 'L0_attn_b_conv_b': _L0_attn_in['b_conv_b'], 'L0_attn_b_dt_bias': _L0_attn_in['b_dt_bias'], 'L0_attn_b_A_log': _L0_attn_in['b_A_log'], 'L0_attn_b_D': _L0_attn_in['b_D'], 'L0_attn_b_norm_w': _L0_attn_in['b_norm_w'], 'L0_attn_b_out_w': _L0_attn_in['b_out_w'], 'L0_attn_ffn_w1': _L0_attn_in['ffn_w1'], 'L0_attn_ffn_b1': _L0_attn_in['ffn_b1'], 'L0_attn_ffn_w2': _L0_attn_in['ffn_w2'], 'L0_attn_ffn_b2': _L0_attn_in['ffn_b2'], 'L0_ffn_w1': _L0_ffn_in['w1'], 'L0_ffn_b1': _L0_ffn_in['b1'], 'L0_ffn_w2': _L0_ffn_in['w2'], 'L0_ffn_b2': _L0_ffn_in['b2'], 'L1_attn_w_q': _L1_attn_in['w_q'], 'L1_attn_w_k': _L1_attn_in['w_k'], 'L1_attn_w_v': _L1_attn_in['w_v'], 'L1_attn_w_o': _L1_attn_in['w_o'], 'L1_attn_b_o': _L1_attn_in['b_o'], 'L1_ffn_input_ids': _L1_ffn_in['input_ids'], 'L1_ffn_gate_w': _L1_ffn_in['gate_w'], 'L1_ffn_gate_bias': _L1_ffn_in['gate_bias'], 'L1_ffn_w1': _L1_ffn_in['w1'], 'L1_ffn_w2': _L1_ffn_in['w2'], 'L1_ffn_w3': _L1_ffn_in['w3'], 'L1_ffn_w1s': _L1_ffn_in['w1s'], 'L1_ffn_w2s': _L1_ffn_in['w2s'], 'L1_ffn_w3s': _L1_ffn_in['w3s']}

def reference(x, x_txt, L0_tok_W, L0_tok_b, L0_txt_emb, L0_attn_ln1_w, L0_attn_ln1_b, L0_attn_ln2_w, L0_attn_ln2_b, L0_attn_f_in_w, L0_attn_f_conv_w, L0_attn_f_conv_b, L0_attn_f_dt_bias, L0_attn_f_A_log, L0_attn_f_D, L0_attn_f_norm_w, L0_attn_f_out_w, L0_attn_b_in_w, L0_attn_b_conv_w, L0_attn_b_conv_b, L0_attn_b_dt_bias, L0_attn_b_A_log, L0_attn_b_D, L0_attn_b_norm_w, L0_attn_b_out_w, L0_attn_ffn_w1, L0_attn_ffn_b1, L0_attn_ffn_w2, L0_attn_ffn_b2, L0_ffn_w1, L0_ffn_b1, L0_ffn_w2, L0_ffn_b2, L1_attn_w_q, L1_attn_w_k, L1_attn_w_v, L1_attn_w_o, L1_attn_b_o, L1_ffn_input_ids, L1_ffn_gate_w, L1_ffn_gate_bias, L1_ffn_w1, L1_ffn_w2, L1_ffn_w3, L1_ffn_w1s, L1_ffn_w2s, L1_ffn_w3s):
    import jax
    import jax.numpy as jnp

    def _L0_tok_ref(x, W, b):
        import jax, jax.numpy as jnp
        import numpy as np
        PATCH = 16
        EMBED = 192
        IN_DIM = PATCH * PATCH * 3

        def extract_patches(x, p):
            B, C, H, Wd = x.shape
            h, w = (H // p, Wd // p)
            xr = x.reshape(B, C, h, p, w, p)
            xr = xr.transpose(0, 2, 4, 3, 5, 1)
            return xr.reshape(B, h * w, p * p * C)
        patches = extract_patches(x, PATCH)
        return jnp.einsum('bnd,ed->bne', patches, W) + b

    def _L0_txt_ref(idx, emb):
        import jax, jax.numpy as jnp
        import numpy as np
        B, T, V, C = (8, 512, 50257, 192)

        def _rosa(x):
            Bx, Tx = x.shape
            eq = (x[:, :, None] == x[:, None, :]).astype(jnp.int32)

            def step(prev, eq_row):
                cur = (jnp.pad(prev[:, :-1], ((0, 0), (1, 0))) + 1) * eq_row
                return (cur, cur)
            init = jnp.zeros((Bx, Tx), jnp.int32)
            _, rows = jax.lax.scan(step, init, jnp.swapaxes(eq, 0, 1)[1:])
            L = jnp.swapaxes(jnp.concatenate([init[None], rows], axis=0), 0, 1)
            mask = jnp.tril(jnp.ones((Tx, Tx), dtype=bool), -1)
            j = jnp.arange(Tx, dtype=jnp.float32)
            TIE = 1e-05
            scored = jnp.where(mask[None], L.astype(jnp.float32) + j[None, None, :] * TIE, -1.0)
            best_j = jnp.argmax(scored, axis=2)
            pred_idx = jnp.minimum(best_j + 1, Tx - 1)
            preds = jnp.take_along_axis(x, pred_idx, axis=1)
            no_match = jnp.max(jnp.where(mask[None], L, 0), axis=2) == 0
            return jnp.where(no_match, -1, preds)
        p = _rosa(idx)
        out = emb[jnp.clip(p, 0)]
        return jnp.where((p == -1)[..., None], 0.0, out)

    def _L0_attn_ref(x, ln1_w, ln1_b, ln2_w, ln2_b, f_in_w, f_conv_w, f_conv_b, f_dt_bias, f_A_log, f_D, f_norm_w, f_out_w, b_in_w, b_conv_w, b_conv_b, b_dt_bias, b_A_log, b_D, b_norm_w, b_out_w, ffn_w1, ffn_b1, ffn_w2, ffn_b2):
        import jax, jax.numpy as jnp
        import numpy as np
        D_MODEL = 192
        D_STATE = 16
        D_CONV = 4
        EXPAND = 2
        HEADDIM = 64
        D_INNER = EXPAND * D_MODEL
        NHEADS = D_INNER // HEADDIM
        CONV_DIM = D_INNER + 2 * D_STATE
        D_IN_PROJ = 2 * D_INNER + 2 * D_STATE + NHEADS
        BATCH, SEQ = (4, 512)

        def _mamba_params(key, scale=0.02):
            ks = jax.random.split(key, 5)
            return dict(in_w=jax.random.normal(ks[0], (D_MODEL, D_IN_PROJ), jnp.float32) * scale, conv_w=jax.random.normal(ks[1], (CONV_DIM, D_CONV), jnp.float32) * scale, conv_b=jnp.zeros((CONV_DIM,), jnp.float32), dt_bias=jax.random.normal(ks[2], (NHEADS,), jnp.float32) * 0.1, A_log=jnp.log(jax.random.uniform(ks[3], (NHEADS,), jnp.float32, 1.0, 16.0)), D=jnp.ones((NHEADS,), jnp.float32), norm_w=jnp.ones((D_INNER,), jnp.float32), out_w=jax.random.normal(ks[4], (D_INNER, D_MODEL), jnp.float32) * scale)

        def _layernorm(x, w, b, eps=1e-05):
            m = jnp.mean(x, -1, keepdims=True)
            v = jnp.mean((x - m) ** 2, -1, keepdims=True)
            return (x - m) * jax.lax.rsqrt(v + eps) * w + b

        def _mamba2(u, in_w, conv_w, conv_b, dt_bias, A_log, D, norm_w, out_w):
            b, l, _ = u.shape
            zxbcdt = u @ in_w
            z = zxbcdt[..., :D_INNER]
            xBC = zxbcdt[..., D_INNER:D_INNER + CONV_DIM]
            dt = jax.nn.softplus(zxbcdt[..., -NHEADS:] + dt_bias)
            xpad = jnp.pad(xBC, ((0, 0), (D_CONV - 1, 0), (0, 0)))
            xc = sum((conv_w[:, k] * xpad[:, k:k + l, :] for k in range(D_CONV))) + conv_b
            xc = jax.nn.silu(xc)
            xh = xc[..., :D_INNER].reshape(b, l, NHEADS, HEADDIM)
            Bm = xc[..., D_INNER:D_INNER + D_STATE]
            Cm = xc[..., D_INNER + D_STATE:]
            A = -jnp.exp(A_log)
            dA = jnp.exp(dt * A)

            def step(h, inp):
                dA_t, dt_t, B_t, C_t, x_t = inp
                h = h * dA_t[:, :, None, None] + (dt_t[:, :, None] * x_t)[..., None] * B_t[:, None, None, :]
                y = jnp.einsum('bhpn,bn->bhp', h, C_t)
                return (h, y)
            h0 = jnp.zeros((b, NHEADS, HEADDIM, D_STATE), u.dtype)
            xs = (dA.transpose(1, 0, 2), dt.transpose(1, 0, 2), Bm.transpose(1, 0, 2), Cm.transpose(1, 0, 2), xh.transpose(1, 0, 2, 3))
            _, ys = jax.lax.scan(step, h0, xs)
            y = ys.transpose(1, 0, 2, 3) + D[None, None, :, None] * xh
            y = y.reshape(b, l, D_INNER)
            yz = y * jax.nn.silu(z)
            yz = yz * jax.lax.rsqrt(jnp.mean(yz * yz, -1, keepdims=True) + 1e-05) * norm_w
            return yz @ out_w
        xn = _layernorm(x, ln1_w, ln1_b)
        fo = _mamba2(xn, f_in_w, f_conv_w, f_conv_b, f_dt_bias, f_A_log, f_D, f_norm_w, f_out_w)
        bo = _mamba2(jnp.flip(xn, 1), b_in_w, b_conv_w, b_conv_b, b_dt_bias, b_A_log, b_D, b_norm_w, b_out_w)
        bo = jnp.flip(bo, 1)
        bi = jnp.concatenate([fo, bo], -1)
        h = jax.nn.gelu(bi @ ffn_w1 + ffn_b1, approximate=False)
        h = jax.nn.gelu(h @ ffn_w2 + ffn_b2, approximate=False)
        return _layernorm(x + h, ln2_w, ln2_b)

    def _L0_ffn_ref(x, w1, b1, w2, b2):
        import jax, jax.numpy as jnp
        import numpy as np
        LN2 = jnp.log(jnp.float32(2.0))
        ALPHA = 0.5
        A_BITS = 8
        W_BITS = 8
        EPS = 1e-08

        def round_ln(x):
            y = jnp.floor(jnp.log(x) / LN2)
            up = x - 2.0 ** y > 2.0 ** (y + 1.0) - x
            return y + up.astype(x.dtype)

        def fq_act_asym(x, bits=A_BITS):
            qmax = 2 ** bits - 1
            xmin = jnp.minimum(x.min(), 0.0)
            xmax = jnp.maximum(x.max(), 0.0)
            scale = jnp.maximum((xmax - xmin) / qmax, EPS)
            zp = jnp.round(-xmin / scale)
            q = jnp.clip(jnp.round(x / scale) + zp, 0, qmax)
            return (q - zp) * scale

        def fq_act_sym(x, bits=A_BITS):
            qmax = 2 ** (bits - 1) - 1
            scale = jnp.maximum(jnp.abs(x).max() / qmax, EPS)
            q = jnp.clip(jnp.round(x / scale), -qmax - 1, qmax)
            return q * scale

        def fq_weight(w, bits=W_BITS):
            qmax = 2 ** (bits - 1) - 1
            scale = jnp.maximum(jnp.abs(w).max(axis=1, keepdims=True) / qmax, EPS)
            q = jnp.clip(jnp.round(w / scale), -qmax - 1, qmax)
            return q * scale
        global_max_x = jnp.abs(x).max(axis=(0, 1))
        max_weight = jnp.abs(w1).max(axis=0)
        cs = global_max_x ** ALPHA / max_weight ** (1.0 - ALPHA)
        cs = 2.0 ** round_ln(cs)
        x_smoothed = x / cs[None, None, :]
        w1_smoothed = w1 * cs[None, :]
        xq = fq_act_asym(x_smoothed)
        h = jnp.einsum('bnc,hc->bnh', xq, fq_weight(w1_smoothed)) + b1
        h = jax.nn.gelu(h, approximate=False)
        hq = fq_act_sym(h)
        out = jnp.einsum('bnh,ch->bnc', hq, fq_weight(w2)) + b2
        out = fq_act_asym(out)
        return out

    def _L1_attn_ref(x, w_q, w_k, w_v, w_o, b_o):
        import jax, jax.numpy as jnp
        import numpy as np
        import math
        B, N, DIM = (4, 512, 192)
        HEADS, DIM_HEAD = (12, 64)
        SCALE = math.sqrt(DIM_HEAD)

        def _split_heads(t):
            b, n, _ = t.shape
            return t.reshape(b, n, HEADS, DIM_HEAD).transpose(0, 2, 1, 3)
        q = _split_heads(x @ w_q)
        k = _split_heads(x @ w_k)
        v = _split_heads(x @ w_v)
        scores = jnp.einsum('bhnd,bhmd->bhnm', q, k) / SCALE
        attn = jax.nn.softmax(scores, axis=-1)
        h = jnp.einsum('bhnm,bhmd->bhnd', attn, v)
        H = h.transpose(0, 2, 1, 3).reshape(x.shape[0], x.shape[1], HEADS * DIM_HEAD)
        out = H @ w_o + b_o
        return out

    def _L1_ffn_ref(x, input_ids, gate_w, gate_bias, w1, w2, w3, w1s, w2s, w3s):
        import jax, jax.numpy as jnp
        import numpy as np
        D = 192
        I = 768
        E = 8
        K = 2
        LIMIT = 10.0
        VOCAB = 8192

        def _expert(xf, W1, W2, W3):
            gate = jnp.minimum(xf @ W1, LIMIT)
            up = jnp.clip(xf @ W3, -LIMIT, LIMIT)
            return jax.nn.silu(gate) * up @ W2
        B, T, _ = x.shape
        flat = x.reshape(-1, D)
        N = flat.shape[0]
        scores = jnp.sqrt(jax.nn.softplus(flat @ gate_w))
        routed_scores = scores + gate_bias
        _, indices = jax.lax.top_k(routed_scores, K)
        weights = jnp.take_along_axis(scores, indices, axis=1)
        weights = weights / jnp.clip(weights.sum(axis=-1, keepdims=True), 1e-06)
        combine = jnp.zeros((N, E), dtype=weights.dtype)
        combine = combine.at[jnp.arange(N)[:, None], indices].add(weights)
        y = _expert(flat, w1s, w2s, w3s)
        gate_h = jnp.minimum(jnp.einsum('td,edi->eti', flat, w1), LIMIT)
        up_h = jnp.clip(jnp.einsum('td,edi->eti', flat, w3), -LIMIT, LIMIT)
        h = jax.nn.silu(gate_h) * up_h
        out_e = jnp.einsum('eti,eid->etd', h, w2)
        routed = jnp.einsum('etd,te->td', out_e, combine)
        return (y + routed).reshape(B, T, D)
    h = _L0_tok_ref(x, L0_tok_W, L0_tok_b)
    h = jnp.concatenate([h, _L0_txt_ref(x_txt, L0_txt_emb)], axis=1)
    h = h + _L0_attn_ref(_layernorm(h, axis=-1), L0_attn_ln1_w, L0_attn_ln1_b, L0_attn_ln2_w, L0_attn_ln2_b, L0_attn_f_in_w, L0_attn_f_conv_w, L0_attn_f_conv_b, L0_attn_f_dt_bias, L0_attn_f_A_log, L0_attn_f_D, L0_attn_f_norm_w, L0_attn_f_out_w, L0_attn_b_in_w, L0_attn_b_conv_w, L0_attn_b_conv_b, L0_attn_b_dt_bias, L0_attn_b_A_log, L0_attn_b_D, L0_attn_b_norm_w, L0_attn_b_out_w, L0_attn_ffn_w1, L0_attn_ffn_b1, L0_attn_ffn_w2, L0_attn_ffn_b2)
    h = h + _L0_ffn_ref(_layernorm(h, axis=-1), L0_ffn_w1, L0_ffn_b1, L0_ffn_w2, L0_ffn_b2)
    h = h + _L1_attn_ref(_layernorm(h, axis=-1), L1_attn_w_q, L1_attn_w_k, L1_attn_w_v, L1_attn_w_o, L1_attn_b_o)
    h = h + _L1_ffn_ref(_layernorm(h, axis=-1), L1_ffn_input_ids, L1_ffn_gate_w, L1_ffn_gate_bias, L1_ffn_w1, L1_ffn_w2, L1_ffn_w3, L1_ffn_w1s, L1_ffn_w2s, L1_ffn_w3s)
    return h

_drawn_inputs = setup_inputs


def setup_inputs(seed=0):
    import zlib

    import numpy as np

    out = dict(_drawn_inputs(seed))
    spreads = {'L0_attn_ln1_w': (1.0, 0.6),
     'L0_attn_ln1_b': (0.0, 0.1),
     'L0_attn_ln2_w': (1.0, 0.2),
     'L0_attn_ln2_b': (0.0, 0.1),
     'L0_attn_f_conv_b': (0.0, 0.277),
     'L0_attn_f_D': (1.0, 0.6),
     'L0_attn_f_norm_w': (1.0, 0.6),
     'L0_attn_b_conv_b': (0.0, 0.1),
     'L0_attn_b_D': (1.0, 0.6),
     'L0_attn_b_norm_w': (1.0, 0.6),
     'L0_attn_ffn_b1': (0.0, 0.1),
     'L0_attn_ffn_b2': (0.0, 0.1),
     'L1_attn_b_o': (0.0, 0.1),
     'L1_ffn_gate_bias': (0.0, 0.8)}
    factors = {'L0_attn_f_conv_w': 8.0,
     'L0_attn_f_dt_bias': 29.852,
     'L0_attn_f_A_log': 8.0,
     'L0_attn_b_conv_w': 8.0,
     'L0_attn_b_dt_bias': 34.471,
     'L0_attn_b_A_log': 8.0,
     'L0_ffn_b1': 8.0,
     'L0_ffn_b2': 4.006,
     'L1_attn_w_q': 8.0,
     'L1_attn_w_k': 8.0,
     'L1_ffn_gate_w': 5.534,
     'L1_ffn_w1': 5.02,
     'L1_ffn_w2': 5.053,
     'L1_ffn_w3': 4.83,
     'L1_ffn_w1s': 3.384,
     'L1_ffn_w2s': 3.621,
     'L1_ffn_w3s': 3.655}
    for name, (base, spread) in spreads.items():
        noise = np.random.default_rng([zlib.crc32(name.encode()), seed]).standard_normal(out[name].shape)
        drawn = base * np.exp(spread * noise) if base else spread * noise
        out[name] = jnp.asarray(drawn.astype(out[name].dtype))
    for name, factor in factors.items():
        out[name] = (out[name] * factor).astype(out[name].dtype)
    return out
```

```python
from contextlib import ExitStack

import concourse.bass as bass
from concourse import mybir

F32 = mybir.dt.float32
BF16 = mybir.dt.bfloat16
I32 = mybir.dt.int32
U32 = mybir.dt.uint32
ALU = mybir.AluOpType
ACT = mybir.ActivationFunctionType
AX = mybir.AxisListType
RMAX = bass.bass_isa.ReduceOp.max

P = 128
NB = 8
NI, NX = 64, 77
L = NI + NX
T = NB * L
TT = -(-T // P)
TP = TT * P
LAST = T - (TT - 1) * P
R = L - P
D = 192
DA, DB = 128, 64
IN = 768
KI = IN // P
DIN = 384
KD = DIN // P
NH = 6
NS = 16
NCONV = 4
PADL = L + NCONV - 1
CC = 0
CX = DIN
CB = 2 * DIN
CDT = 2 * DIN + 48
WCOLS = CDT + NH
HID = 768
KH = HID // P
ROUNDER = 1.5 * 2.0 ** 23
QEPS = 1e-8
AH = 12
NE = 8
CH = 376
CM = 384


def rows(t):
    return P if t < TT - 1 else LAST


class Steps:

    def __init__(self, eng, sem):
        self.eng, self.sem, self.n = eng, sem, 0

    def add(self, ins):
        ins.then_inc(self.sem, 1)
        self.n += 1
        return self.n

    def wait(self):
        self.eng.wait_ge(self.sem, self.n)


def build(nc, i, out):
    ctx = ExitStack()
    with ctx:
        def sb(name, shape, dt=F32):
            return ctx.enter_context(nc.sbuf_tensor(name, shape, dt))

        def sem(name):
            return ctx.enter_context(nc.semaphore(name))

        bank = [ctx.enter_context(nc.psum_tensor(f"bank{k}", [P, 512], F32)) for k in range(8)]
        h0 = nc.dram_tensor("h0_scratch", (NB, L, D), F32, kind="Internal").ap()

        identw = sb("identw", [P, L])
        ident = identw[:, 0:P]
        identb = sb("identb", [P, P], BF16)
        ident3 = sb("ident3", [P, 3 * L])
        identr = sb("identr", [R, NH * R])
        ones = sb("ones", [P, P])
        cst = sb("cst", [P, 4])
        qcol = sb("qcol", [P, 1])
        iota8 = sb("iota8", [P, NE])

        H = sb("H", [P, TT, D])
        X = sb("X", [P, TT, D])
        XTa = sb("XTa", [P, TP])
        XTb = sb("XTb", [DB, TP])
        stats = sb("stats", [P, TT, 6])
        mv = sb("mv", [P, TT, 2])
        std = sb("std", [P, 2 * TT])
        rstd = sb("rstd", [P, TT])
        rstd2 = sb("rstd2", [P, TT])
        prod = sb("prod", [P, TT])

        big1 = sb("big1", [P, KH * TP])
        big2 = sb("big2", [P, KH * TP])
        big3 = sb("big3", [P, KH * TP])
        wreg = sb("wreg", [P, 8448])
        areg = sb("areg", [P, 5150])
        creg = sb("creg", [P, 5120])

        def area(reg, at, shape):
            n = 1
            for s in shape[1:]:
                n *= s
            v = reg[0:shape[0], at:at + n]
            if len(shape) == 3:
                v = v.rearrange("p (a b) -> p a b", b=shape[2])
            if len(shape) == 4:
                v = v.rearrange("p (a b c) -> p a b c", b=shape[2], c=shape[3])
            return v

        patches = area(big1, 0, [P, KI, NB * NI])
        tokw = area(big1, KI * NB * NI, [P, KI, D])
        tokb = area(big1, KI * NB * NI + KI * D, [P, D])
        img = area(big2, 0, [P, NB // 2, D])
        cur = area(big2, 1024, [76, NB, NX]).bitcast(I32)
        shf = area(big2, 1664, [76, NB, NX]).bitcast(I32)
        eq = area(big2, 2304, [76, NB * NX])
        run = area(big2, 2944, [76, NB * NX])
        score = area(big2, 3584, [76, NB * NX])
        nxt = area(big2, 4224, [NX, NB, 76]).bitcast(I32)
        junk = area(big2, 4864, [NX, NB, 76])
        txt = area(big3, 0, [NX, NB, D])
        best = sb("best", [NX, NB])
        found = sb("found", [NX, NB])
        pick = sb("pick", [NX, NB])
        ids = sb("ids", [NX, NB], I32)

        XS = area(big3, 0, [P, TT, D])
        XRa = area(areg, 0, [P, TP])
        XRb = area(areg, TP, [DB, TP])
        ln1 = sb("ln1", [P, 2, 2])
        inw = area(wreg, 0, [P, 2 * 2, WCOLS])
        outw = area(wreg, 4 * WCOLS, [P, 2 * KD, D])
        ffw1 = area(wreg, 4 * WCOLS + 2 * KD * D, [P, KD, HID])
        ffw2 = area(areg, 2 * TP, [P, KH, D])
        ffb1 = sb("ffb1", [P, KH])
        ffb2 = sb("ffb2", [1, D])
        normw = sb("normw", [P, 2 * KD])
        convw = sb("convw", [P, 2, 4, NCONV])
        convb = sb("convb", [P, 2, 4])
        skipd = sb("skipd", [P, 2, KD])
        ZS = area(big1, 0, [P, 2 * KD, T])
        CV = area(big2, 0, [P, 2 * KD, T])
        XP = area(big3, 0, [P, 2 * KD, NB * PADL])
        bcp = area(creg, 0, [48, 2, NB * PADL])
        bcv = area(creg, 2 * NB * PADL, [48, 2, T])
        dtrow = sb("dtrow", [P, 2 * 96])
        alog = sb("alog", [P, 2 * 96])
        dtv = sb("dtv", [P, 192])
        dte = sb("dte", [P, 192])
        dtt = sb("dtt", [P, 192])
        dtq = sb("dtq", [P, 192])
        dtp = sb("dtp", [P, 192])
        dts = sb("dts", [P, 192])
        dA = sb("dA", [P, 192])
        xcs = sb("xcs", [P, 2, KD, L])
        Bs = sb("Bs", [NS, 2, L])
        Cs = sb("Cs", [NS, 2, L])
        dtx = sb("dtx", [P, 2, DIN])
        dtxr = sb("dtxr", [R, 2, DIN])
        DD = area(areg, 3456, [P, NH, L])
        MM = area(wreg, 6744, [P, 2, NH, L])
        dAr = sb("dAr", [R, NH, R])
        DDr = sb("DDr", [R, NH, R])
        MMr = sb("MMr", [R, 2, NH, R])
        w1y = area(areg, 3456 + NH * L, [P, 2, KD, L])
        SQ = area(big3, 0, [P, 2 * KD, T])
        rs = sb("rs", [P, 2 * TT])
        rss = sb("rss", [P, 2 * TT])
        BT = area(big1, 0, [P, TT, 2 * D])
        BI = area(big1, TT * 2 * D, [P, KD, T])
        BIr = area(big2, 0, [P, 2, T])
        H1 = area(big3, 0, [P, KH, T])
        G2 = area(big2, 2 * T, [P, TT, D])
        SS = area(big2, 2 * T + TT * D, [P, TT, D])
        ln2w = sb("ln2w", [P, D])
        ln2b = sb("ln2b", [P, D])

        qw1t = area(areg, 0, [P, 2, HID])
        qw1 = area(creg, 0, [P, KH, D])
        qw2 = area(creg, KH * D, [P, 2, HID])
        qb1 = sb("qb1", [P, KH])
        qb2 = sb("qb2", [P, 2])
        q1 = area(areg, 2 * HID, [P, KH * D // 2]).bitcast(BF16).rearrange("p (a b) -> p a b", b=D)
        q2 = area(areg, 2 * HID + 576, [P, HID]).bitcast(BF16).rearrange("p (a b) -> p a b", b=HID)
        q1t = area(areg, 2 * HID + 576 + HID, [P, HID]).bitcast(BF16).rearrange("p (a b) -> p a b", b=HID)
        q2t = area(areg, 2 * HID + 576 + 2 * HID, [P, KH * D // 2]).bitcast(BF16).rearrange("p (a b) -> p a b", b=D)
        csdiag = area(creg, 3000, [P, D])
        csb = sb("csb", [P, D])
        qs = sb("qs", [P, 64])
        UR = area(big2, 0, [P, 2, T])
        UQ = area(big2, 2 * T, [P, T]).bitcast(BF16).rearrange("p (a b) -> p a b", b=T)
        HG = area(big3, 0, [P, KH, T])
        HQ = area(big1, 0, [P, KH * T // 2]).bitcast(BF16).rearrange("p (a b) -> p a b", b=T)
        OT = area(big2, 3 * T, [P, 2, T])
        ham = sb("ham", [P, 3 * KH])

        awq = area(wreg, 0, [P, 2, AH * 64])
        awk = area(wreg, 2 * HID, [P, 2, AH * 64])
        awv = area(wreg, 4 * HID, [P, 2, AH * 64])
        awo = area(wreg, 6 * HID, [P, KH, D])
        abo = sb("abo", [1, D])
        QK = area(big2, 0, [P, 2, 12 * L])
        Va = area(big2, 2 * 12 * L, [P, 2, HID])
        Vb = area(creg, 12 * L, [R, 2, HID])
        PRS = area(big3, 0, [P, 2 * 6, 3 * L])
        PT = area(big3, 36 * L, [P, AH, L])
        PTr = area(creg, 0, [R, AH, L])
        OA = area(big1, 0, [P, KH, T])
        GROUPS = [(P, 3)] * 4 + [(96, 2)] * 2
        amx = sb("amx", [P, 36])
        asm = sb("asm", [P, 36])
        arc = sb("arc", [P, 36])

        EW = NE + 1
        per = 4 * HID + KH * D
        ew1 = [area(wreg, k * 4224, [P, 2, HID]) for k in range(2)]
        ew3 = [area(areg, k * 1536, [P, 2, HID]) for k in range(2)]
        ew2 = [area(wreg, k * 4224 + 2 * HID, [P, KH, D]) for k in range(2)]
        gatew = sb("gatew", [P, 2, NE])
        gateb = sb("gateb", [P, NE])
        gv = area(creg, 0 * TT * NE, [P, TT * NE])
        gn = area(creg, 1 * TT * NE, [P, TT * NE])
        ge = area(creg, 2 * TT * NE, [P, TT * NE])
        gt = area(creg, 3 * TT * NE, [P, TT * NE])
        gq = area(creg, 4 * TT * NE, [P, TT * NE])
        gp = area(creg, 5 * TT * NE, [P, TT * NE])
        gs = area(creg, 6 * TT * NE, [P, TT * NE])
        gr = area(creg, 7 * TT * NE, [P, TT, NE])
        top = area(creg, 8 * TT * NE, [P, TT, NE])
        topi = area(creg, 10 * TT * NE, [P, TT, NE]).bitcast(U32)
        topf = area(creg, 9 * TT * NE, [P, TT, NE])
        comb = sb("comb", [P, TT, NE])
        csum = sb("csum", [P, TT])
        GM = area(big1, 0, [P, 3, CM])
        GS = area(big1, 3 * CM, [P, 3, CM])
        UM = area(big1, 6 * CM, [P, 3, CM])
        HH = area(big2, 0, [P, 2, KH * CM])

        names = """ld_embed ld_tok ld_ln1 ld_inw ld_dt ld_conv ld_outw ld_ffw1 ld_ffw2 ld_ln2
            const_ready iota_ready v_step img_ready img_out score_ready scoreT ids_ready gathered txt_ready
            h0_stored h_loaded inproj z_evac x_evac dt_ready dt_abs dt_exp a_exp dt_arg dA_exp dA_ready
            flipped convolved xc_ready xc_turned g_ready decay_ready dtx_ready decay_used m_ready y_ready
            yd_ready yz_ready padded sq_ready ss_ready ss_std ss_inv op_ready bt_ready bt_turned bi_act bi_dve
            bi_flip h1_ready h1_out f2_ready f2_out ln2_var ln2_std 
            ld_q1t ld_q1 ld_q2 ld_qb outw_scaled
            q_gmax q_sqrt q_diag q_csb q_range q_range_all q_fac q_u q_ui q_uc q1_ready q1_turned q1_out q2_ready q2_turned q2_out
            hq_mm hg_ready ham_ready ham_all hs_ready hr_ready hc_ready hi_ready ot_mm ot_ready or_ready or_all
            of_ready om_ready oq_ready oq_turned h_ffn 
            ld_att qk_mm qk_out v_mm v_out s_mm s_sub s_exp s_sum p_norm p_turned pt_act pt_dve av_mm av_out
            wo_mm h_att ld_gate g_mm g_abs g_exp g_sp g_sqrt 
            ld_e gu_mm g_min g_silu u_clip hh_ready e_mm e_acc stored   p_step""".split()
        S = {n: sem(n) for n in names}
        ln_var = [sem(f"ln_var{k}") for k in range(4)]
        ln_std = [sem(f"ln_std{k}") for k in range(4)]
        ln_x = [sem(f"ln_x{k}") for k in range(4)]
        ln_turned = [sem(f"ln_turned{k}") for k in range(4)]
        ln_out = [sem(f"ln_out{k}") for k in range(4)]
        ln0_std2 = sem("ln0_std2")
        ln0_vx = sem("ln0_vx")

        block = ctx.enter_context(nc.Block())
        ITS = [(d, b) for d in range(2) for b in range(NB)]
        DTC = lambda d, b: (d * NB + b) * NH

        def k_inproj(d, c, m):
            return (d * 4 + c) * 7 + m

        def inproj_free(k):
            dc, m = divmod(k, 7)
            return (S["z_evac"], dc * 3 + m + 1) if m < 3 else (S["x_evac"], dc * 4 + m - 3 + 1)

        @block.sync
        def _(sp):
            def load(dst, src, s):
                sp.dma_start(dst, src).then_inc(S[s], 16)

            wide = dict(p=76, b=NB, n=NX)
            tok = i["tok"]
            W = 76 + NX

            def window(parts, at, n):
                return bass.AP(tensor=tok.tensor, offset=at, ap=[[1, parts], [W, NB], [1, n]])

            load(cur, bass.AP(tensor=tok.tensor, offset=76, ap=[[0, 76], [W, NB], [1, NX]]), "ld_tok")
            load(shf, window(76, 0, NX), "ld_tok")
            load(nxt, window(NX, 1, 76), "ld_tok")
            load(patches, i["patches"].rearrange("(k p) n -> p k n", p=P), "ld_embed")
            load(tokw, i["tok_w"].rearrange("(k p) n -> p k n", p=P), "ld_embed")
            load(tokb, i["tok_b"].partition_broadcast(P).rearrange("p a n -> p (a n)"), "ld_embed")
            load(ln1[0:DA, 0, :], i["ln1"][0:DA, :], "ld_ln1")
            load(ln1[0:DB, 1, :], i["ln1"][DA:D, :], "ld_ln1")
            for d in range(2):
                load(inw[:, 2 * d, :], i["in_w"][d, 0:DA, :], "ld_inw")
                load(inw[0:DB, 2 * d + 1, :], i["in_w"][d, DA:D, :], "ld_inw")
            load(dtrow[:, :], i["dt_bias"].partition_broadcast(P).rearrange("p a n -> p (a n)"), "ld_dt")
            load(alog[:, :], i["a_log"].partition_broadcast(P).rearrange("p a n -> p (a n)"), "ld_dt")
            load(convw[:], i["conv_w"], "ld_conv")
            load(convb[:], i["conv_b"], "ld_conv")
            load(skipd[:], i["skip_d"], "ld_conv")
            load(outw, i["out_w"].rearrange("d (k p) n -> p (d k) n", p=P), "ld_outw")
            load(normw[:, :], i["norm_w"], "ld_outw")
            load(ffw1, i["ffn_w1"].rearrange("(k p) n -> p k n", p=P), "ld_ffw1")
            load(ffb1[:, :], i["ffn_b1"], "ld_ffw1")
            load(ffw2, i["ffn_w2"].rearrange("(k p) n -> p k n", p=P), "ld_ffw2")
            load(ffb2[:, :], i["ffn_b2"], "ld_ffw2")
            load(ln2w[:, :], i["ln2_w"].partition_broadcast(P).rearrange("p a n -> p (a n)"), "ld_ln2")
            load(ln2b[:, :], i["ln2_b"].partition_broadcast(P).rearrange("p a n -> p (a n)"), "ld_ln2")
            load(qb1[:, :], i["q_b1"], "ld_qb")
            load(qb2[:, 0:1], i["q_b2"][0:DA, :], "ld_qb")
            load(qb2[0:DB, 1:2], i["q_b2"][DA:D, :], "ld_qb")
            load(gatew[:, 0, :], i["gate_w"][0:DA, :], "ld_gate")
            load(gatew[0:DB, 1, :], i["gate_w"][DA:D, :], "ld_gate")
            load(gateb[:, :], i["gate_b"].partition_broadcast(P).rearrange("p a n -> p (a n)"), "ld_gate")
            sp.wait_ge(S["img_ready"], 2)
            for b in range(NB):
                sp.dma_start(h0[b, 0:NI, :], img[(b % 2) * NI:(b % 2 + 1) * NI, b // 2, :]).then_inc(S["h0_stored"], 16)
            sp.wait_ge(S["txt_ready"], 1)
            sp.dma_start(h0[:, NI:L, :].rearrange("b n d -> n b d"), txt).then_inc(S["h0_stored"], 16)
            sp.wait_ge(S["h0_stored"], 16 * (NB + 1))
            hf = h0.rearrange("b n d -> (b n) d")
            sp.wait_ge(S["padded"], 1)
            sp.dma_start(H[:, 0:TT - 1, :], hf[0:(TT - 1) * P, :].rearrange("(t p) d -> p t d", p=P)).then_inc(S["h_loaded"], 16)
            sp.dma_start(H[0:LAST, TT - 1, :], hf[(TT - 1) * P:T, :]).then_inc(S["h_loaded"], 16)
            sp.wait_ge(S["xc_ready"], 3 * 16)
            load(qw1, i["q_w1"].rearrange("(k p) n -> p k n", p=P), "ld_q1")
            load(qw2[:, 0, :], i["q_w2"][0:DA, :], "ld_q2")
            load(qw2[0:DB, 1, :], i["q_w2"][DA:D, :], "ld_q2")
            sp.wait_ge(S["inproj"], 56)
            load(qw1t[:, 0, :], i["q_w1t"][0:DA, :], "ld_q1t")
            load(qw1t[0:DB, 1, :], i["q_w1t"][DA:D, :], "ld_q1t")
            sp.wait_ge(S["f2_ready"], TT)
            for w, src in ((awq, "w_q"), (awk, "w_k"), (awv, "w_v")):
                load(w[:, 0, :], i[src][0:DA, :], "ld_att")
                load(w[0:DB, 1, :], i[src][DA:D, :], "ld_att")
            load(awo, i["w_o"].rearrange("(k p) n -> p k n", p=P), "ld_att")
            load(abo[:, :], i["b_o"], "ld_att")
            for e in range(EW):
                if e == 0:
                    sp.wait_ge(S["wo_mm"], TT)
                if e >= 2:
                    sp.wait_ge(S["e_mm"], TT * (e - 1))
                k = e % 2
                load(ew1[k][:, 0, :], i["e_w1"][e, 0:DA, :], "ld_e")
                load(ew1[k][0:DB, 1, :], i["e_w1"][e, DA:D, :], "ld_e")
                load(ew3[k][:, 0, :], i["e_w3"][e, 0:DA, :], "ld_e")
                load(ew3[k][0:DB, 1, :], i["e_w3"][e, DA:D, :], "ld_e")
                load(ew2[k], i["e_w2"][e].rearrange("(k p) n -> p k n", p=P), "ld_e")
                sp.wait_ge(S["ld_e"], 80 * (e + 1))
            of = out.rearrange("b n d -> (b n) d")
            for t in range(TT):
                sp.wait_ge(S["e_acc"], TT * (EW - 1) + t + 1)
                sp.dma_start(of[t * P:t * P + rows(t), :], H[0:rows(t), t, :]).then_inc(S["stored"], 16)
            sp.wait_ge(S["stored"], 16 * TT)

        @block.gpsimd
        def _(pool):
            st = Steps(pool, S["p_step"])
            st.add(pool.memset(identw[:], 0.0))
            pool.memset(ones[:], 1.0).then_inc(S["const_ready"], 1)
            pool.iota(qcol[:, :], pattern=[[0, 1]], base=0, channel_multiplier=1,
                      allow_small_or_imprecise_dtypes=True).then_inc(S["iota_ready"], 1)
            pool.iota(iota8[:, :], pattern=[[1, NE]], base=0, channel_multiplier=0,
                      allow_small_or_imprecise_dtypes=True).then_inc(S["iota_ready"], 1)
            st.wait()
            st.add(pool.affine_select(out=identw[:], in_=identw[:], compare_op=ALU.not_equal, fill=1.0, base=0,
                                      pattern=[[-1, L]], channel_multiplier=1))
            st.wait()
            pool.tensor_copy(identb[:, :], ident).then_inc(S["const_ready"], 1)
            pool.tensor_copy(ident3[:, :].rearrange("p (a b) -> p a b", b=L), identw[:, :].unsqueeze(1).to_broadcast([P, 3, L])).then_inc(S["const_ready"], 1)
            pool.tensor_copy(identr[:, :].rearrange("p (a b) -> p a b", b=R), identw[0:R, 0:R].unsqueeze(1).to_broadcast([R, NH, R])).then_inc(S["const_ready"], 1)
            pool.memset(cst[:, 0:1], 1e-5).then_inc(S["const_ready"], 1)
            pool.memset(cst[:, 1:2], ROUNDER).then_inc(S["const_ready"], 1)
            pool.memset(cst[:, 2:3], 1.0).then_inc(S["const_ready"], 1)
            pool.memset(H[:, TT - 1, :], 0.0).then_inc(S["padded"], 1)
            pool.memset(dAr[:, :, 0:1], 0.0).then_inc(S["const_ready"], 1)
            pool.memset(dtv[:, :], 0.0).then_inc(S["const_ready"], 1)
            pool.memset(bcp.rearrange("p d (b n) -> p d b n", n=PADL)[:, :, :, 0:NCONV - 1].rearrange("p d b n -> p (d b) n"),
                        0.0).then_inc(S["const_ready"], 1)
            pool.memset(qs[:, :], 0.0).then_inc(S["const_ready"], 1)
            pool.wait_ge(S["ids_ready"], 1)
            for b in range(NB):
                pool.indirect_dma_start(out=txt[:, b, :], out_offset=None, in_=i["emb"],
                                        in_offset=bass.IndirectOffsetOnAxis(ap=ids[:, b:b + 1], axis=0))\
                    .then_inc(S["gathered"], 16)
            pool.wait_ge(ln_turned[0], 3)
            pool.memset(XP.rearrange("p m (b n) -> p m b n", n=PADL)[:, :, :, 0:NCONV - 1].rearrange("p m b n -> p (m b) n"),
                        0.0).then_inc(S["padded"], 1)
            pool.wait_ge(S["ld_outw"], 32)
            for k in range(2 * KD):
                pool.tensor_scalar(outw[:, k, :], outw[:, k, :], normw[:, k:k + 1], 1.0, ALU.mult, ALU.mult).then_inc(S["outw_scaled"], 1)
            for n, (d, b) in enumerate(ITS):
                pool.wait_ge(S["yd_ready"], 3 * (n + 1))
                if n == 0:
                    pool.wait_ge(S["z_evac"], 24)
                pool.tensor_tensor(CV[:, d * KD:(d + 1) * KD, b * L:(b + 1) * L], w1y[:, n % 2, :, :],
                                   ZS[:, d * KD:(d + 1) * KD, b * L:(b + 1) * L], ALU.mult).then_inc(S["yz_ready"], 1)
            pool.wait_ge(S["bi_flip"], 2)
            pool.memset(SS[:, TT - 1, :], 0.0).then_inc(S["padded"], 1)

            pool.wait_ge(S["q_range"], 2)
            pool.partition_all_reduce(qs[:, 16:18], qs[:, 14:16], P, RMAX).then_inc(S["q_range_all"], 1)
            for c in range(2):
                n = DA if c == 0 else DB
                pool.wait_ge(S["q_uc"], c + 1)
                pool.tensor_scalar(UQ[0:n, c, :], UR[0:n, c, :], -ROUNDER, None, ALU.add).then_inc(S["q_ui"], 1)
            pool.wait_ge(S["ham_ready"], 1)
            pool.partition_all_reduce(qs[:, 31:32], qs[:, 30:31], P, RMAX).then_inc(S["ham_all"], 1)
            for m in range(KH):
                pool.wait_ge(S["hc_ready"], m + 1)
                pool.tensor_scalar(HQ[:, m, :], HG[:, m, :], -ROUNDER, None, ALU.add).then_inc(S["hi_ready"], 1)
            pool.wait_ge(S["or_ready"], 1)
            pool.partition_all_reduce(qs[:, 42:44], qs[:, 40:42], P, RMAX).then_inc(S["or_all"], 1)

            for b in range(NB):
                for g, (r, q) in enumerate(GROUPS):
                    pool.wait_ge(S["s_sum"], 6 * b + g + 1)
                    o = PRS[0:r, 6 * (b % 2) + g, 0:q * L].rearrange("p (a b) -> p a b", b=L)
                    pool.tensor_tensor(o, o, arc[0:r, 18 * (b % 2) + 3 * g:18 * (b % 2) + 3 * g + q].unsqueeze(2).to_broadcast([r, q, L]), ALU.mult).then_inc(S["p_norm"], 1)

            for e in range(EW):
                for c in range(3):
                    for m in range(KH):
                        n = (e * 3 + c) * KH + m
                        pool.wait_ge(S["g_silu"], n + 1)
                        pool.wait_ge(S["u_clip"], n + 1)
                        g = e * 3 + c
                        if m == 0 and g >= 2:
                            pool.wait_ge(S["e_mm"], 3 * (g - 1))
                        pool.tensor_tensor(HH[:, g % 2, m * CM:(m + 1) * CM], GS[:, n % 3, :], UM[:, n % 3, :], ALU.mult)\
                            .then_inc(S["hh_ready"], 1)

        @block.scalar
        def _(act):
            def ln(k, w=None):
                act.wait_ge(ln_var[k], TT)
                nc.scalar.activation(std[:, 0:TT], mv[:, :, 1], ACT.Sqrt, bias=cst[:, 0:1]).then_inc(ln_std[k], 1)
                if k == 0:
                    act.wait_ge(ln0_vx, 1)
                    nc.scalar.activation(std[:, TT:2 * TT], prod[:, :], ACT.Sqrt, bias=cst[:, 0:1]).then_inc(ln0_std2, 1)
                for g in range(3):
                    act.wait_ge(ln_turned[k], g + 1)
                    a, b = bank[2 * (g % 2)], bank[2 * (g % 2) + 1]
                    if w is None:
                        nc.scalar.copy(XTa[:, g * CM:(g + 1) * CM], a[:, 0:CM]).then_inc(ln_out[k], 1)
                        nc.scalar.copy(XTb[:, g * CM:(g + 1) * CM], b[0:DB, 0:CM]).then_inc(ln_out[k], 1)
                    else:
                        nc.scalar.activation(XTa[:, g * CM:(g + 1) * CM], a[:, 0:CM], ACT.Identity,
                                             scale=w[:, 0, 0:1], bias=w[:, 0, 1:2]).then_inc(ln_out[k], 1)
                        nc.scalar.activation(XTb[:, g * CM:(g + 1) * CM], b[0:DB, 0:CM], ACT.Identity,
                                             scale=w[0:DB, 1, 0:1], bias=w[0:DB, 1, 1:2]).then_inc(ln_out[k], 1)

            act.wait_ge(S["const_ready"], 11)
            act.wait_ge(S["ld_ln1"], 32)
            ln(0, ln1)
            for d in range(2):
                for c in range(4):
                    for m in range(3):
                        k = k_inproj(d, c, m)
                        act.wait_ge(S["inproj"], k + 1)
                        nc.scalar.activation(ZS[:, d * KD + m, c * 2 * L:(c + 1) * 2 * L], bank[k % 4][:, 0:2 * L], ACT.Silu)\
                            .then_inc(S["z_evac"], 1)
                if d == 0:
                    act.wait_ge(S["ld_dt"], 32)
                    nc.scalar.activation(alog[:, :], alog[:, :], ACT.Exp).then_inc(S["a_exp"], 1)
                    act.wait_ge(S["dt_abs"], 1)
                    nc.scalar.activation(dte[:, :], dte[:, :], ACT.Exp).then_inc(S["dt_exp"], 1)
                    act.wait_ge(S["dt_arg"], 1)
                    nc.scalar.activation(dA[:, :], dA[:, :], ACT.Exp, scale=-1.0).then_inc(S["dA_exp"], 1)
            for n, (d, b) in enumerate(ITS):
                act.wait_ge(S["convolved"], 4 * (d + 1))
                if n >= 2:
                    act.wait_ge(S["g_ready"], n - 1)
                    act.wait_ge(S["yd_ready"], 3 * (n - 1))
                nc.scalar.activation(xcs[:, n % 2, :, :], CV[:, d * KD:(d + 1) * KD, b * L:(b + 1) * L], ACT.Silu).then_inc(S["xc_ready"], 1)
                nc.scalar.activation(Bs[:, n % 2, :], bcv[0:NS, d, b * L:(b + 1) * L], ACT.Silu).then_inc(S["xc_ready"], 1)
                nc.scalar.activation(Cs[:, n % 2, :], bcv[32:32 + NS, d, b * L:(b + 1) * L], ACT.Silu).then_inc(S["xc_ready"], 1)
            act.wait_ge(S["yz_ready"], 16)
            for k in range(2 * KD):
                nc.scalar.activation(SQ[:, k, :], CV[:, k, :], ACT.Square).then_inc(S["sq_ready"], 1)
            act.wait_ge(S["ss_ready"], 1)
            nc.scalar.activation(rss[:, 0:2 * TT - 2], bank[7][:, 0:2 * TT - 2], ACT.Sqrt, scale=1.0 / DIN, bias=cst[:, 0:1]).then_inc(S["ss_std"], 1)
            nc.scalar.activation(rss[0:LAST, 2 * TT - 2:2 * TT], bank[7][0:LAST, 2 * TT - 2:2 * TT], ACT.Sqrt,
                                 scale=1.0 / DIN, bias=cst[0:LAST, 0:1]).then_inc(S["ss_std"], 1)
            act.wait_ge(S["ss_inv"], 2)
            for t in range(TT):
                for d in range(2):
                    n = 2 * t + d
                    act.wait_ge(S["op_ready"], n + 1)
                    nc.scalar.activation(BT[0:rows(t), t, d * D:(d + 1) * D], bank[n % 4][0:rows(t), 0:D], ACT.Identity,
                                         scale=rs[0:rows(t), n:n + 1]).then_inc(S["bt_ready"], 1)
            for g in range(3):
                n = CM if g < 2 else T - 2 * CM
                act.wait_ge(S["bt_turned"], g + 1)
                nc.scalar.copy(BI[:, 0, g * CM:g * CM + n], bank[4][:, 0:n]).then_inc(S["bi_act"], 1)
                nc.scalar.copy(BI[0:64, 1, g * CM:g * CM + n], bank[5][0:64, 0:n]).then_inc(S["bi_act"], 1)
            act.wait_ge(S["ld_ffw1"], 32)
            for k in range(3 * KH):
                c, m = divmod(k, KH)
                act.wait_ge(S["h1_ready"], k + 1)
                nc.scalar.activation(H1[:, m, c * CH:(c + 1) * CH], bank[k % 4][:, 0:CH], ACT.Gelu, bias=ffb1[:, m:m + 1]).then_inc(S["h1_out"], 1)
            for t in range(TT):
                act.wait_ge(S["f2_ready"], t + 1)
                nc.scalar.activation(G2[0:rows(t), t, :], bank[4 + t % 4][0:rows(t), 0:D], ACT.Gelu).then_inc(S["f2_out"], 1)
            act.wait_ge(S["ln2_var"], TT)
            nc.scalar.activation(std[:, 0:TT], mv[:, :, 1], ACT.Sqrt, bias=cst[:, 0:1]).then_inc(S["ln2_std"], 1)

            ln(1)
            act.wait_ge(S["q_gmax"], 1)
            nc.scalar.activation(qs[:, 6:8], qs[:, 4:6], ACT.Sqrt).then_inc(S["q_sqrt"], 1)
            nc.scalar.activation(qs[:, 10:12], qs[:, 8:10], ACT.Sqrt).then_inc(S["q_sqrt"], 1)
            act.wait_ge(S["q_fac"], 1)
            for c in range(2):
                n, xt = (DA, XTa) if c == 0 else (DB, XTb)
                nc.scalar.activation(UR[0:n, c, :], xt[0:n, 0:T], ACT.Identity, scale=qs[0:n, 24 + c:25 + c], bias=cst[0:n, 1:2]).then_inc(S["q_u"], 1)
            for n in range(3 * KH):
                c, m = divmod(n, KH)
                act.wait_ge(S["hq_mm"], n + 1)
                nc.scalar.activation(HG[:, m, c * CH:(c + 1) * CH], bank[n % 4][:, 0:CH], ACT.Gelu,
                                     scale=qs[:, 50 + m:51 + m], bias=qb1[:, m:m + 1]).then_inc(S["hg_ready"], 1)
            act.wait_ge(S["hs_ready"], 1)
            for m in range(KH):
                nc.scalar.activation(HG[:, m, :], HG[:, m, :], ACT.Identity, scale=qs[:, 33:34], bias=cst[:, 1:2]).then_inc(S["hr_ready"], 1)
            for n in range(6):
                c, m = divmod(n, 2)
                r = DA if m == 0 else DB
                act.wait_ge(S["ot_mm"], n + 1)
                nc.scalar.activation(OT[0:r, m, c * CH:(c + 1) * CH], bank[n % 4][0:r, 0:CH], ACT.Identity,
                                     scale=qs[0:r, 34 + m:35 + m], bias=qb2[0:r, m:m + 1]).then_inc(S["ot_ready"], 1)
            act.wait_ge(S["of_ready"], 1)
            for m in range(2):
                r = DA if m == 0 else DB
                nc.scalar.activation(OT[0:r, m, :], OT[0:r, m, :], ACT.Identity, scale=qs[0:r, 46:47], bias=cst[0:r, 1:2]).then_inc(S["om_ready"], 1)

            ln(2)
            for b in range(NB + 1):
                p = b % 2
                if b < NB:
                    for j in range(4):
                        act.wait_ge(S["qk_mm"], 4 * b + j + 1)
                        nc.scalar.copy(QK[:, p, j * 3 * L:(j + 1) * 3 * L], bank[j % 2][:, 0:3 * L]).then_inc(S["qk_out"], 1)
                    for j in range(2):
                        act.wait_ge(S["v_mm"], 2 * b + j + 1)
                        nc.scalar.copy(Va[:, p, j * CM:(j + 1) * CM], bank[0][:, 0:CM]).then_inc(S["v_out"], 1)
                        nc.scalar.copy(Vb[:, p, j * CM:(j + 1) * CM], bank[1][0:R, 0:CM]).then_inc(S["v_out"], 1)
                    for g, (r, q) in enumerate(GROUPS):
                        act.wait_ge(S["s_sub"], 6 * b + g + 1)
                        o = PRS[0:r, 6 * p + g, 0:q * L]
                        nc.scalar.activation(o, o, ACT.Exp, scale=0.125).then_inc(S["s_exp"], 1)
                if b:
                    c = b - 1
                    for g in range(4):
                        act.wait_ge(S["p_turned"], 4 * c + g + 1)
                        if c:
                            act.wait_ge(S["av_mm"], 2 * c)
                        nc.scalar.copy(PT[:, 3 * g:3 * g + 3, :], bank[4][:, 0:3 * L].rearrange("p (a b) -> p a b", b=L)).then_inc(S["pt_act"], 1)
                    for j in range(2):
                        act.wait_ge(S["av_mm"], 2 * c + j + 1)
                        nc.scalar.copy(OA[:, 3 * j:3 * j + 3, c * L:(c + 1) * L],
                                       bank[6 + j][:, 0:3 * L].rearrange("p (a b) -> p a b", b=L)).then_inc(S["av_out"], 1)

            ln(3)
            act.wait_ge(S["g_abs"], 1)
            nc.scalar.activation(ge[:, :], gn[:, :], ACT.Exp).then_inc(S["g_exp"], 1)
            act.wait_ge(S["g_sp"], 1)
            nc.scalar.activation(gs[:, :], gs[:, :], ACT.Sqrt).then_inc(S["g_sqrt"], 1)
            for n in range(EW * 3 * KH):
                act.wait_ge(S["g_min"], n + 1)
                if n >= 3:
                    act.wait_ge(S["hh_ready"], n - 2)
                nc.scalar.activation(GS[:, n % 3, :], GM[:, n % 3, :], ACT.Silu).then_inc(S["g_silu"], 1)

        @block.tensor
        def _(pe):
            mm = nc.tensor.matmul

            def turn(k, src):
                for g in range(3):
                    pe.wait_ge(ln_x[k], 3 * (g + 1))
                    if g == 2:
                        pe.wait_ge(ln_out[k], 2)
                    a, b = bank[2 * (g % 2)], bank[2 * (g % 2) + 1]
                    for j in range(3):
                        t = 3 * g + j
                        nc.tensor.transpose(a[:, j * P:(j + 1) * P], src[:, t, 0:DA], ident)
                        last = nc.tensor.transpose(b[0:DB, j * P:(j + 1) * P], src[:, t, DA:D], ident)
                    last.then_inc(ln_turned[k], 1)

            pe.wait_ge(S["const_ready"], 11)
            pe.wait_ge(S["p_step"], 2)
            pe.wait_ge(S["score_ready"], 1)
            for b in range(NB):
                last = nc.tensor.transpose(bank[2 + b // 4][0:NX, (b % 4) * 76:(b % 4 + 1) * 76], score[:, b * NX:(b + 1) * NX],
                                           identw[0:76, 0:76])
                if b % 4 == 3:
                    last.then_inc(S["scoreT"], 1)
            pe.wait_ge(S["ld_embed"], 48)
            for j in range(NB // 2):
                for k in range(KI):
                    last = mm(bank[j // 2][:, (j % 2) * D:(j % 2 + 1) * D], patches[:, k, j * P:(j + 1) * P], tokw[:, k, :],
                              start=k == 0, stop=k == KI - 1)
                if j % 2:
                    last.then_inc(S["img_out"], 1)
            pe.wait_ge(S["img_ready"], 2)
            pe.wait_ge(S["ids_ready"], 1)
            turn(0, XS)

            def inproj(d):
                xa, xb = (XTa, XTb) if d == 0 else (XRa, XRb)
                for c in range(4):
                    for m in range(7):
                        k = k_inproj(d, c, m)
                        if k >= 4:
                            pe.wait_ge(*inproj_free(k - 4))
                        cols = slice(m * P, m * P + P) if m < 6 else slice(CB, CB + 48)
                        M = P if m < 6 else 48
                        mm(bank[k % 4][0:M, 0:2 * L], inw[:, 2 * d, cols], xa[:, c * 2 * L:(c + 1) * 2 * L], start=True, stop=False)
                        mm(bank[k % 4][0:M, 0:2 * L], inw[0:DB, 2 * d + 1, cols], xb[:, c * 2 * L:(c + 1) * 2 * L],
                           start=False, stop=True).then_inc(S["inproj"], 1)

            pe.wait_ge(ln_out[0], 6)
            pe.wait_ge(S["ld_inw"], 64)
            inproj(0)
            pe.wait_ge(S["flipped"], 2)
            for d, b in ITS:
                xa, xb = (XTa, XTb) if d == 0 else (XRa, XRb)
                for at, n, col in ((0, P, DTC(d, b)), (P, R, 96 + DTC(d, b))):
                    cols = slice(b * L + at, b * L + at + n)
                    mm(bank[4][0:n, col:col + NH], xa[:, cols], inw[:, 2 * d, CDT:WCOLS], start=True, stop=False)
                    last = mm(bank[4][0:n, col:col + NH], xb[:, cols], inw[0:DB, 2 * d + 1, CDT:WCOLS], start=False, stop=True)
            last.then_inc(S["dt_ready"], 1)
            inproj(1)

            def front(n):
                d, b = ITS[n]
                p = n % 2
                pe.wait_ge(S["xc_ready"], 3 * (n + 1))
                if n == 0:
                    pe.wait_ge(S["dA_ready"], 1)
                    pe.wait_ge(S["x_evac"], 32)
                    pe.wait_ge(S["z_evac"], 24)
                else:
                    pe.wait_ge(S["decay_used"], 2 * n)
                for g in range(2):
                    for h in range(3):
                        col = DTC(d, b) + 3 * g + h
                        o = bank[3 + g]
                        mm(o[:, h * L:h * L + P], dA[:, col:col + 1].to_broadcast([P, P]), ident, start=True, stop=True)
                        last = mm(o[:, h * L + P:(h + 1) * L], dA[0:R, 96 + col:97 + col].to_broadcast([R, P]), identw[0:R, 0:R],
                                  start=True, stop=True)
                    last.then_inc(S["decay_ready"], 1)
                if n:
                    pe.wait_ge(S["dtx_ready"], 2 * n)
                for m in range(KD):
                    nc.tensor.transpose(bank[0][:, m * P:(m + 1) * P], xcs[:, p, m, 0:P], ident)
                    last = nc.tensor.transpose(bank[1][0:R, m * P:(m + 1) * P], xcs[:, p, m, P:L], ident)
                last.then_inc(S["xc_turned"], 1)
                if n >= 2:
                    pe.wait_ge(S["m_ready"], 2 * (n - 1))
                o = bank[2 if p == 0 else 7]
                mm(o[:, 0:L], Bs[:, p, 0:P], Cs[:, p, :], start=True, stop=True)
                mm(o[0:R, L:L + R], Bs[:, p, P:L], Cs[:, p, P:L], start=True, stop=True).then_inc(S["g_ready"], 1)

            def back(n):
                p = n % 2
                pe.wait_ge(S["m_ready"], 2 * (n + 1))
                if n >= 2:
                    pe.wait_ge(S["yd_ready"], 3 * (n - 1))
                o = bank[5 + p]
                for h in range(NH):
                    q, r = h // 2, (h % 2) * 64
                    mm(o[r:r + 64, q * L:(q + 1) * L], dtx[:, p, h * 64:(h + 1) * 64], MM[:, p, h, :], start=True, stop=False)
                    last = mm(o[r:r + 64, q * L + P:(q + 1) * L], dtxr[:, p, h * 64:(h + 1) * 64], MMr[:, p, h, :],
                              start=False, stop=True)
                last.then_inc(S["y_ready"], 1)

            for n in range(len(ITS) + 1):
                if n < len(ITS):
                    front(n)
                if n:
                    back(n - 1)
            pe.wait_ge(S["sq_ready"], 2 * KD)
            for t in range(TT):
                for d in range(2):
                    for k in range(KD):
                        last = mm(bank[7][0:rows(t), 2 * t + d:2 * t + d + 1], SQ[:, d * KD + k, t * P:t * P + rows(t)], ones[:, 0:1],
                                  start=k == 0, stop=k == KD - 1)
            last.then_inc(S["ss_ready"], 1)
            pe.wait_ge(S["outw_scaled"], 2 * KD)
            for t in range(TT):
                for d in range(2):
                    n = 2 * t + d
                    if n >= 4:
                        pe.wait_ge(S["bt_ready"], n - 3)
                    for k in range(KD):
                        last = mm(bank[n % 4][0:rows(t), 0:D], CV[:, d * KD + k, t * P:t * P + rows(t)], outw[:, d * KD + k, :],
                                  start=k == 0, stop=k == KD - 1)
                    last.then_inc(S["op_ready"], 1)
            for g in range(3):
                pe.wait_ge(S["bt_ready"], 6 * (g + 1))
                if g == 0:
                    pe.wait_ge(S["yd_ready"], 48)
                else:
                    pe.wait_ge(S["bi_act"], 2 * g)
                    pe.wait_ge(S["bi_dve"], 2 * g)
                for j in range(3):
                    t = 3 * g + j
                    for k in range(3):
                        last = nc.tensor.transpose(bank[4 + k][:, j * P:j * P + rows(t)], BT[0:rows(t), t, k * P:(k + 1) * P],
                                                   identw[0:rows(t), 0:rows(t)])
                last.then_inc(S["bt_turned"], 1)
            pe.wait_ge(S["bi_act"], 6)
            pe.wait_ge(S["bi_flip"], 2)
            pe.wait_ge(S["ld_ffw1"], 32)
            for n in range(3 * KH):
                c, m = divmod(n, KH)
                if n < 4:
                    pe.wait_ge(S["bt_ready"], 18)
                else:
                    pe.wait_ge(S["h1_out"], n - 3)
                for k in range(KD):
                    last = mm(bank[n % 4][:, 0:CH], ffw1[:, k, m * P:(m + 1) * P], BI[:, k, c * CH:(c + 1) * CH],
                              start=k == 0, stop=k == KD - 1)
                last.then_inc(S["h1_ready"], 1)
            pe.wait_ge(S["h1_out"], 3 * KH)
            pe.wait_ge(S["ld_ffw2"], 32)
            for t in range(TT):
                if t >= 4:
                    pe.wait_ge(S["f2_out"], t - 3)
                o = bank[4 + t % 4][0:rows(t), 0:D]
                for k in range(KH):
                    mm(o, H1[:, k, t * P:t * P + rows(t)], ffw2[:, k, :], start=k == 0, stop=False)
                mm(o, ones[0:1, 0:rows(t)], ffb2[:, :], start=False, stop=True).then_inc(S["f2_ready"], 1)

            turn(1, X)
            pe.wait_ge(S["q_diag"], 2)
            pe.wait_ge(ln_out[1], 6)
            mm(bank[4][:, 0:DA], ones[:, :], csdiag[:, 0:DA], start=True, stop=True)
            mm(bank[4][:, DA:D], ones[0:DB, :], csdiag[0:DB, DA:D], start=True, stop=True).then_inc(S["q_csb"], 1)
            for k in range(KH):
                pe.wait_ge(S["q2_ready"], 2)
                o = bank[6 + k % 2]
                if k >= 2:
                    pe.wait_ge(S["q2_out"], k - 1)
                mm(o[:, 0:DA], q2[:, 0, k * P:(k + 1) * P], identb[:, :], start=True, stop=True)
                mm(o[:, DA:D], q2[0:DB, 1, k * P:(k + 1) * P], identb[0:DB, 0:DB], start=True, stop=True).then_inc(S["q2_turned"], 1)
            pe.wait_ge(S["q1_ready"], 1)
            for k in range(KH):
                if k >= 2:
                    pe.wait_ge(S["q1_out"], k - 1)
                elif k == 0:
                    pe.wait_ge(S["q2_out"], KH)
                o = bank[6 + k % 2]
                mm(o[:, 0:P], q1[:, k, 0:DA], identb[:, :], start=True, stop=True)
                mm(o[0:DB, P:2 * P], q1[:, k, DA:D], identb[:, :], start=True, stop=True).then_inc(S["q1_turned"], 1)
            pe.wait_ge(S["q1_out"], KH)
            pe.wait_ge(S["q_ui"], 2)
            for n in range(3 * KH):
                c, m = divmod(n, KH)
                if n >= 4:
                    pe.wait_ge(S["hg_ready"], n - 3)
                mm(bank[n % 4][:, 0:CH], q1t[:, 0, m * P:(m + 1) * P], UQ[:, 0, c * CH:(c + 1) * CH], start=True, stop=False)
                mm(bank[n % 4][:, 0:CH], q1t[0:DB, 1, m * P:(m + 1) * P], UQ[0:DB, 1, c * CH:(c + 1) * CH],
                   start=False, stop=True).then_inc(S["hq_mm"], 1)
            for n in range(6):
                c, m = divmod(n, 2)
                r = DA if m == 0 else DB
                if n == 0:
                    pe.wait_ge(S["hi_ready"], KH)
                if n >= 4:
                    pe.wait_ge(S["ot_ready"], n - 3)
                for k in range(KH):
                    last = mm(bank[n % 4][0:r, 0:CH], q2t[:, k, m * DA:m * DA + r], HQ[:, k, c * CH:(c + 1) * CH],
                              start=k == 0, stop=k == KH - 1)
                last.then_inc(S["ot_mm"], 1)
            for t in range(TT):
                pe.wait_ge(S["oq_ready"], 2)
                if t >= 4:
                    pe.wait_ge(S["h_ffn"], t - 3)
                elif t == 0:
                    pe.wait_ge(S["ot_ready"], 6)
                o = bank[4 + t % 4]
                nc.tensor.transpose(o[0:rows(t), 0:DA], OT[:, 0, t * P:t * P + rows(t)], ident)
                nc.tensor.transpose(o[0:rows(t), DA:D], OT[0:DB, 1, t * P:t * P + rows(t)], identw[0:DB, 0:DB]).then_inc(S["oq_turned"], 1)

            turn(2, X)
            pe.wait_ge(ln_out[2], 6)
            pe.wait_ge(S["ld_att"], 16 * 8)
            def attend_front(b):
                p = b % 2
                cols = slice(b * L, (b + 1) * L)
                for j in range(4):
                    if j < 2 and b:
                        pe.wait_ge(S["v_out"], 4 * b)
                    if j >= 2:
                        pe.wait_ge(S["qk_out"], 4 * b + j - 1)
                    for q in range(3):
                        m = 3 * j + q
                        w, mc = (awq, m) if m < 6 else (awk, m - 6)
                        o = bank[j % 2][:, q * L:(q + 1) * L]
                        mm(o, w[:, 0, mc * P:(mc + 1) * P], XTa[:, cols], start=True, stop=False)
                        last = mm(o, w[0:DB, 1, mc * P:(mc + 1) * P], XTb[:, cols], start=False, stop=True)
                    last.then_inc(S["qk_mm"], 1)
                for j in range(2):
                    if j == 0:
                        pe.wait_ge(S["qk_out"], 4 * (b + 1))
                    else:
                        pe.wait_ge(S["v_out"], 4 * b + 2)
                    for at, n, o in ((0, P, bank[0]), (P, R, bank[1])):
                        tc = slice(b * L + at, b * L + at + n)
                        mm(o[0:n, 0:CM], XTa[:, tc], awv[:, 0, j * CM:(j + 1) * CM], start=True, stop=False)
                        last = mm(o[0:n, 0:CM], XTb[:, tc], awv[0:DB, 1, j * CM:(j + 1) * CM], start=False, stop=True)
                    last.then_inc(S["v_mm"], 1)
                for w in range(3):
                    if w or b:
                        pe.wait_ge(S["s_sub"], 6 * b + 2 * w)
                    for e in (range(3 * w, 3 * w + 3) if w < 2 else range(6)):
                        for par in range(2):
                            r, o = par * 64, bank[2 + par]
                            keys = QK[r:r + 64, p, (6 + e) * L:(7 + e) * L]
                            if w < 2:
                                q = e % 3
                                last = mm(o[:, q * L:(q + 1) * L], QK[r:r + 64, p, e * L:e * L + P], keys, start=True, stop=True)
                            else:
                                sl, q = (e % 3) * 32, e // 3
                                last = mm(o[sl:sl + 32, q * L:(q + 1) * L], QK[r:r + 64, p, (e + 1) * L - 32:(e + 1) * L], keys,
                                          start=True, stop=True)
                            if e == (3 * w + 2 if w < 2 else 5):
                                last.then_inc(S["s_mm"], 1)

            def attend_back(b):
                p = b % 2
                for g in range(4):
                    n = 4 * b + g
                    pe.wait_ge(S["p_norm"], 6 * (b + 1))
                    if n >= 1:
                        pe.wait_ge(S["pt_act"], n)
                        pe.wait_ge(S["pt_dve"], n)
                    for q in range(3):
                        h = 3 * g + q
                        par, e = h % 2, h // 2
                        m, c = 2 * (e // 3) + par, (e % 3) * L
                        u, r = (e // 3) * L, (e % 3) * 32 + 32 - R
                        nc.tensor.transpose(bank[4][:, q * L:q * L + P], PRS[:, 6 * p + m, c:c + P], ident)
                        nc.tensor.transpose(bank[5][0:R, q * L:q * L + P], PRS[:, 6 * p + m, c + P:c + L], ident)
                        rest = identw[0:96, r:r + R]
                        mm(bank[4][:, q * L + P:(q + 1) * L], PRS[0:96, 6 * p + 4 + par, u:u + P], rest, start=True, stop=True)
                        last = mm(bank[5][0:R, q * L + P:(q + 1) * L], PRS[0:96, 6 * p + 4 + par, u + P:u + L], rest, start=True, stop=True)
                    last.then_inc(S["p_turned"], 1)
                for j in range(2):
                    pe.wait_ge(S["pt_act"], 4 * b + 2 * j + 2)
                    pe.wait_ge(S["pt_dve"], 4 * b + 2 * j + 2)
                    pe.wait_ge(S["v_out"], 4 * (b + 1))
                    if b:
                        pe.wait_ge(S["av_out"], 2 * (b - 1) + j + 1)
                    for q in range(6):
                        h = 6 * j + q
                        r, m = (h % 2) * 64, q // 2
                        o = bank[6 + j][r:r + 64, m * L:(m + 1) * L]
                        mm(o, Va[:, p, h * 64:(h + 1) * 64], PT[:, h, :], start=True, stop=False)
                        last = mm(o, Vb[:, p, h * 64:(h + 1) * 64], PTr[:, h, :], start=False, stop=True)
                    last.then_inc(S["av_mm"], 1)

            for b in range(NB + 1):
                if b < NB:
                    attend_front(b)
                if b:
                    attend_back(b - 1)
            pe.wait_ge(S["av_out"], 2 * NB)
            for t in range(TT):
                if t >= 4:
                    pe.wait_ge(S["h_att"], t - 3)
                o = bank[t % 4][0:rows(t), 0:D]
                for k in range(KH):
                    mm(o, OA[:, k, t * P:t * P + rows(t)], awo[:, k, :], start=k == 0, stop=False)
                mm(o, ones[0:1, 0:rows(t)], abo[:, :], start=False, stop=True).then_inc(S["wo_mm"], 1)

            turn(3, X)
            pe.wait_ge(ln_out[3], 6)
            pe.wait_ge(S["ld_gate"], 48)
            for t in range(TT):
                mm(bank[4][:, t * NE:(t + 1) * NE], XTa[:, t * P:(t + 1) * P], gatew[:, 0, :], start=True, stop=False)
                last = mm(bank[4][:, t * NE:(t + 1) * NE], XTb[:, t * P:(t + 1) * P], gatew[0:DB, 1, :], start=False, stop=True)
            last.then_inc(S["g_mm"], 1)

            def up(e, c):
                k = e % 2
                for m in range(KH):
                    n = (e * 3 + c) * KH + m
                    for q, w in ((0, ew1[k]), (1, ew3[k])):
                        if n >= 2:
                            pe.wait_ge(S["g_min"] if q == 0 else S["u_clip"], n - 1)
                        o = bank[2 * (n % 2) + q][:, 0:CM]
                        mm(o, w[:, 0, m * P:(m + 1) * P], XTa[:, c * CM:(c + 1) * CM], start=True, stop=False)
                        mm(o, w[0:DB, 1, m * P:(m + 1) * P], XTb[:, c * CM:(c + 1) * CM], start=False, stop=True).then_inc(S["gu_mm"], 1)

            def down(e, c):
                g = e * 3 + c
                pe.wait_ge(S["hh_ready"], KH * (g + 1))
                for j in range(3):
                    n = 3 * g + j
                    if n == 0:
                        pe.wait_ge(S["g_abs"], 1)
                    if n >= 4:
                        pe.wait_ge(S["e_acc"], n - 3)
                    for k in range(KH):
                        last = mm(bank[4 + n % 4][:, 0:D], HH[:, g % 2, k * CM + j * P:k * CM + (j + 1) * P], ew2[e % 2][:, k, :],
                                  start=k == 0, stop=k == KH - 1)
                    last.then_inc(S["e_mm"], 1)

            for g in range(3 * EW + 1):
                if g < 3 * EW:
                    if g % 3 == 0:
                        pe.wait_ge(S["ld_e"], 80 * (g // 3 + 1))
                    up(g // 3, g % 3)
                if g:
                    down((g - 1) // 3, (g - 1) % 3)

        @block.vector
        def _(dve):
            v = nc.vector
            st = Steps(dve, S["v_step"])

            def ln(k):
                for t in range(TT):
                    st.add(v.bn_stats(stats[:, t, :], H[:, t, :]))
                st.wait()
                for t in range(TT):
                    v.bn_aggr(mv[:, t, :], stats[:, t, :]).then_inc(ln_var[k], 1)
                dve.wait_ge(ln_var[k], TT)
                dve.wait_ge(ln_std[k], 1)
                st.add(v.reciprocal(rstd[:, :], std[:, 0:TT]))
                st.wait()
                if k == 0:
                    st.add(v.tensor_tensor(prod[:, :], mv[:, :, 1], rstd[:, :], ALU.mult))
                    st.wait()
                    v.tensor_tensor(prod[:, :], prod[:, :], rstd[:, :], ALU.mult).then_inc(ln0_vx, 1)
                    dve.wait_ge(ln0_std2, 1)
                    st.add(v.reciprocal(rstd2[:, :], std[:, TT:2 * TT]))
                    st.wait()
                    st.add(v.tensor_tensor(rstd2[:, :], rstd2[:, :], rstd[:, :], ALU.mult))
                    st.wait()
                    for t in range(TT):
                        v.tensor_scalar(XS[:, t, :], H[:, t, :], mv[:, t, 0:1], rstd2[:, t:t + 1], ALU.subtract, ALU.mult).then_inc(ln_x[0], 1)
                        st.add(v.tensor_scalar(X[:, t, :], H[:, t, :], mv[:, t, 0:1], rstd[:, t:t + 1], ALU.subtract, ALU.mult))
                    return
                for t in range(TT):
                    v.tensor_scalar(X[:, t, :], H[:, t, :], mv[:, t, 0:1], rstd[:, t:t + 1], ALU.subtract, ALU.mult).then_inc(ln_x[k], 1)

            def log1p_series(e, t, q, p, s):
                st.add(v.tensor_scalar(t, e, 2.0, None, ALU.add))
                st.wait()
                st.add(v.reciprocal(t, t))
                st.wait()
                st.add(v.tensor_tensor(s, e, t, ALU.mult))
                st.wait()
                st.add(v.tensor_tensor(q, s, s, ALU.mult))
                st.wait()
                st.add(v.tensor_scalar(p, q, 1.0 / 15, None, ALU.mult))
                st.wait()
                for c in (13, 11, 9, 7, 5, 3):
                    st.add(v.scalar_tensor_tensor(out=p, in0=p, scalar=1.0 / c, in1=q, op0=ALU.add, op1=ALU.mult))
                    st.wait()
                st.add(v.scalar_tensor_tensor(out=p, in0=p, scalar=1.0, in1=s, op0=ALU.add, op1=ALU.mult))
                st.wait()
                st.add(v.tensor_scalar(p, p, 2.0, None, ALU.mult))
                st.wait()

            dve.wait_ge(S["const_ready"], 11)
            dve.wait_ge(S["iota_ready"], 2)
            dve.wait_ge(S["ld_tok"], 48)
            st.add(v.tensor_tensor(eq.rearrange("p (b n) -> p b n", n=NX), cur, shf, ALU.is_equal))
            st.wait()
            st.add(v.tensor_tensor_scan(run, ones[0:76, 0:1].to_broadcast([76, NB * NX]), eq, 0.0, ALU.add, ALU.mult))
            st.wait()
            v.tensor_scalar(score, run, 128.0, qcol[0:76, :], ALU.mult, ALU.add).then_inc(S["score_ready"], 1)
            for g in range(2):
                dve.wait_ge(S["scoreT"], g + 1)
                st.add(v.tensor_reduce(best[:, 4 * g:4 * g + 4], bank[2 + g][0:NX, 0:4 * 76].rearrange("p (a b) -> p a b", b=76), AX.X, ALU.max))
            st.wait()
            st.add(v.tensor_scalar(found[:, :], best[:, :], 128.0, None, ALU.is_ge))
            for b in range(NB):
                st.add(v.scalar_tensor_tensor(out=junk[:, b, :], in0=bank[2 + b // 4][0:NX, (b % 4) * 76:(b % 4 + 1) * 76],
                                              scalar=best[:, b:b + 1], in1=nxt[:, b, :], op0=ALU.is_equal, op1=ALU.mult,
                                              accum_out=pick[:, b:b + 1]))
            st.wait()
            v.tensor_copy(ids[:, :], pick[:, :]).then_inc(S["ids_ready"], 1)
            for g in range(2):
                dve.wait_ge(S["img_out"], g + 1)
                v.tensor_tensor(img[:, 2 * g:2 * g + 2, :], bank[g][:, 0:2 * D].rearrange("p (a b) -> p a b", b=D),
                                tokb.unsqueeze(1).to_broadcast([P, 2, D]), ALU.add).then_inc(S["img_ready"], 1)
            dve.wait_ge(S["gathered"], 16 * NB)
            v.tensor_tensor(txt, txt, found[:, :].unsqueeze(2).to_broadcast([NX, NB, D]), ALU.mult).then_inc(S["txt_ready"], 1)

            dve.wait_ge(S["h_loaded"], 32)
            ln(0)
            dve.wait_ge(ln_out[0], 6)
            v.tensor_copy(XRa[:, 0:T].rearrange("p (b n) -> p b n", n=L), XTa[:, 0:T].rearrange("p (b n) -> p b n", n=L)[:, :, ::-1])\
                .then_inc(S["flipped"], 1)
            v.tensor_copy(XRb[:, 0:T].rearrange("p (b n) -> p b n", n=L), XTb[:, 0:T].rearrange("p (b n) -> p b n", n=L)[:, :, ::-1])\
                .then_inc(S["flipped"], 1)
            XP4 = XP.rearrange("p m (b n) -> p m b n", n=PADL)
            BP4 = bcp.rearrange("p m (b n) -> p m b n", n=PADL)

            def evac(d, c):
                for m in range(3, 7):
                    k = k_inproj(d, c, m)
                    dve.wait_ge(S["inproj"], k + 1)
                    if m < 6:
                        v.tensor_copy(XP4[:, d * KD + m - 3, 2 * c:2 * c + 2, NCONV - 1:PADL],
                                      bank[k % 4][:, 0:2 * L].rearrange("p (b n) -> p b n", n=L)).then_inc(S["x_evac"], 1)
                    else:
                        v.tensor_copy(BP4[:, d, 2 * c:2 * c + 2, NCONV - 1:PADL],
                                      bank[k % 4][0:48, 0:2 * L].rearrange("p (b n) -> p b n", n=L)).then_inc(S["x_evac"], 1)

            def conv(d, m):
                n = P if m < 3 else 48
                dve.wait_ge(S["x_evac"], 16 * (d + 1))
                o = (CV[:, d * KD + m, :] if m < 3 else bcv[:, d, :]).rearrange("p (b n) -> p b n", n=L)
                for k in range(NCONV):
                    src = (XP4[:, d * KD + m, :, k:k + L] if m < 3 else BP4[:, d, :, k:k + L])
                    if k == 0:
                        st.add(v.tensor_scalar(o, src, convw[0:n, d, m, 0:1], convb[0:n, d, m:m + 1], ALU.mult, ALU.add))
                        st.wait()
                        continue
                    ins = v.scalar_tensor_tensor(out=o, in0=src, scalar=convw[0:n, d, m, k:k + 1], in1=o, op0=ALU.mult, op1=ALU.add)
                    if k < NCONV - 1:
                        st.add(ins)
                        st.wait()
                    else:
                        ins.then_inc(S["convolved"], 1)

            dve.wait_ge(S["padded"], 2)
            dve.wait_ge(S["ld_conv"], 48)
            for c in range(4):
                evac(0, c)
            dve.wait_ge(S["dt_ready"], 1)
            dve.wait_ge(S["ld_dt"], 32)
            st.add(v.tensor_tensor(dtv[:, 0:96], bank[4][:, 0:96], dtrow[:, 0:96], ALU.add))
            st.add(v.tensor_tensor(dtv[0:R, 96:192], bank[4][0:R, 96:192], dtrow[0:R, 96:192], ALU.add))
            st.wait()
            v.scalar_tensor_tensor(out=dte[:, :], in0=dtv[:, :], scalar=-1.0, in1=dtv[:, :], op0=ALU.mult, op1=ALU.min).then_inc(S["dt_abs"], 1)
            dve.wait_ge(S["dt_exp"], 1)
            log1p_series(dte[:, :], dtt[:, :], dtq[:, :], dtp[:, :], dts[:, :])
            st.add(v.scalar_tensor_tensor(out=dts[:, :], in0=dtv[:, :], scalar=0.0, in1=dtp[:, :], op0=ALU.max, op1=ALU.add))
            st.wait()
            dve.wait_ge(S["a_exp"], 1)
            v.tensor_tensor(dA[:, :], dts[:, :], alog[:, :], ALU.mult).then_inc(S["dt_arg"], 1)
            dve.wait_ge(S["dA_exp"], 1)
            v.memset(dA[0:1, 0:96], 0.0).then_inc(S["dA_ready"], 1)
            for c in range(4):
                evac(1, c)
                conv(0, c)
            for m in range(4):
                conv(1, m)

            def scan_part(n):
                d, b = ITS[n]
                p = n % 2
                col = DTC(d, b)
                if n:
                    dve.wait_ge(S["m_ready"], 2 * n)
                for g in range(2):
                    dve.wait_ge(S["decay_ready"], 2 * n + g + 1)
                    e = bank[3 + g][:, 0:3 * L].rearrange("p (h n) -> p h n", n=L)
                    st.add(v.tensor_tensor_scan(DD[:, 3 * g:3 * g + 3, :].rearrange("p h n -> p (h n)"), bank[3 + g][:, 0:3 * L], ident3[:, :],
                                                0.0, ALU.mult, ALU.add))
                    v.tensor_copy(dAr[:, 3 * g:3 * g + 3, 1:R], e[0:R, :, P + 1:L]).then_inc(S["decay_used"], 1)
                dve.wait_ge(S["xc_turned"], n + 1)
                v.tensor_tensor(dtx[:, p, :].rearrange("p (h c) -> p h c", c=64), bank[0][:, 0:DIN].rearrange("p (h c) -> p h c", c=64),
                                dts[:, col:col + NH].unsqueeze(2).to_broadcast([P, NH, 64]), ALU.mult).then_inc(S["dtx_ready"], 1)
                v.tensor_tensor(dtxr[:, p, :].rearrange("p (h c) -> p h c", c=64), bank[1][0:R, 0:DIN].rearrange("p (h c) -> p h c", c=64),
                                dts[0:R, 96 + col:96 + col + NH].unsqueeze(2).to_broadcast([R, NH, 64]), ALU.mult).then_inc(S["dtx_ready"], 1)
                dve.wait_ge(S["decay_used"], 2 * n + 2)
                st.add(v.tensor_tensor_scan(DDr[:, :, :].rearrange("p h n -> p (h n)"), dAr[:, :, :].rearrange("p h n -> p (h n)"), identr[:, :],
                                            0.0, ALU.mult, ALU.add))
                st.wait()
                dve.wait_ge(S["g_ready"], n + 1)
                G = bank[2 if p == 0 else 7]
                v.tensor_tensor(MM[:, p, :, :], DD[:, :, :], G[:, 0:L].unsqueeze(1).to_broadcast([P, NH, L]), ALU.mult)\
                    .then_inc(S["m_ready"], 1)
                v.tensor_tensor(MMr[:, p, :, :], DDr[:, :, :], G[0:R, L:L + R].unsqueeze(1).to_broadcast([R, NH, R]), ALU.mult)\
                    .then_inc(S["m_ready"], 1)

            def skip_part(n):
                d, b = ITS[n]
                p = n % 2
                dve.wait_ge(S["y_ready"], n + 1)
                if n >= 2:
                    dve.wait_ge(S["yz_ready"], n - 1)
                for m in range(KD):
                    v.scalar_tensor_tensor(out=w1y[:, p, m, :], in0=xcs[:, p, m, :], scalar=skipd[:, d, m:m + 1],
                                           in1=bank[5 + p][:, m * L:(m + 1) * L], op0=ALU.mult, op1=ALU.add).then_inc(S["yd_ready"], 1)

            for n in range(len(ITS) + 1):
                if n < len(ITS):
                    scan_part(n)
                if n:
                    skip_part(n - 1)
            dve.wait_ge(S["ss_std"], 2)
            v.reciprocal(rs[:, 0:2 * TT - 2], rss[:, 0:2 * TT - 2]).then_inc(S["ss_inv"], 1)
            v.reciprocal(rs[0:LAST, 2 * TT - 2:2 * TT], rss[0:LAST, 2 * TT - 2:2 * TT]).then_inc(S["ss_inv"], 1)
            dve.wait_ge(S["op_ready"], 18)
            for g in range(3):
                n = CM if g < 2 else T - 2 * CM
                dve.wait_ge(S["bt_turned"], g + 1)
                v.tensor_copy(BIr[64:P, 0, g * CM:g * CM + n], bank[5][64:P, 0:n]).then_inc(S["bi_dve"], 1)
                v.tensor_copy(BIr[:, 1, g * CM:g * CM + n], bank[6][:, 0:n]).then_inc(S["bi_dve"], 1)
            dve.wait_ge(S["bi_dve"], 6)
            v.tensor_copy(BI[64:P, 1, :].rearrange("p (b n) -> p b n", n=L), BIr[64:P, 0, :].rearrange("p (b n) -> p b n", n=L)[:, :, ::-1])\
                .then_inc(S["bi_flip"], 1)
            v.tensor_copy(BI[:, 2, :].rearrange("p (b n) -> p b n", n=L), BIr[:, 1, :].rearrange("p (b n) -> p b n", n=L)[:, :, ::-1])\
                .then_inc(S["bi_flip"], 1)
            dve.wait_ge(S["padded"], 3)
            for t in range(TT):
                dve.wait_ge(S["f2_out"], t + 1)
                st.add(v.tensor_tensor(SS[0:rows(t), t, :], G2[0:rows(t), t, :], X[0:rows(t), t, :], ALU.add))
            st.wait()
            for t in range(TT):
                st.add(v.bn_stats(stats[:, t, :], SS[:, t, :]))
            st.wait()
            for t in range(TT):
                v.bn_aggr(mv[:, t, :], stats[:, t, :]).then_inc(S["ln2_var"], 1)
            dve.wait_ge(S["ln2_var"], TT)
            dve.wait_ge(S["ln2_std"], 1)
            st.add(v.reciprocal(rstd[:, :], std[:, 0:TT]))
            st.wait()
            for t in range(TT):
                st.add(v.tensor_scalar(SS[:, t, :], SS[:, t, :], mv[:, t, 0:1], rstd[:, t:t + 1], ALU.subtract, ALU.mult))
            st.wait()
            dve.wait_ge(S["ld_ln2"], 32)
            st.add(v.tensor_tensor(SS, SS, ln2w[:, :].unsqueeze(1).to_broadcast([P, TT, D]), ALU.mult))
            st.wait()
            st.add(v.tensor_tensor(SS, SS, ln2b[:, :].unsqueeze(1).to_broadcast([P, TT, D]), ALU.add))
            st.wait()
            st.add(v.tensor_tensor(H[:, 0:TT - 1, :], H[:, 0:TT - 1, :], SS[:, 0:TT - 1, :], ALU.add))
            st.add(v.tensor_tensor(H[0:LAST, TT - 1, :], H[0:LAST, TT - 1, :], SS[0:LAST, TT - 1, :], ALU.add))
            st.wait()

            ln(1)
            dve.wait_ge(ln_out[1], 6)
            dve.wait_ge(S["ld_q1t"], 32)
            blocks = ((0, DA, XTa), (1, DB, XTb))
            st.add(v.memset(qs[64:P, 9:10], 1.0))
            for c, n, xt in blocks:
                st.add(v.tensor_reduce(qs[0:n, c:c + 1], xt[0:n, 0:T], AX.X, ALU.max))
                st.add(v.tensor_reduce(qs[0:n, 2 + c:3 + c], xt[0:n, 0:T], AX.X, ALU.min))
                st.add(v.tensor_reduce(qs[0:n, 8 + c:9 + c], qw1t[0:n, c, :], AX.X, ALU.max, apply_absolute_value=True))
            st.wait()
            v.scalar_tensor_tensor(out=qs[:, 4:6], in0=qs[:, 2:4], scalar=-1.0, in1=qs[:, 0:2], op0=ALU.mult, op1=ALU.max).then_inc(S["q_gmax"], 1)
            dve.wait_ge(S["q_sqrt"], 2)
            st.add(v.reciprocal(qs[:, 12:14], qs[:, 10:12]))
            st.wait()
            st.add(v.tensor_tensor(qs[:, 4:6], qs[:, 6:8], qs[:, 12:14], ALU.mult))
            st.wait()
            st.add(v.memset(qs[64:P, 5:6], 1.0))
            st.wait()
            st.add(v.tensor_scalar(qs[:, 6:8].bitcast(U32), qs[:, 4:6].bitcast(U32), 0x7F800000, None, ALU.bitwise_and))
            st.wait()
            st.add(v.scalar_tensor_tensor(out=qs[:, 8:10], in0=qs[:, 6:8], scalar=1.5, in1=qs[:, 4:6], op0=ALU.mult, op1=ALU.is_lt))
            st.wait()
            st.add(v.scalar_tensor_tensor(out=qs[:, 18:20], in0=qs[:, 8:10], scalar=1.0, in1=qs[:, 6:8], op0=ALU.add, op1=ALU.mult))
            st.wait()
            v.tensor_scalar(csdiag[:, 0:DA], ident, qs[:, 18:19], None, ALU.mult).then_inc(S["q_diag"], 1)
            v.tensor_scalar(csdiag[0:DB, DA:D], identw[0:DB, 0:DB], qs[0:DB, 19:20], None, ALU.mult).then_inc(S["q_diag"], 1)
            st.add(v.reciprocal(qs[:, 20:22], qs[:, 18:20]))
            st.wait()
            st.add(v.tensor_tensor(qs[:, 0:2], qs[:, 0:2], qs[:, 20:22], ALU.mult))
            st.add(v.scalar_tensor_tensor(out=qs[:, 2:4], in0=qs[:, 2:4], scalar=-1.0, in1=qs[:, 20:22], op0=ALU.mult, op1=ALU.mult))
            st.wait()
            v.tensor_reduce(qs[:, 14:15], qs[:, 0:2], AX.X, ALU.max).then_inc(S["q_range"], 1)
            v.tensor_reduce(qs[:, 15:16], qs[:, 2:4], AX.X, ALU.max).then_inc(S["q_range"], 1)

            def asym(src, scale, inv, lo, hi):
                st.add(v.tensor_scalar(qs[:, src:src + 2], qs[:, src:src + 2], 0.0, None, ALU.max))
                st.wait()
                st.add(v.tensor_tensor(qs[:, scale:scale + 1], qs[:, src:src + 1], qs[:, src + 1:src + 2], ALU.add))
                st.wait()
                st.add(v.tensor_scalar(qs[:, scale:scale + 1], qs[:, scale:scale + 1], 1.0 / 255, QEPS, ALU.mult, ALU.max))
                st.wait()
                st.add(v.reciprocal(qs[:, inv:inv + 1], qs[:, scale:scale + 1]))
                st.wait()
                st.add(v.tensor_tensor(qs[:, lo:lo + 1], qs[:, src + 1:src + 2], qs[:, inv:inv + 1], ALU.mult))
                st.wait()
                st.add(v.tensor_scalar(qs[:, lo:lo + 1], qs[:, lo:lo + 1], ROUNDER, -ROUNDER, ALU.add, ALU.add))
                st.wait()
                st.add(v.tensor_scalar(qs[:, lo:lo + 1], qs[:, lo:lo + 1], -1.0, ROUNDER, ALU.mult, ALU.add))
                st.wait()
                st.add(v.tensor_scalar(qs[:, hi:hi + 1], qs[:, lo:lo + 1], 255.0, None, ALU.add))
                st.wait()

            dve.wait_ge(S["q_range_all"], 1)
            asym(16, 22, 23, 26, 27)
            v.tensor_tensor(qs[:, 24:26], qs[:, 20:22], qs[:, 23:24].to_broadcast([P, 2]), ALU.mult).then_inc(S["q_fac"], 1)
            dve.wait_ge(S["ld_q2"], 32)
            for c, n, _x in blocks:
                st.add(v.tensor_reduce(qs[0:n, 36 + c:37 + c], qw2[0:n, c, :], AX.X, ALU.max, apply_absolute_value=True))
            st.wait()
            st.add(v.tensor_scalar(qs[:, 36:38], qs[:, 36:38], 1.0 / 127, QEPS, ALU.mult, ALU.max))
            st.wait()
            st.add(v.reciprocal(qs[:, 38:40], qs[:, 36:38]))
            st.wait()
            for c, n, _x in blocks:
                st.add(v.tensor_scalar(qw2[0:n, c, :], qw2[0:n, c, :], qs[0:n, 38 + c:39 + c], 127.0, ALU.mult, ALU.min))
            st.wait()
            for c, n, _x in blocks:
                st.add(v.tensor_scalar(qw2[0:n, c, :], qw2[0:n, c, :], -128.0, ROUNDER, ALU.max, ALU.add))
            st.wait()
            for c, n, _x in blocks:
                v.tensor_scalar(q2[0:n, c, :], qw2[0:n, c, :], -ROUNDER, None, ALU.add).then_inc(S["q2_ready"], 1)
            for c, n, _x in blocks:
                dve.wait_ge(S["q_u"], c + 1)
                v.tensor_scalar(UR[0:n, c, :], UR[0:n, c, :], qs[0:n, 26:27], qs[0:n, 27:28], ALU.max, ALU.min).then_inc(S["q_uc"], 1)
            dve.wait_ge(S["q_csb"], 1)
            st.add(v.tensor_copy(csb[:, :], bank[4][:, 0:D]))
            st.wait()
            dve.wait_ge(S["ld_q1"], 16)
            st.add(v.tensor_tensor(qw1, qw1, csb[:, :].unsqueeze(1).to_broadcast([P, KH, D]), ALU.mult))
            st.wait()
            st.add(v.tensor_reduce(qs[:, 50:56], qw1, AX.X, ALU.max, apply_absolute_value=True))
            st.wait()
            st.add(v.tensor_scalar(qs[:, 50:56], qs[:, 50:56], 1.0 / 127, QEPS, ALU.mult, ALU.max))
            st.wait()
            st.add(v.reciprocal(qs[:, 56:62], qs[:, 50:56]))
            st.wait()
            for k in range(KH):
                st.add(v.tensor_scalar(qw1[:, k, :], qw1[:, k, :], qs[:, 56 + k:57 + k], 127.0, ALU.mult, ALU.min))
            st.wait()
            st.add(v.tensor_scalar(qw1, qw1, -128.0, ROUNDER, ALU.max, ALU.add))
            st.add(v.tensor_scalar(qs[:, 50:56], qs[:, 50:56], qs[:, 22:23], None, ALU.mult))
            st.wait()
            v.tensor_scalar(q1, qw1, -ROUNDER, None, ALU.add).then_inc(S["q1_ready"], 1)
            for k in range(KH):
                dve.wait_ge(S["q2_turned"], k + 1)
                v.tensor_copy(q2t[:, k, :], bank[6 + k % 2][:, 0:D]).then_inc(S["q2_out"], 1)
            for k in range(KH):
                dve.wait_ge(S["q1_turned"], k + 1)
                st.add(v.tensor_copy(q1t[:, 0, k * P:(k + 1) * P], bank[6 + k % 2][:, 0:P]))
                v.tensor_copy(q1t[0:DB, 1, k * P:(k + 1) * P], bank[6 + k % 2][0:DB, P:2 * P]).then_inc(S["q1_out"], 1)
            for n in range(3 * KH):
                c, m = divmod(n, KH)
                dve.wait_ge(S["hg_ready"], n + 1)
                st.add(v.tensor_reduce(ham[:, n:n + 1], HG[:, m, c * CH:(c + 1) * CH], AX.X, ALU.max, apply_absolute_value=True))
            st.wait()
            v.tensor_reduce(qs[:, 30:31], ham[:, :], AX.X, ALU.max).then_inc(S["ham_ready"], 1)
            dve.wait_ge(S["ham_all"], 1)
            st.add(v.tensor_scalar(qs[:, 32:33], qs[:, 31:32], 1.0 / 127, QEPS, ALU.mult, ALU.max))
            st.wait()
            st.add(v.tensor_tensor(qs[:, 34:36], qs[:, 36:38], qs[:, 32:33].to_broadcast([P, 2]), ALU.mult))
            v.reciprocal(qs[:, 33:34], qs[:, 32:33]).then_inc(S["hs_ready"], 1)
            for m in range(KH):
                dve.wait_ge(S["hr_ready"], m + 1)
                v.tensor_scalar(HG[:, m, :], HG[:, m, :], ROUNDER - 128.0, ROUNDER + 127.0, ALU.max, ALU.min).then_inc(S["hc_ready"], 1)
            dve.wait_ge(S["ot_ready"], 6)
            for c, n, _x in blocks:
                st.add(v.tensor_reduce(qs[0:n, c:c + 1], OT[0:n, c, :], AX.X, ALU.max))
                st.add(v.tensor_reduce(qs[0:n, 2 + c:3 + c], OT[0:n, c, :], AX.X, ALU.min))
            st.add(v.memset(qs[64:P, 1:2], 0.0))
            st.add(v.memset(qs[64:P, 3:4], 0.0))
            st.wait()
            st.add(v.tensor_reduce(qs[:, 40:41], qs[:, 0:2], AX.X, ALU.max))
            st.add(v.tensor_reduce(qs[:, 41:42], qs[:, 2:4], AX.X, ALU.min))
            st.wait()
            v.tensor_scalar(qs[:, 41:42], qs[:, 41:42], -1.0, None, ALU.mult).then_inc(S["or_ready"], 1)
            dve.wait_ge(S["or_all"], 1)
            asym(42, 45, 46, 48, 49)
            st.add(v.tensor_scalar(qs[:, 47:48], qs[:, 45:46], 1.0, None, ALU.mult).then_inc(S["of_ready"], 1)) if False else \
                v.tensor_scalar(qs[:, 47:48], qs[:, 45:46], 1.0, None, ALU.mult).then_inc(S["of_ready"], 1)
            for c, n, _x in blocks:
                dve.wait_ge(S["om_ready"], c + 1)
                st.add(v.tensor_scalar(OT[0:n, c, :], OT[0:n, c, :], qs[0:n, 48:49], qs[0:n, 49:50], ALU.max, ALU.min))
                st.wait()
                v.tensor_scalar(OT[0:n, c, :], OT[0:n, c, :], -ROUNDER, qs[0:n, 45:46], ALU.add, ALU.mult).then_inc(S["oq_ready"], 1)
            for t in range(TT):
                dve.wait_ge(S["oq_turned"], t + 1)
                v.tensor_tensor(H[0:rows(t), t, :], H[0:rows(t), t, :], bank[4 + t % 4][0:rows(t), 0:D], ALU.add).then_inc(S["h_ffn"], 1)
            dve.wait_ge(S["h_ffn"], TT)

            ln(2)
            for b in range(NB + 1):
                p = b % 2
                if b < NB:
                    for g, (r, q) in enumerate(GROUPS):
                        dve.wait_ge(S["s_mm"], 6 * b + g + 1)
                        sc = bank[2 + g % 2][0:r, 0:q * L].rearrange("p (a b) -> p a b", b=L)
                        k = 18 * p + 3 * g
                        st.add(v.tensor_reduce(amx[0:r, k:k + q], sc, AX.X, ALU.max))
                        st.wait()
                        if b >= 2:
                            dve.wait_ge(S["p_turned"], 4 * (b - 1))
                        v.tensor_tensor(PRS[0:r, 6 * p + g, 0:q * L].rearrange("p (a b) -> p a b", b=L), sc,
                                        amx[0:r, k:k + q].unsqueeze(2).to_broadcast([r, q, L]), ALU.subtract).then_inc(S["s_sub"], 1)
                if b:
                    for g in range(4):
                        dve.wait_ge(S["p_turned"], 4 * (b - 1) + g + 1)
                        if b >= 2:
                            dve.wait_ge(S["av_mm"], 2 * (b - 1))
                        v.tensor_copy(PTr[:, 3 * g:3 * g + 3, :], bank[5][0:R, 0:3 * L].rearrange("p (a b) -> p a b", b=L)).then_inc(S["pt_dve"], 1)
                if b < NB:
                    for g, (r, q) in enumerate(GROUPS):
                        k = 18 * p + 3 * g
                        dve.wait_ge(S["s_exp"], 6 * b + g + 1)
                        st.add(v.tensor_reduce(asm[0:r, k:k + q], PRS[0:r, 6 * p + g, 0:q * L].rearrange("p (a b) -> p a b", b=L), AX.X, ALU.add))
                    st.wait()
                    if b >= 2:
                        dve.wait_ge(S["p_norm"], 6 * (b - 1))
                    for g, (r, q) in enumerate(GROUPS):
                        k = 18 * p + 3 * g
                        v.reciprocal(arc[0:r, k:k + q], asm[0:r, k:k + q]).then_inc(S["s_sum"], 1)
            for t in range(TT):
                dve.wait_ge(S["wo_mm"], t + 1)
                v.tensor_tensor(H[0:rows(t), t, :], H[0:rows(t), t, :], bank[t % 4][0:rows(t), 0:D], ALU.add).then_inc(S["h_att"], 1)
            dve.wait_ge(S["h_att"], TT)

            ln(3)
            dve.wait_ge(S["g_mm"], 1)
            st.add(v.tensor_copy(gv[:, :], bank[4][:, 0:TT * NE]))
            st.wait()
            v.scalar_tensor_tensor(out=gn[:, :], in0=gv[:, :], scalar=-1.0, in1=gv[:, :], op0=ALU.mult, op1=ALU.min).then_inc(S["g_abs"], 1)
            dve.wait_ge(S["g_exp"], 1)
            log1p_series(ge[:, :], gt[:, :], gq[:, :], gp[:, :], gs[:, :])
            v.scalar_tensor_tensor(out=gs[:, :], in0=gv[:, :], scalar=0.0, in1=gp[:, :], op0=ALU.max, op1=ALU.add).then_inc(S["g_sp"], 1)
            dve.wait_ge(S["g_sqrt"], 1)
            dve.wait_ge(S["ld_gate"], 48)
            gs3 = gs[:, :].rearrange("p (t e) -> p t e", e=NE)
            st.add(v.tensor_tensor(gr[:, :, :], gs3, gateb[:, :].unsqueeze(1).to_broadcast([P, TT, NE]), ALU.add))
            st.wait()
            for t in range(TT):
                st.add(v.max(top[:, t, :], gr[:, t, :]))
            st.wait()
            for t in range(TT):
                st.add(v.max_index(topi[:, t, :], top[:, t, :], gr[:, t, :]))
            st.wait()
            st.add(v.tensor_copy(topf[:, :, :], topi[:, :, :]))
            st.wait()
            it3 = iota8[:, :].unsqueeze(1).to_broadcast([P, TT, NE])
            st.add(v.tensor_tensor(comb[:, :, :], it3, topf[:, :, 0:1].to_broadcast([P, TT, NE]), ALU.is_equal))
            st.add(v.tensor_tensor(gr[:, :, :], it3, topf[:, :, 1:2].to_broadcast([P, TT, NE]), ALU.is_equal))
            st.wait()
            st.add(v.tensor_tensor(comb[:, :, :], comb[:, :, :], gr[:, :, :], ALU.add))
            st.wait()
            st.add(v.tensor_tensor(comb[:, :, :], comb[:, :, :], gs3, ALU.mult))
            st.wait()
            st.add(v.tensor_reduce(csum[:, :], comb[:, :, :], AX.X, ALU.add))
            st.wait()
            st.add(v.tensor_scalar(csum[:, :], csum[:, :], 1e-6, None, ALU.max))
            st.wait()
            st.add(v.reciprocal(csum[:, :], csum[:, :]))
            st.wait()
            st.add(v.tensor_tensor(comb[:, :, :], comb[:, :, :], csum[:, :].unsqueeze(2).to_broadcast([P, TT, NE]), ALU.mult))
            st.wait()

            def acc(e, c):
                for j in range(3):
                    t = 3 * c + j
                    n = e * TT + t
                    dve.wait_ge(S["e_mm"], n + 1)
                    w = comb[:, t, e:e + 1] if e < NE else cst[:, 2:3]
                    if e:
                        dve.wait_ge(S["e_acc"], n - TT + 1)
                    v.scalar_tensor_tensor(out=H[:, t, :], in0=bank[4 + n % 4][:, 0:D], scalar=w, in1=H[:, t, :],
                                           op0=ALU.mult, op1=ALU.add).then_inc(S["e_acc"], 1)

            for g in range(3 * EW + 1):
                if g < 3 * EW:
                    for m in range(KH):
                        n = g * KH + m
                        dve.wait_ge(S["gu_mm"], 2 * n + 1)
                        if n >= 3:
                            dve.wait_ge(S["g_silu"], n - 2)
                        v.tensor_scalar(GM[:, n % 3, :], bank[2 * (n % 2)][:, 0:CM], 10.0, None, ALU.min).then_inc(S["g_min"], 1)
                        dve.wait_ge(S["gu_mm"], 2 * n + 2)
                        if n >= 3:
                            dve.wait_ge(S["hh_ready"], n - 2)
                        v.tensor_scalar(UM[:, n % 3, :], bank[2 * (n % 2) + 1][:, 0:CM], 10.0, -10.0, ALU.min, ALU.max).then_inc(S["u_clip"], 1)
                if g:
                    acc((g - 1) // 3, (g - 1) % 3)


def kernel(**inputs):
    import numpy as np
    import concourse.bacc as bacc
    from concourse.bass_utils import run_bass_kernel_spmd

    a = {k: np.asarray(x) for k, x in inputs.items()}
    f = np.float32

    def both(name):
        return np.stack([a[f"L0_attn_f_{name}"], a[f"L0_attn_b_{name}"]])

    def packed(w):
        gap = np.zeros((D, 16), f)
        return np.concatenate([w[:, 0:784], gap, w[:, 784:800], w[:, 800:806]], 1)

    def taps(w):
        z = np.zeros((16,) + w.shape[1:], f)
        z2 = np.zeros((80,) + w.shape[1:], f)
        return np.concatenate([w[0:400], z, w[400:416], z2]).reshape((4, P) + w.shape[1:])

    dt_bias, a_log = both("dt_bias"), both("A_log")
    heads = lambda x: np.tile(np.repeat(x[:, None, :], NB, 1).reshape(1, -1), (1, 2))
    arrays = {
        "patches": a["x"].reshape(NB, 3, 8, 16, 8, 16).transpose(3, 5, 1, 0, 2, 4).reshape(IN, NB * NI),
        "tok": np.pad(a["x_txt"], ((0, 0), (76, 0)), constant_values=-1),
        "tok_w": a["L0_tok_W"].T, "tok_b": a["L0_tok_b"][None], "emb": a["L0_txt_emb"],
        "ln1": np.stack([a["L0_attn_ln1_w"], a["L0_attn_ln1_b"]], 1),
        "ln2_w": a["L0_attn_ln2_w"][None], "ln2_b": a["L0_attn_ln2_b"][None],
        "in_w": np.stack([packed(a["L0_attn_f_in_w"]), packed(a["L0_attn_b_in_w"])]),
        "dt_bias": heads(dt_bias), "a_log": heads(a_log),
        "conv_w": np.stack([taps(a["L0_attn_f_conv_w"]), taps(a["L0_attn_b_conv_w"])]).transpose(2, 0, 1, 3),
        "conv_b": np.stack([taps(a["L0_attn_f_conv_b"]), taps(a["L0_attn_b_conv_b"])]).transpose(2, 0, 1),
        "skip_d": np.repeat(both("D"), 64, axis=1).reshape(2, KD, P).transpose(2, 0, 1),
        "norm_w": both("norm_w").reshape(2 * KD, P).T, "out_w": both("out_w"),
        "ffn_w1": a["L0_attn_ffn_w1"], "ffn_b1": a["L0_attn_ffn_b1"].reshape(KH, P).T,
        "ffn_w2": a["L0_attn_ffn_w2"], "ffn_b2": a["L0_attn_ffn_b2"][None],
        "q_w1": a["L0_ffn_w1"], "q_w1t": a["L0_ffn_w1"].T, "q_w2": a["L0_ffn_w2"],
        "q_b1": a["L0_ffn_b1"].reshape(KH, P).T, "q_b2": a["L0_ffn_b2"][:, None],
        "w_q": a["L1_attn_w_q"], "w_k": a["L1_attn_w_k"], "w_v": a["L1_attn_w_v"],
        "w_o": a["L1_attn_w_o"], "b_o": a["L1_attn_b_o"][None],
        "gate_w": a["L1_ffn_gate_w"], "gate_b": a["L1_ffn_gate_bias"][None],
        "e_w1": np.concatenate([a["L1_ffn_w1"], a["L1_ffn_w1s"][None]]),
        "e_w3": np.concatenate([a["L1_ffn_w3"], a["L1_ffn_w3s"][None]]),
        "e_w2": np.concatenate([a["L1_ffn_w2"], a["L1_ffn_w2s"][None]]),
    }
    nc = bacc.Bacc("TRN2", target_bir_lowering=False, num_devices=1)
    feed, aps = {}, {}
    for name, x in arrays.items():
        x = np.ascontiguousarray(x)
        feed[f"in_{name}"] = x
        aps[name] = nc.dram_tensor(f"in_{name}", x.shape, mybir.dt.from_np(x.dtype), kind="ExternalInput").ap()
    out = nc.dram_tensor("out_0", (NB, L, D), F32, kind="ExternalOutput").ap()
    build(nc, aps, out)
    r = run_bass_kernel_spmd(nc, [feed], core_ids=[0])
    return r.results[0]["out_0"]
```

```python
from contextlib import ExitStack

import concourse.bass as bass
from concourse import mybir

F32 = mybir.dt.float32
F32R = mybir.dt.float32r
BF16 = mybir.dt.bfloat16
I32 = mybir.dt.int32
U32 = mybir.dt.uint32
ALU = mybir.AluOpType
ACT = mybir.ActivationFunctionType
AX = mybir.AxisListType
RMAX = bass.bass_isa.ReduceOp.max

P = 128
NB = 8
NI, NX = 64, 77
L = NI + NX
T = NB * L
TT = -(-T // P)
TP = TT * P
LAST = T - (TT - 1) * P
R = L - P
D = 192
DA, DB = 128, 64
IN = 768
KI = IN // P
DIN = 384
KD = DIN // P
NH = 6
NS = 16
NCONV = 4
PADL = L + NCONV - 1
CC = 0
CX = DIN
CB = 2 * DIN
CDT = 2 * DIN + 48
WCOLS = CDT + NH
HID = 768
KH = HID // P
ROUNDER = 1.5 * 2.0 ** 23
QEPS = 1e-8
AH = 12
NE = 8
CH = 376
CM = 384


def rows(t):
    return P if t < TT - 1 else LAST


class Steps:

    def __init__(self, eng, sem):
        self.eng, self.sem, self.n = eng, sem, 0

    def add(self, ins):
        ins.then_inc(self.sem, 1)
        self.n += 1
        return self.n

    def wait(self):
        self.eng.wait_ge(self.sem, self.n)


def build(nc, i, out):
    ctx = ExitStack()
    with ctx:
        def sb(name, shape, dt=F32):
            return ctx.enter_context(nc.sbuf_tensor(name, shape, dt))

        def sem(name):
            return ctx.enter_context(nc.semaphore(name))

        bank = [ctx.enter_context(nc.psum_tensor(f"bank{k}", [P, 512], F32)) for k in range(8)]
        h0 = nc.dram_tensor("h0_scratch", (NB, L, D), F32, kind="Internal").ap()

        identw = sb("identw", [P, L])
        ident = identw[:, 0:P]
        identb = sb("identb", [P, P], BF16)
        ident3 = sb("ident3", [P, 3 * L])
        identr = sb("identr", [R, NH * R])
        ones = sb("ones", [P, P])
        cst = sb("cst", [P, 4])
        qcol = sb("qcol", [P, 1])
        iota8 = sb("iota8", [P, NE])

        H = sb("H", [P, TT, D])
        X = sb("X", [P, TT, D])
        XTa = sb("XTa", [P, TP])
        XTb = sb("XTb", [P, TP])
        stats = sb("stats", [P, TT, 6])
        mv = sb("mv", [P, TT, 2])
        std = sb("std", [P, 2 * TT])
        rstd = sb("rstd", [P, TT])
        rstd2 = sb("rstd2", [P, TT])
        prod = sb("prod", [P, TT])

        big1 = sb("big1", [P, KH * TP])
        big2 = sb("big2", [P, KH * TP])
        big2_end = nc.sbuf_base
        big3 = sb("big3", [P, KH * TP])
        wreg = sb("wreg", [P, 8448])
        areg = sb("areg", [P, 5150])
        creg = sb("creg", [P, 5120])
        creg_end = nc.sbuf_base

        def reduced(name, at, width, end, size):
            return nc.alloc_sbuf_tensor_at(name, [P, width], F32R, offset=end - 4 * (size - at))

        def area(reg, at, shape):
            n = 1
            for s in shape[1:]:
                n *= s
            v = reg[0:shape[0], at:at + n]
            if len(shape) == 3:
                v = v.rearrange("p (a b) -> p a b", b=shape[2])
            if len(shape) == 4:
                v = v.rearrange("p (a b c) -> p a b c", b=shape[2], c=shape[3])
            return v

        patches = area(big1, 0, [P, KI, NB * NI])
        tokw = area(big1, KI * NB * NI, [P, KI, D])
        tokb = area(big1, KI * NB * NI + KI * D, [P, D])
        img = area(big2, 0, [P, NB // 2, D])
        cur = area(big2, 1024, [76, NB, NX]).bitcast(I32)
        shf = area(big2, 1664, [76, NB, NX]).bitcast(I32)
        eq = area(big2, 2304, [76, NB * NX])
        run = area(big2, 2944, [76, NB * NX])
        score = area(big2, 3584, [76, NB * NX])
        nxt = area(big2, 4224, [NX, NB, 76]).bitcast(I32)
        junk = area(big2, 4864, [NX, NB, 76])
        txt = area(big3, 0, [NX, NB, D])
        best = sb("best", [NX, NB])
        found = sb("found", [NX, NB])
        pick = sb("pick", [NX, NB])
        ids = sb("ids", [NX, NB], I32)

        XS = area(big3, 0, [P, TT, D])
        XRa = area(areg, 0, [P, TP])
        XRb = area(areg, TP, [DB, TP])
        ln1 = sb("ln1", [P, 2, 2])
        inw = area(wreg, 0, [P, 2 * 2, WCOLS])
        outw = area(wreg, 4 * WCOLS, [P, 2 * KD, D])
        ffw1 = area(wreg, 4 * WCOLS + 2 * KD * D, [P, KD, HID])
        ffw2 = area(areg, 2 * TP, [P, KH, D])
        ffb1 = sb("ffb1", [P, KH])
        ffb2 = sb("ffb2", [1, D])
        normw = sb("normw", [P, 2 * KD])
        convw = sb("convw", [P, 2, 4, NCONV])
        convb = sb("convb", [P, 2, 4])
        skipd = sb("skipd", [P, 2, KD])
        ZS = area(big1, 0, [P, 2 * KD, T])
        CV = area(big2, 0, [P, 2 * KD, T])
        XP = area(big3, 0, [P, 2 * KD, NB * PADL])
        bcp = area(creg, 0, [48, 2, NB * PADL])
        bcv = area(creg, 2 * NB * PADL, [48, 2, T])
        dtrow = sb("dtrow", [P, 2 * 96])
        alog = sb("alog", [P, 2 * 96])
        dtv = sb("dtv", [P, 192])
        dte = sb("dte", [P, 192])
        dtt = sb("dtt", [P, 192])
        dtq = sb("dtq", [P, 192])
        dtp = sb("dtp", [P, 192])
        dts = sb("dts", [P, 192])
        dA = sb("dA", [P, 192])
        dAT = sb("dAT", [P, L])
        xcs = sb("xcs", [P, 2, KD, L])
        Bs = sb("Bs", [NS, 2, L])
        Cs = sb("Cs", [NS, 2, L])
        dtx = sb("dtx", [P, 2, DIN])
        dtxr = sb("dtxr", [R, 2, DIN])
        DD = area(areg, 3456, [P, NH, L])
        MM = area(wreg, 6744, [P, 2, NH, L])
        dAr = sb("dAr", [R, NH, R])
        DDr = sb("DDr", [R, NH, R])
        MMr = sb("MMr", [R, 2, NH, R])
        w1y = area(areg, 3456 + NH * L, [P, 2, KD, L])
        SQ = area(big3, 0, [P, 2 * KD, T])
        rs = sb("rs", [P, 2 * TT])
        rss = sb("rss", [P, 2 * TT])
        BT = area(big1, 0, [P, TT, 2 * D])
        BI = area(big1, TT * 2 * D, [P, KD, T])
        BIr = area(big2, 0, [P, 2, T])
        H1 = area(big3, 0, [P, KH, T])
        G2 = area(big2, 2 * T, [P, TT, D])
        SS = area(big2, 2 * T + TT * D, [P, TT, D])
        ln2w = sb("ln2w", [P, D])
        ln2b = sb("ln2b", [P, D])

        qw1t = area(areg, 0, [P, 2, HID])
        qw1 = area(creg, 0, [P, KH, D])
        qw2 = area(creg, KH * D, [P, 2, HID])
        qb1 = sb("qb1", [P, KH])
        qb2 = sb("qb2", [P, 2])
        q1 = area(areg, 2 * HID, [P, KH * D // 2]).bitcast(BF16).rearrange("p (a b) -> p a b", b=D)
        q2 = area(areg, 2 * HID + 576, [P, HID]).bitcast(BF16).rearrange("p (a b) -> p a b", b=HID)
        q1t = area(areg, 2 * HID + 576 + HID, [P, HID]).bitcast(BF16).rearrange("p (a b) -> p a b", b=HID)
        q2t = area(areg, 2 * HID + 576 + 2 * HID, [P, KH * D // 2]).bitcast(BF16).rearrange("p (a b) -> p a b", b=D)
        csdiag = area(creg, 3000, [P, D])
        csb = sb("csb", [P, D])
        qs = sb("qs", [P, 64])
        UR = area(big2, 0, [P, 2, T])
        UQ = area(big2, 2 * T, [P, T]).bitcast(BF16).rearrange("p (a b) -> p a b", b=T)
        HG = area(big3, 0, [P, KH, T])
        HQ = area(big1, 0, [P, KH * T // 2]).bitcast(BF16).rearrange("p (a b) -> p a b", b=T)
        OT = area(big2, 3 * T, [P, 2, T])
        ham = sb("ham", [P, 3 * KH])

        EWC = 4 * HID + KH * D
        awq = area(wreg, 0, [P, HID])
        awk = area(wreg, HID, [P, HID])
        awv = area(wreg, 2 * HID, [P, HID])
        awqk2 = area(wreg, 3 * HID, [P, HID])
        awv2 = area(wreg, 4 * HID, [P, CM])
        awo = area(wreg, 4 * HID + CM, [P, KH, D])
        abo = sb("abo", [1, D])
        QK = area(big2, 0, [P, 2, 12 * L])
        Va = area(big2, 2 * 12 * L, [P, 2, HID])
        Vb = area(creg, 12 * L, [R, 2, HID])
        XL = area(big2, 24 * L + 2 * HID, [P, 2, NB * R])
        VL = area(big2, 24 * L + 2 * HID + 2 * NB * R, [NB * R, HID])
        PRS = area(big3, 0, [P, 2 * 6, 3 * L])
        PT = area(big3, 36 * L, [P, AH, L])
        PTr = area(creg, 0, [R, AH, L])
        OA = area(big1, 0, [P, KH, T])
        GROUPS = [(P, 3)] * 4 + [(96, 2)] * 2
        SBANK = (2, 3, 6, 7, 2, 3)
        amx = sb("amx", [P, 36])
        asm = sb("asm", [P, 36])
        arc = sb("arc", [P, 36])

        SLOTS = 256
        NTILE = (2 * T + NE * (SLOTS - 1)) // SLOTS
        BLK = 4 * P
        W2 = KH * BLK
        GCH = SLOTS // P
        SHARED = [min(GCH, TT - GCH * c) for c in range(-(-TT // GCH))]
        FIRST = 3
        ITEMS = [("shared", c) for c in range(FIRST)] + [("routed", j) for j in range(NTILE)] \
            + [("shared", c) for c in range(FIRST, len(SHARED))]
        WS = area(areg, 0, [P, EWC])
        WR = [area(wreg, 0, [P, EWC]), area(wreg, EWC, [P, EWC]), area(big3, 0, [P, EWC])]
        XG = area(big3, EWC, [P, 2, GCH * D])
        YS = area(big3, EWC + 2 * GCH * D, [P, 2, GCH * D])
        N2 = KH * TP
        XH = [reduced(f"x_lead{k}", KH * SLOTS * 2 + k * SLOTS, SLOTS, big2_end, N2) for k in range(2)]
        XR = [reduced(f"x_rest{k}", KH * SLOTS * 2 + (2 + k) * SLOTS, SLOTS, big2_end, N2) for k in range(2)]
        XB = [reduced(f"x_both{k}", KH * SLOTS * 2 + (4 + k) * SLOTS, SLOTS, big2_end, N2) for k in range(2)]
        WAT = [(KH * SLOTS * 2 + 6 * SLOTS + k * 2 * BLK, big2_end, N2) for k in range(2)] \
            + [(1024 + k * 2 * BLK, creg_end, 5120) for k in range(2)]
        WH = [reduced(f"w_lead{k}", at, BLK, end, size) for k, (at, end, size) in enumerate(WAT)]
        WL = [reduced(f"w_rest{k}", at + BLK, BLK, end, size) for k, (at, end, size) in enumerate(WAT)]
        x_slots = nc.dram_tensor("x_slots", (NTILE * SLOTS, D), F32, kind="Internal").ap()
        y_slots = nc.dram_tensor("y_slots", (NTILE * SLOTS, D), F32, kind="Internal").ap()
        zeros = area(creg, 3400, [P, D])
        column = area(creg, 3600, [P, P])
        before = area(creg, 3728, [P, P])
        RT = TT * NE
        M1 = area(creg, 3900, [P, TT, NE])
        M2 = area(creg, 3900 + RT, [P, TT, NE])
        MB = area(creg, 3900 + 2 * RT, [P, TT, NE])
        tot = area(creg, 3900 + 3 * RT, [P, NE, TT])
        seg = area(creg, 3900 + 4 * RT, [P, NE, TT])
        inc = area(creg, 3900 + 5 * RT, [P, NE, TT])
        slot = area(creg, 3900 + 6 * RT, [P, NE, TT])
        pk = area(creg, 3900 + 7 * RT, [P, TT, NE])
        tiles = area(creg, 3900 + 8 * RT, [P, NE])
        upto = area(creg, 3900 + 8 * RT + NE, [P, NE])
        valid = area(creg, 3900 + 8 * RT + 2 * NE, [P, 1])
        slotf = area(creg, 3900 + 8 * RT + 3 * NE, [P, 2 * TT])
        past = area(creg, 3900 + 9 * RT, [P, NTILE, NE])
        expf = area(creg, 3900 + 9 * RT + NTILE * NE, [P, NTILE])
        slots = sb("slots", [P, 2 * TT], I32)
        expert = sb("expert", [P, NTILE], I32)
        wt = sb("wt", [P, 2 * TT])
        gatew = sb("gatew", [P, 2, NE])
        gateb = sb("gateb", [P, NE])
        gv = area(creg, 0 * TT * NE, [P, TT * NE])
        gn = area(creg, 1 * TT * NE, [P, TT * NE])
        ge = area(creg, 2 * TT * NE, [P, TT * NE])
        gt = area(creg, 3 * TT * NE, [P, TT * NE])
        gq = area(creg, 4 * TT * NE, [P, TT * NE])
        gp = area(creg, 5 * TT * NE, [P, TT * NE])
        gs = area(creg, 6 * TT * NE, [P, TT * NE])
        gr = area(creg, 7 * TT * NE, [P, TT, NE])
        top = area(creg, 8 * TT * NE, [P, TT, NE])
        topi = area(creg, 10 * TT * NE, [P, TT, NE]).bitcast(U32)
        topf = area(creg, 9 * TT * NE, [P, TT, NE])
        comb = sb("comb", [P, TT, NE])
        csum = sb("csum", [P, TT])
        GM = area(big1, 0, [P, 3, SLOTS])
        GS = area(big1, 3 * SLOTS, [P, 3, SLOTS])
        UM = area(big1, 6 * SLOTS, [P, 3, SLOTS])
        YG = area(big1, 9 * SLOTS, [P, 2 * TT, D])
        HH = area(big2, 0, [P, 2, KH * SLOTS])

        names = """ld_embed ld_tok ld_inw ld_mamba ld_ffw
            const_ready iota_ready v_step img_ready img_out score_ready scoreT ids_ready gathered txt_ready
            h0_stored h_loaded inproj z_evac x_evac dt_ready dt_abs dt_exp a_exp dt_arg dA_exp dA_ready
            flipped convolved xc_ready xc_turned g_ready decay_ready dtx_ready decay_used m_ready y_ready
            yd_ready yz_ready padded sq_ready sq_added ss_ready ss_std ss_inv op_ready bt_ready bt_turned bi_act bi_dve
            bi_flip h1_ready h1_out f2_ready f2_out ln2_var ln2_std 
            ld_q1t ld_q1 ld_q2 ld_small outw_scaled
            q_gmax q_sqrt q_diag q_csb q_range q_range_all q_fac q_u q_ui q1_ready q1_turned q1_out q2_ready q2_turned q2_out
            hq_mm hg_ready ham_ready ham_all hs_ready hr_ready hi_ready ot_mm ot_ready or_ready or_all
            of_ready om_ready oq_ready oq_turned h_ffn 
            ld_att qk_mm qk_out v_mm v_out tails_ready vb_in s_mm s_sub s_exp s_sum p_norm p_turned pt_act pt_dve av_mm av_out
            wo_mm h_att g_mm g_dve g_act 
            x_cleared picked counted slots_ready scattered slots_turned x_lead x_rest w_lead w_rest
            ld_shared gu_mm g_min g_silu u_clip hh_ready e_mm y_out s_acc h_moe stored p_step""".split()
        S = {n: sem(n) for n in names}
        LN_OUT = (2, 2, 3, 2)
        LN_BASE = [3 * sum(LN_OUT[:k]) for k in range(5)]
        ln_var, ln_std, ln_x, ln_turned, ln_out = [sem(n) for n in ("ln_var", "ln_std", "ln_x", "ln_turned", "ln_out")]
        ld_down = [sem(f"ld_down{k}") for k in range(3)]
        ld_w = [sem(f"ld_w{k}") for k in range(3)]
        ld_slots = [sem(f"ld_slots{k}") for k in range(2)]
        y_back = [sem(f"y_back{k}") for k in range(3)]
        y_stored = [sem(f"y_stored{k}") for k in range(2)]
        ln0_std2 = sem("ln0_std2")
        ln0_vx = sem("ln0_vx")

        block = ctx.enter_context(nc.Block())
        ITS = [(d, b) for d in range(2) for b in range(NB)]
        DTC = lambda d, b: (d * NB + b) * NH

        def k_inproj(d, c, m):
            return (d * 4 + c) * 7 + m

        INBANK = (0, 1, 2, 3, 5, 6, 7)

        def inproj_free(k):
            dc, m = divmod(k, 7)
            return (S["z_evac"], dc * 3 + m + 1) if m < 3 else (S["x_evac"], dc * 4 + m - 3 + 1)

        AFTER = FIRST + NTILE
        DOWN_AT, OUT_AT = 1, 2
        STEPS = len(ITEMS) * KH

        def on_dve(g):
            return 1 <= g < FIRST or g >= FIRST + NTILE

        def weights(g):
            kind, c = ITEMS[g]
            return WS if kind == "shared" else WR[c % 3]

        TOK = lambda kind, c: (SHARED[c] if kind == "shared" else GCH) * P

        def emptied(g):
            kind, c = ITEMS[g]
            return (S["s_acc"], c + 1) if kind == "shared" else (S["y_out"], c + 1)

        @block.sync
        def _(sp):
            def load(dst, src, s):
                sp.dma_start(dst, src).then_inc(S[s], 16)

            wide = dict(p=76, b=NB, n=NX)
            tok = i["tok"]
            W = 76 + NX

            def window(parts, at, n):
                return bass.AP(tensor=tok.tensor, offset=at, ap=[[1, parts], [W, NB], [1, n]])

            load(cur, bass.AP(tensor=tok.tensor, offset=76, ap=[[0, 76], [W, NB], [1, NX]]), "ld_tok")
            load(shf, window(76, 0, NX), "ld_tok")
            load(nxt, window(NX, 1, 76), "ld_tok")
            load(patches, i["patches"].rearrange("(k p) n -> p k n", p=P), "ld_embed")
            load(tokw, i["tok_w"].rearrange("(k p) n -> p k n", p=P), "ld_embed")
            load(tokb, i["tok_b"].partition_broadcast(P).rearrange("p a n -> p (a n)"), "ld_embed")
            load(ln1[0:DA, 0, :], i["ln1"][0:DA, :], "ld_inw")
            load(ln1[0:DB, 1, :], i["ln1"][DA:D, :], "ld_inw")
            for d in range(2):
                load(inw[:, 2 * d, :], i["in_w"][d, 0:DA, :], "ld_inw")
                load(inw[0:DB, 2 * d + 1, :], i["in_w"][d, DA:D, :], "ld_inw")
            load(dtrow[:, :], i["dt_bias"].partition_broadcast(P).rearrange("p a n -> p (a n)"), "ld_mamba")
            load(alog[:, :], i["a_log"].partition_broadcast(P).rearrange("p a n -> p (a n)"), "ld_mamba")
            load(convw[:], i["conv_w"], "ld_mamba")
            load(convb[:], i["conv_b"], "ld_mamba")
            load(skipd[:], i["skip_d"], "ld_mamba")
            load(outw, i["out_w"].rearrange("d (k p) n -> p (d k) n", p=P), "ld_mamba")
            load(normw[:, :], i["norm_w"], "ld_mamba")
            load(ffw1, i["ffn_w1"].rearrange("(k p) n -> p k n", p=P), "ld_ffw")
            load(ffb1[:, :], i["ffn_b1"], "ld_ffw")
            load(ffw2, i["ffn_w2"].rearrange("(k p) n -> p k n", p=P), "ld_ffw")
            load(ffb2[:, :], i["ffn_b2"], "ld_ffw")
            load(ln2w[:, :], i["ln2_w"].partition_broadcast(P).rearrange("p a n -> p (a n)"), "ld_mamba")
            load(ln2b[:, :], i["ln2_b"].partition_broadcast(P).rearrange("p a n -> p (a n)"), "ld_mamba")
            load(qb1[:, :], i["q_b1"], "ld_small")
            load(qb2[:, 0:1], i["q_b2"][0:DA, :], "ld_small")
            load(qb2[0:DB, 1:2], i["q_b2"][DA:D, :], "ld_small")
            load(gatew[:, 0, :], i["gate_w"][0:DA, :], "ld_small")
            load(gatew[0:DB, 1, :], i["gate_w"][DA:D, :], "ld_small")
            load(gateb[:, :], i["gate_b"].partition_broadcast(P).rearrange("p a n -> p (a n)"), "ld_small")
            sp.wait_ge(S["img_ready"], 2)
            for b in range(NB):
                sp.dma_start(h0[b, 0:NI, :], img[(b % 2) * NI:(b % 2 + 1) * NI, b // 2, :]).then_inc(S["h0_stored"], 16)
            sp.wait_ge(S["txt_ready"], 1)
            sp.dma_start(h0[:, NI:L, :].rearrange("b n d -> n b d"), txt).then_inc(S["h0_stored"], 16)
            sp.wait_ge(S["h0_stored"], 16 * (NB + 1))
            hf = h0.rearrange("b n d -> (b n) d")
            sp.wait_ge(S["padded"], 1)
            sp.dma_start(H[:, 0:TT - 1, :], hf[0:(TT - 1) * P, :].rearrange("(t p) d -> p t d", p=P)).then_inc(S["h_loaded"], 16)
            sp.dma_start(H[0:LAST, TT - 1, :], hf[(TT - 1) * P:T, :]).then_inc(S["h_loaded"], 16)
            sp.wait_ge(S["xc_ready"], 3 * 16)
            load(qw1, i["q_w1"].rearrange("(k p) n -> p k n", p=P), "ld_q1")
            load(qw2[:, 0, :], i["q_w2"][0:DA, :], "ld_q2")
            load(qw2[0:DB, 1, :], i["q_w2"][DA:D, :], "ld_q2")
            sp.wait_ge(S["inproj"], 56)
            load(qw1t[:, 0, :], i["q_w1t"][0:DA, :], "ld_q1t")
            load(qw1t[0:DB, 1, :], i["q_w1t"][DA:D, :], "ld_q1t")
            sp.wait_ge(S["f2_ready"], TT)
            for w, src in ((awq, "w_q"), (awk, "w_k"), (awv, "w_v")):
                load(w[:, :], i[src][0:DA, :], "ld_att")
            load(awqk2[0:DB, :], i["w_q"][DA:D, :], "ld_att")
            load(awqk2[DB:P, :], i["w_k"][DA:D, :], "ld_att")
            load(awv2[0:DB, :], i["w_v"][DA:D, 0:CM], "ld_att")
            load(awv2[DB:P, :], i["w_v"][DA:D, CM:HID], "ld_att")
            load(awo, i["w_o"].rearrange("(k p) n -> p k n", p=P), "ld_att")
            load(abo[:, :], i["b_o"], "ld_att")
            sp.wait_ge(S["const_ready"], 13)
            sp.dma_start(x_slots.rearrange("(k p) d -> p k d", p=P), zeros[:, :].unsqueeze(1).to_broadcast([P, NTILE * GCH, D]))\
                .then_inc(S["x_cleared"], 16)
            sp.wait_ge(S["ot_mm"], 6)
            load(WS[:, 0:W2], i["e_gate_up"][NE * P:(NE + 1) * P, :], "ld_shared")
            load(WS[:, W2:EWC], i["e_down"][NE * P:(NE + 1) * P, :], "ld_shared")

            sp.wait_ge(S["v_out"], 2)
            for b in range(NB):
                if b >= 2:
                    sp.wait_ge(S["av_mm"], 2 * (b - 1))
                if b:
                    sp.wait_ge(S["vb_in"], 16 * b)
                sp.dma_start(Vb[:, b % 2, :], VL[b * R:(b + 1) * R, :]).then_inc(S["vb_in"], 16)

            def load_slots(j):
                src = x_slots[j * SLOTS:(j + 1) * SLOTS, :].rearrange("(q p) d -> p q d", p=P)
                sp.dma_start(XG[:, j % 2, :].rearrange("p (q d) -> p q d", d=D), src).then_inc(ld_slots[j % 2], 16)

            sp.wait_ge(S["scattered"], 16 * 2 * TT)
            sp.wait_ge(S["av_out"], 2 * NB)
            load_slots(0)
            load_slots(1)
            for j in range(NTILE):
                if j + 2 < NTILE:
                    sp.wait_ge(S["slots_turned"], j + 1)
                    load_slots(j + 2)
                sp.wait_ge(S["y_out"], j + 1)
                dst = y_slots[j * SLOTS:(j + 1) * SLOTS, :].rearrange("(q p) d -> p q d", p=P)
                sp.dma_start(dst, YS[:, j % 2, :].rearrange("p (q d) -> p q d", d=D)).then_inc(y_stored[j % 2], 16)
            of = out.rearrange("b n d -> (b n) d")
            for t in range(TT):
                sp.wait_ge(S["h_moe"], 2 * (t + 1))
                sp.dma_start(of[t * P:t * P + rows(t), :], H[0:rows(t), t, :]).then_inc(S["stored"], 16)
            sp.wait_ge(S["stored"], 16 * TT)

        @block.gpsimd
        def _(pool):
            st = Steps(pool, S["p_step"])
            st.add(pool.memset(identw[:], 0.0))
            pool.memset(ones[:], 1.0).then_inc(S["const_ready"], 1)
            pool.iota(qcol[:, :], pattern=[[0, 1]], base=0, channel_multiplier=1,
                      allow_small_or_imprecise_dtypes=True).then_inc(S["iota_ready"], 1)
            pool.iota(iota8[:, :], pattern=[[1, NE]], base=0, channel_multiplier=0,
                      allow_small_or_imprecise_dtypes=True).then_inc(S["iota_ready"], 1)
            st.wait()
            st.add(pool.affine_select(out=identw[:], in_=identw[:], compare_op=ALU.not_equal, fill=1.0, base=0,
                                      pattern=[[-1, L]], channel_multiplier=1))
            st.wait()
            pool.tensor_copy(identb[:, :], ident).then_inc(S["const_ready"], 1)
            pool.tensor_copy(ident3[:, :].rearrange("p (a b) -> p a b", b=L), identw[:, :].unsqueeze(1).to_broadcast([P, 3, L])).then_inc(S["const_ready"], 1)
            pool.tensor_copy(identr[:, :].rearrange("p (a b) -> p a b", b=R), identw[0:R, 0:R].unsqueeze(1).to_broadcast([R, NH, R])).then_inc(S["const_ready"], 1)
            pool.memset(cst[:, 0:1], 1e-5).then_inc(S["const_ready"], 1)
            pool.memset(cst[:, 1:2], ROUNDER).then_inc(S["const_ready"], 1)
            pool.memset(cst[:, 2:3], 1.0).then_inc(S["const_ready"], 1)
            pool.memset(H[:, TT - 1, :], 0.0).then_inc(S["padded"], 1)
            pool.memset(dAr[:, :, 0:1], 0.0).then_inc(S["const_ready"], 1)
            pool.memset(dtv[:, :], 0.0).then_inc(S["const_ready"], 1)
            pool.memset(bcp.rearrange("p d (b n) -> p d b n", n=PADL)[:, :, :, 0:NCONV - 1].rearrange("p d b n -> p (d b) n"),
                        0.0).then_inc(S["const_ready"], 1)
            pool.memset(qs[:, :], 0.0).then_inc(S["const_ready"], 1)
            pool.memset(dAT[:, :], 0.0).then_inc(S["const_ready"], 1)
            pool.wait_ge(S["ids_ready"], 1)
            for b in range(NB):
                pool.indirect_dma_start(out=txt[:, b, :], out_offset=None, in_=i["emb"],
                                        in_offset=bass.IndirectOffsetOnAxis(ap=ids[:, b:b + 1], axis=0))\
                    .then_inc(S["gathered"], 16)
            pool.wait_ge(ln_turned, 3)
            pool.memset(XP.rearrange("p m (b n) -> p m b n", n=PADL)[:, :, :, 0:NCONV - 1].rearrange("p m b n -> p (m b) n"),
                        0.0).then_inc(S["padded"], 1)
            pool.wait_ge(S["ld_mamba"], 144)
            for k in range(2 * KD):
                pool.tensor_scalar(outw[:, k, :], outw[:, k, :], normw[:, k:k + 1], 1.0, ALU.mult, ALU.mult).then_inc(S["outw_scaled"], 1)
            for n, (d, b) in enumerate(ITS):
                pool.wait_ge(S["yd_ready"], 3 * (n + 1))
                if n == 0:
                    pool.wait_ge(S["z_evac"], 24)
                pool.tensor_tensor(CV[:, d * KD:(d + 1) * KD, b * L:(b + 1) * L], w1y[:, n % 2, :, :],
                                   ZS[:, d * KD:(d + 1) * KD, b * L:(b + 1) * L], ALU.mult).then_inc(S["yz_ready"], 1)
            pool.wait_ge(S["bi_flip"], 2)
            pool.memset(SS[:, TT - 1, :], 0.0).then_inc(S["padded"], 1)

            pool.wait_ge(S["q_range"], 2)
            pool.partition_all_reduce(qs[:, 16:18], qs[:, 14:16], P, RMAX).then_inc(S["q_range_all"], 1)
            pool.wait_ge(S["ham_ready"], 1)
            pool.partition_all_reduce(qs[:, 31:32], qs[:, 30:31], P, RMAX).then_inc(S["ham_all"], 1)
            pool.wait_ge(S["or_ready"], 1)
            pool.partition_all_reduce(qs[:, 42:44], qs[:, 40:42], P, RMAX).then_inc(S["or_all"], 1)

            pool.wait_ge(S["xc_ready"], 3 * 16)
            pool.memset(zeros[:, :], 0.0).then_inc(S["const_ready"], 1)
            pool.iota(column[:, :], pattern=[[1, P]], base=0, channel_multiplier=0,
                      allow_small_or_imprecise_dtypes=True).then_inc(S["const_ready"], 1)
            for b in range(NB):
                for g, (r, q) in enumerate(GROUPS):
                    pool.wait_ge(S["s_sum"], 6 * b + g + 1)
                    o = PRS[0:r, 6 * (b % 2) + g, 0:q * L].rearrange("p (a b) -> p a b", b=L)
                    pool.tensor_tensor(o, o, arc[0:r, 18 * (b % 2) + 3 * g:18 * (b % 2) + 3 * g + q].unsqueeze(2).to_broadcast([r, q, L]), ALU.mult).then_inc(S["p_norm"], 1)

            def load_weights(j, cols, src, s):
                pool.indirect_dma_start(out=WR[j % 3][:, cols], out_offset=None, in_=i[src],
                                        in_offset=bass.IndirectOffsetOnAxis(ap=expert[:, j:j + 1], axis=0))\
                    .then_inc(s[j % 3], 16)

            GATE_UP, DOWN = slice(0, W2), slice(W2, EWC)
            for g, (kind, c) in enumerate(ITEMS):
                w = TOK(kind, c)
                for m in range(KH):
                    n = g * KH + m
                    if not on_dve(g):
                        pool.wait_ge(S["g_silu"], n + 1)
                        pool.wait_ge(S["u_clip"], n + 1)
                        if g:
                            pool.wait_ge(S["hh_ready"], n)
                        if m == 0 and g >= 2:
                            pool.wait_ge(S["e_mm"], g - 1)
                        pool.tensor_tensor(HH[:, g % 2, m * SLOTS:m * SLOTS + w], GS[:, n % 3, 0:w], UM[:, n % 3, 0:w], ALU.mult)\
                            .then_inc(S["hh_ready"], 1)
                    t = n - KH
                    if 0 <= t < TT:
                        if t == 0:
                            pool.wait_ge(S["x_cleared"], 16)
                            pool.wait_ge(S["slots_ready"], 1)
                        for k in range(2):
                            at = slots[0:rows(t), k * TT + t:k * TT + t + 1]
                            pool.indirect_dma_start(out=x_slots, in_=X[0:rows(t), t, :], in_offset=None,
                                                    out_offset=bass.IndirectOffsetOnAxis(ap=at, axis=0))\
                                .then_inc(S["scattered"], 16)
                    elif TT <= t < TT + 3:
                        if t == TT:
                            pool.wait_ge(S["slots_ready"], 2)
                            pool.wait_ge(S["wo_mm"], TT)
                        load_weights(t - TT, GATE_UP, "e_gate_up", ld_w)
                        load_weights(t - TT, DOWN, "e_down", ld_down)
                    if kind == "routed" and 1 <= c and c + 2 < NTILE:
                        if m == 0:
                            pool.wait_ge(S["gu_mm"], 2 * KH * g)
                            load_weights(c + 2, GATE_UP, "e_gate_up", ld_w)
                        elif m == KH - 1:
                            pool.wait_ge(S["e_mm"], g)
                            load_weights(c + 2, DOWN, "e_down", ld_down)
            for k in range(2):
                pool.wait_ge(y_stored[k], 16 * (NTILE // 2))
            for t in range(TT):
                for k in range(2):
                    pool.indirect_dma_start(out=YG[0:rows(t), k * TT + t, :], out_offset=None, in_=y_slots,
                                            in_offset=bass.IndirectOffsetOnAxis(ap=slots[0:rows(t), k * TT + t:k * TT + t + 1], axis=0))\
                        .then_inc(y_back[t // 3], 16)

        @block.scalar
        def _(act):
            def ln(k, w=None):
                act.wait_ge(ln_var, k * TT + TT)
                nc.scalar.activation(std[:, 0:TT], mv[:, :, 1], ACT.Sqrt, bias=cst[:, 0:1]).then_inc(ln_std, 1)
                if k == 0:
                    act.wait_ge(ln0_vx, 1)
                    nc.scalar.activation(std[:, TT:2 * TT], prod[:, :], ACT.Sqrt, bias=cst[:, 0:1]).then_inc(ln0_std2, 1)
                for g in range(3):
                    act.wait_ge(ln_turned, k * 3 + g + 1)
                    a, b = bank[2 * (g % 2)], bank[2 * (g % 2) + 1]
                    if w is None:
                        nc.scalar.copy(XTa[:, g * CM:(g + 1) * CM], a[:, 0:CM]).then_inc(ln_out, 1)
                        nc.scalar.copy(XTb[0:DB, g * CM:(g + 1) * CM], b[0:DB, 0:CM]).then_inc(ln_out, 1)
                        if LN_OUT[k] == 3:
                            nc.scalar.copy(XTb[DB:P, g * CM:(g + 1) * CM], b[0:DB, 0:CM]).then_inc(ln_out, 1)
                    else:
                        nc.scalar.activation(XTa[:, g * CM:(g + 1) * CM], a[:, 0:CM], ACT.Identity,
                                             scale=w[:, 0, 0:1], bias=w[:, 0, 1:2]).then_inc(ln_out, 1)
                        nc.scalar.activation(XTb[0:DB, g * CM:(g + 1) * CM], b[0:DB, 0:CM], ACT.Identity,
                                             scale=w[0:DB, 1, 0:1], bias=w[0:DB, 1, 1:2]).then_inc(ln_out, 1)

            act.wait_ge(S["const_ready"], 12)
            act.wait_ge(S["ld_inw"], 96)
            ln(0, ln1)
            for d, c in [(0, c) for c in range(4)] + [(1, c) for c in range(4)]:
                if (d, c) == (1, 2):
                    act.wait_ge(S["dt_abs"], 1)
                    nc.scalar.activation(dte[:, :], dte[:, :], ACT.Exp).then_inc(S["dt_exp"], 1)
                    act.wait_ge(S["dt_arg"], 1)
                    nc.scalar.activation(dA[:, :], dA[:, :], ACT.Exp, scale=-1.0).then_inc(S["dA_exp"], 1)
                for m in range(3):
                    k = k_inproj(d, c, m)
                    act.wait_ge(S["inproj"], k + 1)
                    nc.scalar.activation(ZS[:, d * KD + m, c * 2 * L:(c + 1) * 2 * L], bank[INBANK[k % len(INBANK)]][:, 0:2 * L], ACT.Silu)\
                        .then_inc(S["z_evac"], 1)
                if (d, c) == (0, 3):
                    act.wait_ge(S["ld_mamba"], 144)
                    nc.scalar.activation(alog[:, :], alog[:, :], ACT.Exp).then_inc(S["a_exp"], 1)
            act.wait_ge(S["dt_ready"], 2)
            nc.scalar.copy(dAT[0:96, :], bank[4][0:96, 0:L]).then_inc(S["dA_exp"], 1)
            def squares(d):
                act.wait_ge(S["yz_ready"], 8 * (d + 1))
                act.wait_ge(S["convolved"], 8)
                for k in range(KD):
                    nc.scalar.activation(SQ[:, d * KD + k, :], CV[:, d * KD + k, :], ACT.Square).then_inc(S["sq_ready"], 1)

            for n, (d, b) in enumerate(ITS):
                act.wait_ge(S["convolved"], 4 * (d + 1))
                if n >= 2:
                    act.wait_ge(S["g_ready"], n - 1)
                    act.wait_ge(S["yd_ready"], 3 * (n - 1))
                nc.scalar.activation(xcs[:, n % 2, :, :], CV[:, d * KD:(d + 1) * KD, b * L:(b + 1) * L], ACT.Silu).then_inc(S["xc_ready"], 1)
                nc.scalar.activation(Bs[:, n % 2, :], bcv[0:NS, d, b * L:(b + 1) * L], ACT.Silu).then_inc(S["xc_ready"], 1)
                nc.scalar.activation(Cs[:, n % 2, :], bcv[32:32 + NS, d, b * L:(b + 1) * L], ACT.Silu).then_inc(S["xc_ready"], 1)
                if n == 11:
                    squares(0)
            squares(1)
            act.wait_ge(S["ss_ready"], 1)
            nc.scalar.activation(rss[:, 0:2 * TT - 2], bank[7][:, 0:2 * TT - 2], ACT.Sqrt, scale=1.0 / DIN, bias=cst[:, 0:1]).then_inc(S["ss_std"], 1)
            nc.scalar.activation(rss[0:LAST, 2 * TT - 2:2 * TT], bank[7][0:LAST, 2 * TT - 2:2 * TT], ACT.Sqrt,
                                 scale=1.0 / DIN, bias=cst[0:LAST, 0:1]).then_inc(S["ss_std"], 1)
            act.wait_ge(S["ss_inv"], 2)
            for t in range(TT):
                for d in range(2):
                    n = 2 * t + d
                    act.wait_ge(S["op_ready"], n + 1)
                    nc.scalar.activation(BT[0:rows(t), t, d * D:(d + 1) * D], bank[n % 4][0:rows(t), 0:D], ACT.Identity,
                                         scale=rs[0:rows(t), n:n + 1]).then_inc(S["bt_ready"], 1)
            for g in range(3):
                n = CM if g < 2 else T - 2 * CM
                act.wait_ge(S["bt_turned"], g + 1)
                nc.scalar.copy(BI[:, 0, g * CM:g * CM + n], bank[4][:, 0:n]).then_inc(S["bi_act"], 1)
                nc.scalar.copy(BI[0:64, 1, g * CM:g * CM + n], bank[5][0:64, 0:n]).then_inc(S["bi_act"], 1)
            act.wait_ge(S["ld_ffw"], 64)
            for k in range(3 * KH):
                c, m = divmod(k, KH)
                act.wait_ge(S["h1_ready"], k + 1)
                nc.scalar.activation(H1[:, m, c * CH:(c + 1) * CH], bank[k % 4][:, 0:CH], ACT.Gelu, bias=ffb1[:, m:m + 1]).then_inc(S["h1_out"], 1)
            for t in range(TT):
                act.wait_ge(S["f2_ready"], t + 1)
                nc.scalar.activation(G2[0:rows(t), t, :], bank[4 + t % 4][0:rows(t), 0:D], ACT.Gelu).then_inc(S["f2_out"], 1)
            act.wait_ge(S["ln2_var"], TT)
            nc.scalar.activation(std[:, 0:TT], mv[:, :, 1], ACT.Sqrt, bias=cst[:, 0:1]).then_inc(S["ln2_std"], 1)

            ln(1)
            act.wait_ge(S["q_gmax"], 1)
            nc.scalar.activation(qs[:, 6:8], qs[:, 4:6], ACT.Sqrt).then_inc(S["q_sqrt"], 1)
            nc.scalar.activation(qs[:, 10:12], qs[:, 8:10], ACT.Sqrt).then_inc(S["q_sqrt"], 1)
            act.wait_ge(S["q_fac"], 1)
            for c in range(2):
                n, xt = (DA, XTa) if c == 0 else (DB, XTb)
                nc.scalar.activation(UR[0:n, c, :], xt[0:n, 0:T], ACT.Identity, scale=qs[0:n, 24 + c:25 + c], bias=cst[0:n, 1:2]).then_inc(S["q_u"], 1)
            act.wait_ge(S["ld_small"], 96)
            for n in range(3 * KH):
                c, m = divmod(n, KH)
                act.wait_ge(S["hq_mm"], n + 1)
                nc.scalar.activation(HG[:, m, c * CH:(c + 1) * CH], bank[n % 4][:, 0:CH], ACT.Gelu,
                                     scale=qs[:, 50 + m:51 + m], bias=qb1[:, m:m + 1]).then_inc(S["hg_ready"], 1)
            act.wait_ge(S["hs_ready"], 1)
            for m in range(KH):
                nc.scalar.activation(HG[:, m, :], HG[:, m, :], ACT.Identity, scale=qs[:, 33:34], bias=cst[:, 1:2]).then_inc(S["hr_ready"], 1)
            for n in range(6):
                c, m = divmod(n, 2)
                r = DA if m == 0 else DB
                act.wait_ge(S["ot_mm"], n + 1)
                nc.scalar.activation(OT[0:r, m, c * CH:(c + 1) * CH], bank[n % 4][0:r, 0:CH], ACT.Identity,
                                     scale=qs[0:r, 34 + m:35 + m], bias=qb2[0:r, m:m + 1]).then_inc(S["ot_ready"], 1)
            act.wait_ge(S["of_ready"], 1)
            for m in range(2):
                r = DA if m == 0 else DB
                nc.scalar.activation(OT[0:r, m, :], OT[0:r, m, :], ACT.Identity, scale=qs[0:r, 46:47], bias=cst[0:r, 1:2]).then_inc(S["om_ready"], 1)

            ln(2)
            def value_out(n, V):
                for k in range(2):
                    m = (0 if V is VL else 2 * n + 2) + k
                    act.wait_ge(S["v_mm"], m + 1)
                    if V is VL:
                        nc.scalar.copy(VL[:, k * CM:(k + 1) * CM], bank[k][0:NB * R, 0:CM]).then_inc(S["v_out"], 1)
                    else:
                        if n >= 2:
                            act.wait_ge(S["av_mm"], 2 * (n - 1))
                        nc.scalar.copy(Va[:, n % 2, k * CM:(k + 1) * CM], bank[k][:, 0:CM]).then_inc(S["v_out"], 1)

            def query_key_out(b, j):
                for k in range(2):
                    act.wait_ge(S["qk_mm"], 4 * b + 2 * j + k + 1)
                    at = (2 * k + j) * 3 * L
                    nc.scalar.copy(QK[:, b % 2, at:at + 3 * L], bank[k][:, 0:3 * L]).then_inc(S["qk_out"], 1)

            def exponentials(b, w):
                for g in (2 * w, 2 * w + 1):
                    r, q = GROUPS[g]
                    act.wait_ge(S["s_sub"], 6 * b + g + 1)
                    o = PRS[0:r, 6 * (b % 2) + g, 0:q * L]
                    nc.scalar.activation(o, o, ACT.Exp, scale=0.125).then_inc(S["s_exp"], 1)

            def turned_out(b, g):
                act.wait_ge(S["p_turned"], 4 * b + g + 1)
                if b:
                    act.wait_ge(S["av_mm"], 2 * b)
                nc.scalar.copy(PT[:, 3 * g:3 * g + 3, :], bank[4][:, 0:3 * L].rearrange("p (a b) -> p a b", b=L)).then_inc(S["pt_act"], 1)

            def heads_out(b, j):
                act.wait_ge(S["av_mm"], 2 * b + j + 1)
                nc.scalar.copy(OA[:, 3 * j:3 * j + 3, b * L:(b + 1) * L],
                               bank[6 + j][:, 0:3 * L].rearrange("p (a b) -> p a b", b=L)).then_inc(S["av_out"], 1)

            value_out(0, VL)
            query_key_out(0, 0)
            query_key_out(0, 1)
            for i in range(NB + 1):
                if i:
                    turned_out(i - 1, 0)
                if i < NB:
                    exponentials(i, 0)
                if i:
                    turned_out(i - 1, 1)
                if i < NB:
                    exponentials(i, 1)
                if i:
                    turned_out(i - 1, 2)
                if i < NB:
                    exponentials(i, 2)
                if i:
                    turned_out(i - 1, 3)
                if i + 1 < NB:
                    query_key_out(i + 1, 0)
                if i:
                    heads_out(i - 1, 0)
                if i + 1 < NB:
                    query_key_out(i + 1, 1)
                if i:
                    heads_out(i - 1, 1)
                if i < NB:
                    value_out(i, Va)

            ln(3)

            def lead_x(g):
                kind, c = ITEMS[g]
                w = TOK(kind, c)
                if kind == "shared":
                    a, b = XTa[:, c * SLOTS:c * SLOTS + w], XTb[0:DB, c * SLOTS:c * SLOTS + w]
                else:
                    act.wait_ge(S["slots_turned"], c + 1)
                    o = bank[6 + c % 2]
                    a, b = o[:, 0:SLOTS], o[0:DB, SLOTS:2 * SLOTS]
                if g >= 2:
                    act.wait_ge(S["gu_mm"], 2 * KH * (g - 1))
                nc.scalar.copy(XH[g % 2][:, 0:w], a).then_inc(S["x_lead"], 1)
                nc.scalar.copy(XB[g % 2][0:DB, 0:w], b).then_inc(S["x_lead"], 1)

            def lead_w(n):
                g, m = divmod(n, KH)
                kind, c = ITEMS[g]
                if m == 0 and kind == "routed":
                    act.wait_ge(ld_w[c % 3], 16 * (c // 3 + 1))
                elif n == 0:
                    act.wait_ge(S["ld_shared"], 32)
                if n >= 4:
                    act.wait_ge(S["gu_mm"], 2 * (n - 3))
                nc.scalar.copy(WH[n % 4][:, :], weights(g)[:, m * BLK:(m + 1) * BLK]).then_inc(S["w_lead"], 1)

            lead_x(0)
            for n in range(4):
                lead_w(n)
            act.wait_ge(S["g_dve"], 1)
            nc.scalar.activation(ge[:, :], gn[:, :], ACT.Exp).then_inc(S["g_act"], 1)
            act.wait_ge(S["g_dve"], 2)
            nc.scalar.activation(gs[:, :], gs[:, :], ACT.Sqrt).then_inc(S["g_act"], 1)
            def output(g):
                j = ITEMS[g][1]
                act.wait_ge(S["e_mm"], g + 1)
                if j >= 2:
                    act.wait_ge(y_stored[j % 2], 16 * (j // 2))
                nc.scalar.copy(YS[:, j % 2, :], bank[4 + g % 2][:, 0:GCH * D]).then_inc(S["y_out"], 1)

            for g, (kind, c) in enumerate(ITEMS):
                w = TOK(kind, c)
                for m in range(KH):
                    n = g * KH + m
                    act.wait_ge(S["g_min"], n + 1)
                    if n >= 3:
                        act.wait_ge(S["hh_ready"], n - 2)
                    nc.scalar.activation(GS[:, n % 3, 0:w], GM[:, n % 3, 0:w], ACT.Silu).then_inc(S["g_silu"], 1)
                    if n + 4 < STEPS:
                        lead_w(n + 4)
                    if g == AFTER and m + 1 == OUT_AT:
                        output(g - 1)
                        lead_x(g + 1)
                if g != AFTER and g + 1 < len(ITEMS):
                    lead_x(g + 1)
                if g and g != AFTER and ITEMS[g - 1][0] == "routed":
                    output(g - 1)

        @block.tensor
        def _(pe):
            mm = nc.tensor.matmul

            def turn(k, src):
                for g in range(3):
                    pe.wait_ge(ln_x, k * TT + 3 * (g + 1))
                    if g == 2:
                        pe.wait_ge(ln_out, LN_BASE[k] + LN_OUT[k])
                    a, b = bank[2 * (g % 2)], bank[2 * (g % 2) + 1]
                    for j in range(3):
                        t = 3 * g + j
                        nc.tensor.transpose(a[:, j * P:(j + 1) * P], src[:, t, 0:DA], ident)
                        last = nc.tensor.transpose(b[0:DB, j * P:(j + 1) * P], src[:, t, DA:D], ident)
                    last.then_inc(ln_turned, 1)

            pe.wait_ge(S["const_ready"], 12)
            pe.wait_ge(S["p_step"], 2)
            pe.wait_ge(S["score_ready"], 1)
            for b in range(NB):
                last = nc.tensor.transpose(bank[2 + b // 4][0:NX, (b % 4) * 76:(b % 4 + 1) * 76], score[:, b * NX:(b + 1) * NX],
                                           identw[0:76, 0:76])
                if b % 4 == 3:
                    last.then_inc(S["scoreT"], 1)
            pe.wait_ge(S["ld_embed"], 48)
            for j in range(NB // 2):
                for k in range(KI):
                    last = mm(bank[j // 2][:, (j % 2) * D:(j % 2 + 1) * D], patches[:, k, j * P:(j + 1) * P], tokw[:, k, :],
                              start=k == 0, stop=k == KI - 1)
                if j % 2:
                    last.then_inc(S["img_out"], 1)
            pe.wait_ge(S["img_ready"], 2)
            pe.wait_ge(S["ids_ready"], 1)
            turn(0, XS)

            def inproj(d, chunks):
                xa, xb = (XTa, XTb) if d == 0 else (XRa, XRb)
                for c in chunks:
                    for m in range(7):
                        k = k_inproj(d, c, m)
                        if k >= len(INBANK):
                            pe.wait_ge(*inproj_free(k - len(INBANK)))
                        o = bank[INBANK[k % len(INBANK)]]
                        cols = slice(m * P, m * P + P) if m < 6 else slice(CB, CB + 48)
                        M = P if m < 6 else 48
                        mm(o[0:M, 0:2 * L], inw[:, 2 * d, cols], xa[:, c * 2 * L:(c + 1) * 2 * L], start=True, stop=False)
                        mm(o[0:M, 0:2 * L], inw[0:DB, 2 * d + 1, cols], xb[0:DB, c * 2 * L:(c + 1) * 2 * L],
                           start=False, stop=True).then_inc(S["inproj"], 1)

            pe.wait_ge(ln_out, 6)
            pe.wait_ge(S["ld_inw"], 96)
            inproj(0, range(4))
            pe.wait_ge(S["flipped"], 2)
            inproj(1, range(2))
            for d, b in ITS:
                xa, xb = (XTa, XTb) if d == 0 else (XRa, XRb)
                for at, n, col in ((0, P, DTC(d, b)), (P, R, 96 + DTC(d, b))):
                    cols = slice(b * L + at, b * L + at + n)
                    mm(bank[4][0:n, col:col + NH], xa[:, cols], inw[:, 2 * d, CDT:WCOLS], start=True, stop=False)
                    last = mm(bank[4][0:n, col:col + NH], xb[0:DB, cols], inw[0:DB, 2 * d + 1, CDT:WCOLS], start=False, stop=True)
            last.then_inc(S["dt_ready"], 1)
            inproj(1, range(2, 4))
            pe.wait_ge(S["dA_ready"], 1)
            pe.wait_ge(S["x_evac"], 32)
            pe.wait_ge(S["z_evac"], 24)
            nc.tensor.transpose(bank[4][0:96, 0:P], dA[:, 0:96], ident)
            nc.tensor.transpose(bank[4][0:96, P:L], dA[0:R, 96:192], identw[0:R, 0:R]).then_inc(S["dt_ready"], 1)
            pe.wait_ge(S["dA_exp"], 2)

            def front(n):
                d, b = ITS[n]
                p = n % 2
                if n:
                    pe.wait_ge(S["decay_used"], 2 * n)
                for g in range(2):
                    for h in range(3):
                        row = DTC(d, b) + 3 * g + h
                        last = mm(bank[3 + g][:, h * L:(h + 1) * L], ident[:, row:row + 1].to_broadcast([P, P]), dAT[:, :],
                                  start=True, stop=True)
                    last.then_inc(S["decay_ready"], 1)
                pe.wait_ge(S["xc_ready"], 3 * (n + 1))
                if n:
                    pe.wait_ge(S["dtx_ready"], 2 * n)
                for m in range(KD):
                    nc.tensor.transpose(bank[0][:, m * P:(m + 1) * P], xcs[:, p, m, 0:P], ident)
                    last = nc.tensor.transpose(bank[1][0:R, m * P:(m + 1) * P], xcs[:, p, m, P:L], ident)
                last.then_inc(S["xc_turned"], 1)
                if n >= 2:
                    pe.wait_ge(S["m_ready"], 2 * (n - 1))
                o = bank[2 if p == 0 else 7]
                mm(o[:, 0:L], Bs[:, p, 0:P], Cs[:, p, :], start=True, stop=True)
                mm(o[0:R, L:L + R], Bs[:, p, P:L], Cs[:, p, P:L], start=True, stop=True).then_inc(S["g_ready"], 1)

            def back(n):
                p = n % 2
                pe.wait_ge(S["m_ready"], 2 * (n + 1))
                if n >= 2:
                    pe.wait_ge(S["yd_ready"], 3 * (n - 1))
                o = bank[5 + p]
                for h in range(NH):
                    q, r = h // 2, (h % 2) * 64
                    mm(o[r:r + 64, q * L:(q + 1) * L], dtx[:, p, h * 64:(h + 1) * 64], MM[:, p, h, :], start=True, stop=False)
                    last = mm(o[r:r + 64, q * L + P:(q + 1) * L], dtxr[:, p, h * 64:(h + 1) * 64], MMr[:, p, h, :],
                              start=False, stop=True)
                last.then_inc(S["y_ready"], 1)

            for n in range(len(ITS) + 1):
                if n < len(ITS):
                    front(n)
                if n:
                    back(n - 1)
            for d in range(2):
                pe.wait_ge(S["sq_added"], d + 1)
                for t in range(TT):
                    last = mm(bank[7][0:rows(t), 2 * t + d:2 * t + d + 1], SQ[:, d * KD, t * P:t * P + rows(t)], ones[:, 0:1],
                              start=True, stop=True)
            last.then_inc(S["ss_ready"], 1)
            pe.wait_ge(S["outw_scaled"], 2 * KD)
            for t in range(TT):
                for d in range(2):
                    n = 2 * t + d
                    if n >= 4:
                        pe.wait_ge(S["bt_ready"], n - 3)
                    for k in range(KD):
                        last = mm(bank[n % 4][0:rows(t), 0:D], CV[:, d * KD + k, t * P:t * P + rows(t)], outw[:, d * KD + k, :],
                                  start=k == 0, stop=k == KD - 1)
                    last.then_inc(S["op_ready"], 1)
            for g in range(3):
                pe.wait_ge(S["bt_ready"], 6 * (g + 1))
                if g == 0:
                    pe.wait_ge(S["yd_ready"], 48)
                else:
                    pe.wait_ge(S["bi_act"], 2 * g)
                    pe.wait_ge(S["bi_dve"], 2 * g)
                for j in range(3):
                    t = 3 * g + j
                    for k in range(3):
                        last = nc.tensor.transpose(bank[4 + k][:, j * P:j * P + rows(t)], BT[0:rows(t), t, k * P:(k + 1) * P],
                                                   identw[0:rows(t), 0:rows(t)])
                last.then_inc(S["bt_turned"], 1)
            pe.wait_ge(S["bi_act"], 6)
            pe.wait_ge(S["bi_flip"], 2)
            pe.wait_ge(S["ld_ffw"], 64)
            for n in range(3 * KH):
                c, m = divmod(n, KH)
                if n < 4:
                    pe.wait_ge(S["bt_ready"], 18)
                else:
                    pe.wait_ge(S["h1_out"], n - 3)
                for k in range(KD):
                    last = mm(bank[n % 4][:, 0:CH], ffw1[:, k, m * P:(m + 1) * P], BI[:, k, c * CH:(c + 1) * CH],
                              start=k == 0, stop=k == KD - 1)
                last.then_inc(S["h1_ready"], 1)
            pe.wait_ge(S["h1_out"], 3 * KH)
            pe.wait_ge(S["ld_ffw"], 64)
            for t in range(TT):
                if t >= 4:
                    pe.wait_ge(S["f2_out"], t - 3)
                o = bank[4 + t % 4][0:rows(t), 0:D]
                for k in range(KH):
                    mm(o, H1[:, k, t * P:t * P + rows(t)], ffw2[:, k, :], start=k == 0, stop=False)
                mm(o, ones[0:1, 0:rows(t)], ffb2[:, :], start=False, stop=True).then_inc(S["f2_ready"], 1)

            turn(1, X)
            pe.wait_ge(S["q_diag"], 2)
            pe.wait_ge(ln_out, LN_BASE[2])
            mm(bank[4][:, 0:DA], ones[:, :], csdiag[:, 0:DA], start=True, stop=True)
            mm(bank[4][:, DA:D], ones[0:DB, :], csdiag[0:DB, DA:D], start=True, stop=True).then_inc(S["q_csb"], 1)
            for k in range(KH):
                pe.wait_ge(S["q2_ready"], 2)
                o = bank[6 + k % 2]
                if k >= 2:
                    pe.wait_ge(S["q2_out"], k - 1)
                mm(o[:, 0:DA], q2[:, 0, k * P:(k + 1) * P], identb[:, :], start=True, stop=True)
                mm(o[:, DA:D], q2[0:DB, 1, k * P:(k + 1) * P], identb[0:DB, 0:DB], start=True, stop=True).then_inc(S["q2_turned"], 1)
            pe.wait_ge(S["q1_ready"], 1)
            for k in range(KH):
                if k >= 2:
                    pe.wait_ge(S["q1_out"], k - 1)
                elif k == 0:
                    pe.wait_ge(S["q2_out"], KH)
                o = bank[6 + k % 2]
                mm(o[:, 0:P], q1[:, k, 0:DA], identb[:, :], start=True, stop=True)
                mm(o[0:DB, P:2 * P], q1[:, k, DA:D], identb[:, :], start=True, stop=True).then_inc(S["q1_turned"], 1)
            pe.wait_ge(S["q1_out"], KH)
            pe.wait_ge(S["q_ui"], 2)
            for n in range(3 * KH):
                c, m = divmod(n, KH)
                if n >= 4:
                    pe.wait_ge(S["hg_ready"], n - 3)
                mm(bank[n % 4][:, 0:CH], q1t[:, 0, m * P:(m + 1) * P], UQ[:, 0, c * CH:(c + 1) * CH], start=True, stop=False)
                mm(bank[n % 4][:, 0:CH], q1t[0:DB, 1, m * P:(m + 1) * P], UQ[0:DB, 1, c * CH:(c + 1) * CH],
                   start=False, stop=True).then_inc(S["hq_mm"], 1)
            for n in range(6):
                c, m = divmod(n, 2)
                r = DA if m == 0 else DB
                if n >= 4:
                    pe.wait_ge(S["ot_ready"], n - 3)
                for k in range(KH):
                    if n == 0:
                        pe.wait_ge(S["hi_ready"], k + 1)
                    last = mm(bank[n % 4][0:r, 0:CH], q2t[:, k, m * DA:m * DA + r], HQ[:, k, c * CH:(c + 1) * CH],
                              start=k == 0, stop=k == KH - 1)
                last.then_inc(S["ot_mm"], 1)
            for t in range(TT):
                pe.wait_ge(S["oq_ready"], 2)
                if t >= 4:
                    pe.wait_ge(S["h_ffn"], t - 3)
                elif t == 0:
                    pe.wait_ge(S["ot_ready"], 6)
                o = bank[4 + t % 4]
                nc.tensor.transpose(o[0:rows(t), 0:DA], OT[:, 0, t * P:t * P + rows(t)], ident)
                nc.tensor.transpose(o[0:rows(t), DA:D], OT[0:DB, 1, t * P:t * P + rows(t)], identw[0:DB, 0:DB]).then_inc(S["oq_turned"], 1)

            turn(2, X)
            pe.wait_ge(ln_out, LN_BASE[3])
            pe.wait_ge(S["ld_att"], 16 * 9)
            def query_key(b, j):
                cols = slice(b * L, (b + 1) * L)
                if j == 0:
                    pe.wait_ge(S["v_out"], 2 + 2 * max(b - 1, 0))
                else:
                    pe.wait_ge(S["qk_out"], 4 * b + 2)
                for q in range(3):
                    m = 3 * j + q
                    for k, w in ((0, awq), (1, awk)):
                        mm(bank[k][:, q * L:(q + 1) * L], w[:, m * P:(m + 1) * P], XTa[:, cols], start=True, stop=False)
                    for k in range(2):
                        r = slice(k * DB, (k + 1) * DB)
                        last = mm(bank[k][:, q * L:(q + 1) * L], awqk2[r, m * P:(m + 1) * P], XTb[r, cols], start=False, stop=True)
                        if q == 2:
                            last.then_inc(S["qk_mm"], 1)

            def value(xa, xb, n):
                for k in range(2):
                    mm(bank[k][0:n, 0:CM], xa, awv[:, k * CM:(k + 1) * CM], start=True, stop=False)
                for k in range(2):
                    r = slice(k * DB, (k + 1) * DB)
                    mm(bank[k][0:n, 0:CM], xb[r, :], awv2[r, :], start=False, stop=True).then_inc(S["v_mm"], 1)

            def scores(b, w):
                p = b % 2
                if w == 0:
                    pe.wait_ge(S["qk_out"], 4 * (b + 1))
                if w == 1 and b >= 2:
                    pe.wait_ge(S["av_out"], 2 * (b - 1))
                if w != 1 and (w or b):
                    pe.wait_ge(S["s_sub"], 6 * b + (2 if w else 0))
                for e in (range(3 * w, 3 * w + 3) if w < 2 else range(6)):
                    for par in range(2):
                        r, o = par * 64, bank[SBANK[2 * w + par]]
                        keys = QK[r:r + 64, p, (6 + e) * L:(7 + e) * L]
                        if w < 2:
                            q = e % 3
                            last = mm(o[:, q * L:(q + 1) * L], QK[r:r + 64, p, e * L:e * L + P], keys, start=True, stop=True)
                        else:
                            sl, q = (e % 3) * 32, e // 3
                            last = mm(o[sl:sl + 32, q * L:(q + 1) * L], QK[r:r + 64, p, (e + 1) * L - 32:(e + 1) * L], keys,
                                      start=True, stop=True)
                        if e == (3 * w + 2 if w < 2 else 5):
                            last.then_inc(S["s_mm"], 1)

            def turn_probs(b, g):
                p, n = b % 2, 4 * b + g
                if g == 0:
                    pe.wait_ge(S["p_norm"], 6 * (b + 1))
                if n >= 1:
                    pe.wait_ge(S["pt_act"], n)
                    pe.wait_ge(S["pt_dve"], n)
                for q in range(3):
                    h = 3 * g + q
                    par, e = h % 2, h // 2
                    m, c = 2 * (e // 3) + par, (e % 3) * L
                    u, r = (e // 3) * L, (e % 3) * 32 + 32 - R
                    nc.tensor.transpose(bank[4][:, q * L:q * L + P], PRS[:, 6 * p + m, c:c + P], ident)
                    nc.tensor.transpose(bank[5][0:R, q * L:q * L + P], PRS[:, 6 * p + m, c + P:c + L], ident)
                    rest = identw[0:96, r:r + R]
                    mm(bank[4][:, q * L + P:(q + 1) * L], PRS[0:96, 6 * p + 4 + par, u:u + P], rest, start=True, stop=True)
                    last = mm(bank[5][0:R, q * L + P:(q + 1) * L], PRS[0:96, 6 * p + 4 + par, u + P:u + L], rest, start=True, stop=True)
                last.then_inc(S["p_turned"], 1)

            def apply(b, j):
                p = b % 2
                pe.wait_ge(S["pt_act"], 4 * b + 2 * j + 2)
                pe.wait_ge(S["pt_dve"], 4 * b + 2 * j + 2)
                pe.wait_ge(S["v_out"], 2 + 2 * (b + 1))
                pe.wait_ge(S["vb_in"], 16 * (b + 1))
                pe.wait_ge(S["s_sub"], min(6 * (b + 1) + 4, 6 * NB))
                if b:
                    pe.wait_ge(S["av_out"], 2 * (b - 1) + j + 1)
                for q in range(6):
                    h = 6 * j + q
                    r, m = (h % 2) * 64, q // 2
                    o = bank[6 + j][r:r + 64, m * L:(m + 1) * L]
                    mm(o, Va[:, p, h * 64:(h + 1) * 64], PT[:, h, :], start=True, stop=False)
                    last = mm(o, Vb[:, p, h * 64:(h + 1) * 64], PTr[:, h, :], start=False, stop=True)
                last.then_inc(S["av_mm"], 1)

            pe.wait_ge(S["tails_ready"], 1)
            value(XL[:, 0, :], XL[:, 1, :], NB * R)
            query_key(0, 0)
            query_key(0, 1)
            for i in range(NB + 1):
                if i < NB:
                    scores(i, 0)
                if i:
                    turn_probs(i - 1, 0)
                if i < NB:
                    scores(i, 1)
                if i:
                    turn_probs(i - 1, 1)
                if i < NB:
                    scores(i, 2)
                if i:
                    turn_probs(i - 1, 2)
                    turn_probs(i - 1, 3)
                if i + 1 < NB:
                    query_key(i + 1, 0)
                if i:
                    apply(i - 1, 0)
                if i + 1 < NB:
                    query_key(i + 1, 1)
                if i:
                    apply(i - 1, 1)
                if i < NB:
                    pe.wait_ge(S["qk_out"], min(4 * (i + 2), 4 * NB))
                    value(XTa[:, i * L:i * L + P], XTb[:, i * L:i * L + P], P)
            pe.wait_ge(S["av_out"], 2 * NB)
            for t in range(TT):
                if t >= 4:
                    pe.wait_ge(S["h_att"], t - 3)
                o = bank[t % 4][0:rows(t), 0:D]
                for k in range(KH):
                    mm(o, OA[:, k, t * P:t * P + rows(t)], awo[:, k, :], start=k == 0, stop=False)
                mm(o, ones[0:1, 0:rows(t)], abo[:, :], start=False, stop=True).then_inc(S["wo_mm"], 1)

            turn(3, X)
            pe.wait_ge(ln_out, LN_BASE[4])
            pe.wait_ge(S["ld_small"], 96)
            for t in range(TT):
                mm(bank[4][:, t * NE:(t + 1) * NE], XTa[:, t * P:(t + 1) * P], gatew[:, 0, :], start=True, stop=False)
                last = mm(bank[4][:, t * NE:(t + 1) * NE], XTb[0:DB, t * P:(t + 1) * P], gatew[0:DB, 1, :], start=False, stop=True)
            last.then_inc(S["g_mm"], 1)

            def up(g):
                kind, c = ITEMS[g]
                w = TOK(kind, c)
                pe.wait_ge(S["x_rest"], 2 * (g + 1))
                xh, xr, xb = XH[g % 2][:, 0:w], XR[g % 2][:, 0:w], XB[g % 2][:, 0:w]
                for m in range(KH):
                    n = g * KH + m
                    pe.wait_ge(S["w_rest"], n + 1)
                    if n >= 2:
                        pe.wait_ge(S["g_min"], n - 1)
                        pe.wait_ge(S["u_clip"], n - 1)
                    for q in range(2):
                        o = bank[2 * (n % 2) + q][:, 0:w]
                        a, b = slice(q * P, (q + 1) * P), slice((2 + q) * P, (3 + q) * P)
                        mm(o, WH[n % 4][:, a], xh, start=True, stop=False)
                        mm(o, WH[n % 4][:, a], xr, start=False, stop=False)
                        mm(o, WL[n % 4][:, a], xh, start=False, stop=False)
                        mm(o, WH[n % 4][:, b], xb, start=False, stop=False)
                        mm(o, WL[n % 4][:, b], xb, start=False, stop=True).then_inc(S["gu_mm"], 1)
                    if g == AFTER and m + 1 == DOWN_AT:
                        down(g - 1)

            def turn_slots(j):
                pe.wait_ge(ld_slots[j % 2], 16 * (j // 2 + 1))
                if j >= 2:
                    pe.wait_ge(S["x_rest"], 2 * (FIRST + j - 1))
                o = bank[6 + j % 2]
                for q in range(GCH):
                    x = XG[:, j % 2, q * D:(q + 1) * D]
                    nc.tensor.transpose(o[:, q * P:(q + 1) * P], x[:, 0:DA], ident)
                    last = nc.tensor.transpose(o[0:DB, SLOTS + q * P:SLOTS + (q + 1) * P], x[:, DA:D], ident)
                last.then_inc(S["slots_turned"], 1)

            def down(g):
                kind, c = ITEMS[g]
                W = WS if kind == "shared" else WR[c % 3]
                pe.wait_ge(S["hh_ready"], KH * (g + 1))
                if kind == "routed":
                    pe.wait_ge(ld_down[c % 3], 16 * (c // 3 + 1))
                if g == 0:
                    pe.wait_ge(S["g_dve"], 1)
                if g >= 2:
                    pe.wait_ge(*emptied(g - 2))
                for q in range(TOK(kind, c) // P):
                    for k in range(KH):
                        at = k * SLOTS + q * P
                        last = mm(bank[4 + g % 2][:, q * D:(q + 1) * D], HH[:, g % 2, at:at + P], W[:, W2 + k * D:W2 + (k + 1) * D],
                                  start=k == 0, stop=k == KH - 1)
                last.then_inc(S["e_mm"], 1)

            for g in range(len(ITEMS) + 1):
                if g < len(ITEMS):
                    up(g)
                if g == 0:
                    pe.wait_ge(S["picked"], 1)
                    mm(bank[7][:, 0:RT], before[:, :], MB[:, :, :].rearrange("p t e -> p (t e)"), start=True, stop=True)
                    mm(bank[7][:, RT:2 * RT], ones[:, :], MB[:, :, :].rearrange("p t e -> p (t e)"), start=True, stop=True)\
                        .then_inc(S["counted"], 1)
                if g + 1 < len(ITEMS) and ITEMS[g + 1][0] == "routed":
                    if ITEMS[g + 1][1] == 0:
                        pe.wait_ge(S["slots_ready"], 1)
                    turn_slots(ITEMS[g + 1][1])
                if g and g != AFTER:
                    down(g - 1)

        @block.vector
        def _(dve):
            v = nc.vector
            st = Steps(dve, S["v_step"])

            def ln(k):
                for t in range(TT):
                    st.add(v.bn_stats(stats[:, t, :], H[:, t, :]))
                st.wait()
                for t in range(TT):
                    v.bn_aggr(mv[:, t, :], stats[:, t, :]).then_inc(ln_var, 1)
                dve.wait_ge(ln_var, k * TT + TT)
                dve.wait_ge(ln_std, k + 1)
                st.add(v.reciprocal(rstd[:, :], std[:, 0:TT]))
                st.wait()
                if k == 0:
                    st.add(v.tensor_tensor(prod[:, :], mv[:, :, 1], rstd[:, :], ALU.mult))
                    st.wait()
                    v.tensor_tensor(prod[:, :], prod[:, :], rstd[:, :], ALU.mult).then_inc(ln0_vx, 1)
                    dve.wait_ge(ln0_std2, 1)
                    st.add(v.reciprocal(rstd2[:, :], std[:, TT:2 * TT]))
                    st.wait()
                    st.add(v.tensor_tensor(rstd2[:, :], rstd2[:, :], rstd[:, :], ALU.mult))
                    st.wait()
                    for t in range(TT):
                        v.tensor_scalar(XS[:, t, :], H[:, t, :], mv[:, t, 0:1], rstd2[:, t:t + 1], ALU.subtract, ALU.mult).then_inc(ln_x, 1)
                        st.add(v.tensor_scalar(X[:, t, :], H[:, t, :], mv[:, t, 0:1], rstd[:, t:t + 1], ALU.subtract, ALU.mult))
                    return
                for t in range(TT):
                    v.tensor_scalar(X[:, t, :], H[:, t, :], mv[:, t, 0:1], rstd[:, t:t + 1], ALU.subtract, ALU.mult).then_inc(ln_x, 1)

            def log1p_series(e, t, q, p, s):
                st.add(v.tensor_scalar(t, e, 2.0, None, ALU.add))
                st.wait()
                st.add(v.reciprocal(t, t))
                st.wait()
                st.add(v.tensor_tensor(s, e, t, ALU.mult))
                st.wait()
                st.add(v.tensor_tensor(q, s, s, ALU.mult))
                st.wait()
                st.add(v.tensor_scalar(p, q, 1.0 / 15, None, ALU.mult))
                st.wait()
                for c in (13, 11, 9, 7, 5, 3):
                    st.add(v.scalar_tensor_tensor(out=p, in0=p, scalar=1.0 / c, in1=q, op0=ALU.add, op1=ALU.mult))
                    st.wait()
                st.add(v.scalar_tensor_tensor(out=p, in0=p, scalar=1.0, in1=s, op0=ALU.add, op1=ALU.mult))
                st.wait()
                st.add(v.tensor_scalar(p, p, 2.0, None, ALU.mult))
                st.wait()

            dve.wait_ge(S["const_ready"], 12)
            dve.wait_ge(S["iota_ready"], 2)
            dve.wait_ge(S["ld_tok"], 48)
            st.add(v.tensor_tensor(eq.rearrange("p (b n) -> p b n", n=NX), cur, shf, ALU.is_equal))
            st.wait()
            st.add(v.tensor_tensor_scan(run, ones[0:76, 0:1].to_broadcast([76, NB * NX]), eq, 0.0, ALU.add, ALU.mult))
            st.wait()
            v.tensor_scalar(score, run, 128.0, qcol[0:76, :], ALU.mult, ALU.add).then_inc(S["score_ready"], 1)
            for g in range(2):
                dve.wait_ge(S["scoreT"], g + 1)
                st.add(v.tensor_reduce(best[:, 4 * g:4 * g + 4], bank[2 + g][0:NX, 0:4 * 76].rearrange("p (a b) -> p a b", b=76), AX.X, ALU.max))
            st.wait()
            st.add(v.tensor_scalar(found[:, :], best[:, :], 128.0, None, ALU.is_ge))
            for b in range(NB):
                st.add(v.scalar_tensor_tensor(out=junk[:, b, :], in0=bank[2 + b // 4][0:NX, (b % 4) * 76:(b % 4 + 1) * 76],
                                              scalar=best[:, b:b + 1], in1=nxt[:, b, :], op0=ALU.is_equal, op1=ALU.mult,
                                              accum_out=pick[:, b:b + 1]))
            st.wait()
            v.tensor_copy(ids[:, :], pick[:, :]).then_inc(S["ids_ready"], 1)
            for g in range(2):
                dve.wait_ge(S["img_out"], g + 1)
                v.tensor_tensor(img[:, 2 * g:2 * g + 2, :], bank[g][:, 0:2 * D].rearrange("p (a b) -> p a b", b=D),
                                tokb.unsqueeze(1).to_broadcast([P, 2, D]), ALU.add).then_inc(S["img_ready"], 1)
            dve.wait_ge(S["gathered"], 16 * NB)
            v.tensor_tensor(txt, txt, found[:, :].unsqueeze(2).to_broadcast([NX, NB, D]), ALU.mult).then_inc(S["txt_ready"], 1)

            dve.wait_ge(S["h_loaded"], 32)
            ln(0)
            dve.wait_ge(ln_out, 6)
            v.tensor_copy(XRa[:, 0:T].rearrange("p (b n) -> p b n", n=L), XTa[:, 0:T].rearrange("p (b n) -> p b n", n=L)[:, :, ::-1])\
                .then_inc(S["flipped"], 1)
            v.tensor_copy(XRb[:, 0:T].rearrange("p (b n) -> p b n", n=L), XTb[0:DB, 0:T].rearrange("p (b n) -> p b n", n=L)[:, :, ::-1])\
                .then_inc(S["flipped"], 1)
            XP4 = XP.rearrange("p m (b n) -> p m b n", n=PADL)
            BP4 = bcp.rearrange("p m (b n) -> p m b n", n=PADL)

            def evac(d, c):
                for m in range(3, 7):
                    k = k_inproj(d, c, m)
                    o = bank[INBANK[k % len(INBANK)]]
                    dve.wait_ge(S["inproj"], k + 1)
                    if m < 6:
                        v.tensor_copy(XP4[:, d * KD + m - 3, 2 * c:2 * c + 2, NCONV - 1:PADL],
                                      o[:, 0:2 * L].rearrange("p (b n) -> p b n", n=L)).then_inc(S["x_evac"], 1)
                    else:
                        v.tensor_copy(BP4[:, d, 2 * c:2 * c + 2, NCONV - 1:PADL],
                                      o[0:48, 0:2 * L].rearrange("p (b n) -> p b n", n=L)).then_inc(S["x_evac"], 1)

            def conv_tap(d, m, k):
                n = P if m < 3 else 48
                o = (CV[:, d * KD + m, :] if m < 3 else bcv[:, d, :]).rearrange("p (b n) -> p b n", n=L)
                src = (XP4[:, d * KD + m, :, k:k + L] if m < 3 else BP4[:, d, :, k:k + L])
                if k == 0:
                    dve.wait_ge(S["x_evac"], 16 * (d + 1))
                    st.add(v.tensor_scalar(o, src, convw[0:n, d, m, 0:1], convb[0:n, d, m:m + 1], ALU.mult, ALU.add))
                    return
                st.wait()
                ins = v.scalar_tensor_tensor(out=o, in0=src, scalar=convw[0:n, d, m, k:k + 1], in1=o, op0=ALU.mult, op1=ALU.add)
                if k < NCONV - 1:
                    st.add(ins)
                else:
                    ins.then_inc(S["convolved"], 1)

            def conv(d, m):
                for k in range(NCONV):
                    conv_tap(d, m, k)

            dve.wait_ge(S["padded"], 2)
            dve.wait_ge(S["ld_mamba"], 144)
            for c in range(4):
                evac(0, c)
            for c in range(2):
                evac(1, c)
                conv(0, c)
            dve.wait_ge(S["dt_ready"], 1)
            dve.wait_ge(S["ld_mamba"], 144)
            st.add(v.tensor_tensor(dtv[:, 0:96], bank[4][:, 0:96], dtrow[:, 0:96], ALU.add))
            st.add(v.tensor_tensor(dtv[0:R, 96:192], bank[4][0:R, 96:192], dtrow[0:R, 96:192], ALU.add))
            st.wait()
            v.scalar_tensor_tensor(out=dte[:, :], in0=dtv[:, :], scalar=-1.0, in1=dtv[:, :], op0=ALU.mult, op1=ALU.min).then_inc(S["dt_abs"], 1)
            dve.wait_ge(S["dt_exp"], 1)
            log1p_series(dte[:, :], dtt[:, :], dtq[:, :], dtp[:, :], dts[:, :])
            st.add(v.scalar_tensor_tensor(out=dts[:, :], in0=dtv[:, :], scalar=0.0, in1=dtp[:, :], op0=ALU.max, op1=ALU.add))
            st.wait()
            dve.wait_ge(S["a_exp"], 1)
            v.tensor_tensor(dA[:, :], dts[:, :], alog[:, :], ALU.mult).then_inc(S["dt_arg"], 1)
            dve.wait_ge(S["dA_exp"], 1)
            v.memset(dA[0:1, 0:96], 0.0).then_inc(S["dA_ready"], 1)
            for c in range(2, 4):
                evac(1, c)
                conv(0, c)

            def scan_part(n):
                d, b = ITS[n]
                p = n % 2
                col = DTC(d, b)
                if n:
                    dve.wait_ge(S["m_ready"], 2 * n)
                for g in range(2):
                    dve.wait_ge(S["decay_ready"], 2 * n + g + 1)
                    e = bank[3 + g][:, 0:3 * L].rearrange("p (h n) -> p h n", n=L)
                    st.add(v.tensor_tensor_scan(DD[:, 3 * g:3 * g + 3, :].rearrange("p h n -> p (h n)"), bank[3 + g][:, 0:3 * L], ident3[:, :],
                                                0.0, ALU.mult, ALU.add))
                    v.tensor_copy(dAr[:, 3 * g:3 * g + 3, 1:R], e[0:R, :, P + 1:L]).then_inc(S["decay_used"], 1)
                dve.wait_ge(S["xc_turned"], n + 1)
                v.tensor_tensor(dtx[:, p, :].rearrange("p (h c) -> p h c", c=64), bank[0][:, 0:DIN].rearrange("p (h c) -> p h c", c=64),
                                dts[:, col:col + NH].unsqueeze(2).to_broadcast([P, NH, 64]), ALU.mult).then_inc(S["dtx_ready"], 1)
                v.tensor_tensor(dtxr[:, p, :].rearrange("p (h c) -> p h c", c=64), bank[1][0:R, 0:DIN].rearrange("p (h c) -> p h c", c=64),
                                dts[0:R, 96 + col:96 + col + NH].unsqueeze(2).to_broadcast([R, NH, 64]), ALU.mult).then_inc(S["dtx_ready"], 1)
                dve.wait_ge(S["decay_used"], 2 * n + 2)
                st.add(v.tensor_tensor_scan(DDr[:, :, :].rearrange("p h n -> p (h n)"), dAr[:, :, :].rearrange("p h n -> p (h n)"), identr[:, :],
                                            0.0, ALU.mult, ALU.add))
                st.wait()
                dve.wait_ge(S["g_ready"], n + 1)
                G = bank[2 if p == 0 else 7]
                v.tensor_tensor(MM[:, p, :, :], DD[:, :, :], G[:, 0:L].unsqueeze(1).to_broadcast([P, NH, L]), ALU.mult)\
                    .then_inc(S["m_ready"], 1)
                v.tensor_tensor(MMr[:, p, :, :], DDr[:, :, :], G[0:R, L:L + R].unsqueeze(1).to_broadcast([R, NH, R]), ALU.mult)\
                    .then_inc(S["m_ready"], 1)

            def skip_part(n):
                d, b = ITS[n]
                p = n % 2
                dve.wait_ge(S["y_ready"], n + 1)
                if n >= 2:
                    dve.wait_ge(S["yz_ready"], n - 1)
                for m in range(KD):
                    v.scalar_tensor_tensor(out=w1y[:, p, m, :], in0=xcs[:, p, m, :], scalar=skipd[:, d, m:m + 1],
                                           in1=bank[5 + p][:, m * L:(m + 1) * L], op0=ALU.mult, op1=ALU.add).then_inc(S["yd_ready"], 1)

            def add_squares(d):
                o = SQ[:, d * KD, :]
                dve.wait_ge(S["sq_ready"], d * KD + 2)
                st.add(v.tensor_tensor(o, o, SQ[:, d * KD + 1, :], ALU.add))
                st.wait()
                dve.wait_ge(S["sq_ready"], d * KD + 3)
                v.tensor_tensor(o, o, SQ[:, d * KD + 2, :], ALU.add).then_inc(S["sq_added"], 1)

            for n in range(len(ITS) + 1):
                if n < len(ITS):
                    scan_part(n)
                if n:
                    skip_part(n - 1)
                if n == 12:
                    add_squares(0)
                if n < NB:
                    for k in range(2):
                        conv_tap(1, n // 2, 2 * (n % 2) + k)
            add_squares(1)
            dve.wait_ge(S["ss_std"], 2)
            v.reciprocal(rs[:, 0:2 * TT - 2], rss[:, 0:2 * TT - 2]).then_inc(S["ss_inv"], 1)
            v.reciprocal(rs[0:LAST, 2 * TT - 2:2 * TT], rss[0:LAST, 2 * TT - 2:2 * TT]).then_inc(S["ss_inv"], 1)
            dve.wait_ge(S["ld_q1t"], 32)
            blocks = ((0, DA, XTa), (1, DB, XTb))
            st.add(v.memset(qs[64:P, 9:10], 1.0))
            for c, n, _x in blocks:
                st.add(v.tensor_reduce(qs[0:n, 8 + c:9 + c], qw1t[0:n, c, :], AX.X, ALU.max, apply_absolute_value=True))
            dve.wait_ge(S["ld_q2"], 32)
            for c, n, _x in blocks:
                st.add(v.tensor_reduce(qs[0:n, 36 + c:37 + c], qw2[0:n, c, :], AX.X, ALU.max, apply_absolute_value=True))
            st.wait()
            st.add(v.tensor_scalar(qs[:, 36:38], qs[:, 36:38], 1.0 / 127, QEPS, ALU.mult, ALU.max))
            st.wait()
            st.add(v.reciprocal(qs[:, 38:40], qs[:, 36:38]))
            st.wait()
            for c, n, _x in blocks:
                st.add(v.tensor_scalar(qw2[0:n, c, :], qw2[0:n, c, :], qs[0:n, 38 + c:39 + c], 127.0, ALU.mult, ALU.min))
            st.wait()
            for c, n, _x in blocks:
                st.add(v.tensor_scalar(qw2[0:n, c, :], qw2[0:n, c, :], -128.0, ROUNDER, ALU.max, ALU.add))
            st.wait()
            dve.wait_ge(S["op_ready"], 18)
            for g in range(3):
                n = CM if g < 2 else T - 2 * CM
                dve.wait_ge(S["bt_turned"], g + 1)
                v.tensor_copy(BIr[64:P, 0, g * CM:g * CM + n], bank[5][64:P, 0:n]).then_inc(S["bi_dve"], 1)
                v.tensor_copy(BIr[:, 1, g * CM:g * CM + n], bank[6][:, 0:n]).then_inc(S["bi_dve"], 1)
            dve.wait_ge(S["bi_dve"], 6)
            v.tensor_copy(BI[64:P, 1, :].rearrange("p (b n) -> p b n", n=L), BIr[64:P, 0, :].rearrange("p (b n) -> p b n", n=L)[:, :, ::-1])\
                .then_inc(S["bi_flip"], 1)
            v.tensor_copy(BI[:, 2, :].rearrange("p (b n) -> p b n", n=L), BIr[:, 1, :].rearrange("p (b n) -> p b n", n=L)[:, :, ::-1])\
                .then_inc(S["bi_flip"], 1)
            dve.wait_ge(S["padded"], 3)
            for t in range(TT):
                dve.wait_ge(S["f2_out"], t + 1)
                st.add(v.tensor_tensor(SS[0:rows(t), t, :], G2[0:rows(t), t, :], X[0:rows(t), t, :], ALU.add))
                st.wait()
                st.add(v.bn_stats(stats[:, t, :], SS[:, t, :]))
            st.wait()
            for t in range(TT):
                v.bn_aggr(mv[:, t, :], stats[:, t, :]).then_inc(S["ln2_var"], 1)
            dve.wait_ge(S["ln2_var"], TT)
            dve.wait_ge(S["ln2_std"], 1)
            st.add(v.reciprocal(rstd[:, :], std[:, 0:TT]))
            st.wait()
            for t in range(TT):
                st.add(v.tensor_scalar(SS[:, t, :], SS[:, t, :], mv[:, t, 0:1], rstd[:, t:t + 1], ALU.subtract, ALU.mult))
            st.wait()
            dve.wait_ge(S["ld_mamba"], 144)
            st.add(v.tensor_tensor(SS, SS, ln2w[:, :].unsqueeze(1).to_broadcast([P, TT, D]), ALU.mult))
            st.wait()
            st.add(v.tensor_tensor(SS, SS, ln2b[:, :].unsqueeze(1).to_broadcast([P, TT, D]), ALU.add))
            st.wait()
            st.add(v.tensor_tensor(H[:, 0:TT - 1, :], H[:, 0:TT - 1, :], SS[:, 0:TT - 1, :], ALU.add))
            st.add(v.tensor_tensor(H[0:LAST, TT - 1, :], H[0:LAST, TT - 1, :], SS[0:LAST, TT - 1, :], ALU.add))
            st.wait()

            ln(1)
            for g in range(3):
                for c, n, xt in blocks:
                    dve.wait_ge(ln_out, LN_BASE[1] + 2 * g + c + 1)
                    x = xt[0:n, g * CM:min((g + 1) * CM, T)]
                    st.add(v.tensor_reduce(ham[0:n, 3 * c + g:3 * c + g + 1], x, AX.X, ALU.max))
                    st.add(v.tensor_reduce(ham[0:n, 6 + 3 * c + g:7 + 3 * c + g], x, AX.X, ALU.min))
            st.wait()
            for c, n, xt in blocks:
                st.add(v.tensor_reduce(qs[0:n, c:c + 1], ham[0:n, 3 * c:3 * c + 3], AX.X, ALU.max))
                st.add(v.tensor_reduce(qs[0:n, 2 + c:3 + c], ham[0:n, 6 + 3 * c:9 + 3 * c], AX.X, ALU.min))
            st.wait()
            v.scalar_tensor_tensor(out=qs[:, 4:6], in0=qs[:, 2:4], scalar=-1.0, in1=qs[:, 0:2], op0=ALU.mult, op1=ALU.max).then_inc(S["q_gmax"], 1)
            dve.wait_ge(S["q_sqrt"], 2)
            st.add(v.reciprocal(qs[:, 12:14], qs[:, 10:12]))
            st.wait()
            st.add(v.tensor_tensor(qs[:, 4:6], qs[:, 6:8], qs[:, 12:14], ALU.mult))
            st.wait()
            st.add(v.memset(qs[64:P, 5:6], 1.0))
            st.wait()
            st.add(v.tensor_scalar(qs[:, 6:8].bitcast(U32), qs[:, 4:6].bitcast(U32), 0x7F800000, None, ALU.bitwise_and))
            st.wait()
            st.add(v.scalar_tensor_tensor(out=qs[:, 8:10], in0=qs[:, 6:8], scalar=1.5, in1=qs[:, 4:6], op0=ALU.mult, op1=ALU.is_lt))
            st.wait()
            st.add(v.scalar_tensor_tensor(out=qs[:, 18:20], in0=qs[:, 8:10], scalar=1.0, in1=qs[:, 6:8], op0=ALU.add, op1=ALU.mult))
            st.wait()
            v.tensor_scalar(csdiag[:, 0:DA], ident, qs[:, 18:19], None, ALU.mult).then_inc(S["q_diag"], 1)
            v.tensor_scalar(csdiag[0:DB, DA:D], identw[0:DB, 0:DB], qs[0:DB, 19:20], None, ALU.mult).then_inc(S["q_diag"], 1)
            st.add(v.reciprocal(qs[:, 20:22], qs[:, 18:20]))
            st.wait()
            st.add(v.tensor_tensor(qs[:, 0:2], qs[:, 0:2], qs[:, 20:22], ALU.mult))
            st.add(v.scalar_tensor_tensor(out=qs[:, 2:4], in0=qs[:, 2:4], scalar=-1.0, in1=qs[:, 20:22], op0=ALU.mult, op1=ALU.mult))
            st.wait()
            v.tensor_reduce(qs[:, 14:15], qs[:, 0:2], AX.X, ALU.max).then_inc(S["q_range"], 1)
            v.tensor_reduce(qs[:, 15:16], qs[:, 2:4], AX.X, ALU.max).then_inc(S["q_range"], 1)

            def asym(src, scale, inv, lo, hi):
                st.add(v.tensor_scalar(qs[:, src:src + 2], qs[:, src:src + 2], 0.0, None, ALU.max))
                st.wait()
                st.add(v.tensor_tensor(qs[:, scale:scale + 1], qs[:, src:src + 1], qs[:, src + 1:src + 2], ALU.add))
                st.wait()
                st.add(v.tensor_scalar(qs[:, scale:scale + 1], qs[:, scale:scale + 1], 1.0 / 255, QEPS, ALU.mult, ALU.max))
                st.wait()
                st.add(v.reciprocal(qs[:, inv:inv + 1], qs[:, scale:scale + 1]))
                st.wait()
                st.add(v.tensor_tensor(qs[:, lo:lo + 1], qs[:, src + 1:src + 2], qs[:, inv:inv + 1], ALU.mult))
                st.wait()
                st.add(v.tensor_scalar(qs[:, lo:lo + 1], qs[:, lo:lo + 1], ROUNDER, -ROUNDER, ALU.add, ALU.add))
                st.wait()
                st.add(v.tensor_scalar(qs[:, lo:lo + 1], qs[:, lo:lo + 1], -1.0, ROUNDER, ALU.mult, ALU.add))
                st.wait()
                st.add(v.tensor_scalar(qs[:, hi:hi + 1], qs[:, lo:lo + 1], 255.0, None, ALU.add))
                st.wait()

            for c, n, _x in blocks:
                v.tensor_scalar(q2[0:n, c, :], qw2[0:n, c, :], -ROUNDER, None, ALU.add).then_inc(S["q2_ready"], 1)
            dve.wait_ge(S["q_csb"], 1)
            st.add(v.tensor_copy(csb[:, :], bank[4][:, 0:D]))
            st.wait()
            dve.wait_ge(S["ld_q1"], 16)
            st.add(v.tensor_tensor(qw1, qw1, csb[:, :].unsqueeze(1).to_broadcast([P, KH, D]), ALU.mult))
            dve.wait_ge(S["q_range_all"], 1)
            asym(16, 22, 23, 26, 27)
            v.tensor_tensor(qs[:, 24:26], qs[:, 20:22], qs[:, 23:24].to_broadcast([P, 2]), ALU.mult).then_inc(S["q_fac"], 1)
            st.add(v.tensor_reduce(qs[:, 50:56], qw1, AX.X, ALU.max, apply_absolute_value=True))
            st.wait()
            st.add(v.tensor_scalar(qs[:, 50:56], qs[:, 50:56], 1.0 / 127, QEPS, ALU.mult, ALU.max))
            st.wait()
            st.add(v.reciprocal(qs[:, 56:62], qs[:, 50:56]))
            st.wait()
            for k in range(KH):
                st.add(v.tensor_scalar(qw1[:, k, :], qw1[:, k, :], qs[:, 56 + k:57 + k], 127.0, ALU.mult, ALU.min))
            st.wait()
            st.add(v.tensor_scalar(qw1, qw1, -128.0, ROUNDER, ALU.max, ALU.add))
            st.add(v.tensor_scalar(qs[:, 50:56], qs[:, 50:56], qs[:, 22:23], None, ALU.mult))
            st.wait()
            v.tensor_scalar(q1, qw1, -ROUNDER, None, ALU.add).then_inc(S["q1_ready"], 1)
            for c, n, _x in blocks:
                dve.wait_ge(S["q_u"], c + 1)
                st.add(v.tensor_scalar(UR[0:n, c, :], UR[0:n, c, :], qs[0:n, 26:27], qs[0:n, 27:28], ALU.max, ALU.min))
            st.wait()
            for c, n, _x in blocks:
                v.tensor_scalar(UQ[0:n, c, :], UR[0:n, c, :], -ROUNDER, None, ALU.add).then_inc(S["q_ui"], 1)
            for k in range(KH):
                dve.wait_ge(S["q2_turned"], k + 1)
                v.tensor_copy(q2t[:, k, :], bank[6 + k % 2][:, 0:D]).then_inc(S["q2_out"], 1)
            for k in range(KH):
                dve.wait_ge(S["q1_turned"], k + 1)
                st.add(v.tensor_copy(q1t[:, 0, k * P:(k + 1) * P], bank[6 + k % 2][:, 0:P]))
                v.tensor_copy(q1t[0:DB, 1, k * P:(k + 1) * P], bank[6 + k % 2][0:DB, P:2 * P]).then_inc(S["q1_out"], 1)
            for n in range(3 * KH):
                c, m = divmod(n, KH)
                dve.wait_ge(S["hg_ready"], n + 1)
                st.add(v.tensor_reduce(ham[:, n:n + 1], HG[:, m, c * CH:(c + 1) * CH], AX.X, ALU.max, apply_absolute_value=True))
            st.wait()
            v.tensor_reduce(qs[:, 30:31], ham[:, :], AX.X, ALU.max).then_inc(S["ham_ready"], 1)
            dve.wait_ge(S["ham_all"], 1)
            st.add(v.tensor_scalar(qs[:, 32:33], qs[:, 31:32], 1.0 / 127, QEPS, ALU.mult, ALU.max))
            st.wait()
            st.add(v.tensor_tensor(qs[:, 34:36], qs[:, 36:38], qs[:, 32:33].to_broadcast([P, 2]), ALU.mult))
            v.reciprocal(qs[:, 33:34], qs[:, 32:33]).then_inc(S["hs_ready"], 1)
            for m in range(KH):
                dve.wait_ge(S["hr_ready"], m + 1)
                st.add(v.tensor_scalar(HG[:, m, :], HG[:, m, :], ROUNDER - 128.0, ROUNDER + 127.0, ALU.max, ALU.min))
                st.wait()
                v.tensor_scalar(HQ[:, m, :], HG[:, m, :], -ROUNDER, None, ALU.add).then_inc(S["hi_ready"], 1)
            st.add(v.memset(ham[64:P, 0:12], 0.0))
            st.wait()
            for n in range(6):
                c, m = divmod(n, 2)
                r = DA if m == 0 else DB
                dve.wait_ge(S["ot_ready"], n + 1)
                st.add(v.tensor_reduce(ham[0:r, n:n + 1], OT[0:r, m, c * CH:(c + 1) * CH], AX.X, ALU.max))
                st.add(v.tensor_reduce(ham[0:r, 6 + n:7 + n], OT[0:r, m, c * CH:(c + 1) * CH], AX.X, ALU.min))
            st.wait()
            st.add(v.tensor_reduce(qs[:, 40:41], ham[:, 0:6], AX.X, ALU.max))
            st.add(v.tensor_reduce(qs[:, 41:42], ham[:, 6:12], AX.X, ALU.min))
            st.wait()
            v.tensor_scalar(qs[:, 41:42], qs[:, 41:42], -1.0, None, ALU.mult).then_inc(S["or_ready"], 1)
            dve.wait_ge(S["or_all"], 1)
            asym(42, 45, 46, 48, 49)
            v.tensor_scalar(qs[:, 47:48], qs[:, 45:46], 1.0, None, ALU.mult).then_inc(S["of_ready"], 1)
            for c, n, _x in blocks:
                dve.wait_ge(S["om_ready"], c + 1)
                st.add(v.tensor_scalar(OT[0:n, c, :], OT[0:n, c, :], qs[0:n, 48:49], qs[0:n, 49:50], ALU.max, ALU.min))
                st.wait()
                v.tensor_scalar(OT[0:n, c, :], OT[0:n, c, :], -ROUNDER, qs[0:n, 45:46], ALU.add, ALU.mult).then_inc(S["oq_ready"], 1)
            for t in range(TT):
                dve.wait_ge(S["oq_turned"], t + 1)
                v.tensor_tensor(H[0:rows(t), t, :], H[0:rows(t), t, :], bank[4 + t % 4][0:rows(t), 0:D], ALU.add).then_inc(S["h_ffn"], 1)
            dve.wait_ge(S["h_ffn"], TT)

            ln(2)
            dve.wait_ge(ln_out, LN_BASE[3])
            for k, xt in enumerate((XTa, XTb)):
                last = v.tensor_copy(XL[:, k, :].rearrange("p (b n) -> p b n", n=R),
                                     xt[:, 0:T].rearrange("p (b n) -> p b n", n=L)[:, :, P:L])
                if k:
                    last.then_inc(S["tails_ready"], 1)
                else:
                    st.add(last)

            def subtract_maxima(b, w):
                for g in (2 * w, 2 * w + 1):
                    r, q = GROUPS[g]
                    k = 18 * (b % 2) + 3 * g
                    dve.wait_ge(S["s_mm"], 6 * b + g + 1)
                    sc = bank[SBANK[g]][0:r, 0:q * L].rearrange("p (a b) -> p a b", b=L)
                    st.add(v.tensor_reduce(amx[0:r, k:k + q], sc, AX.X, ALU.max))
                    st.wait()
                    if b >= 2:
                        dve.wait_ge(S["p_turned"], 4 * (b - 1))
                    v.tensor_tensor(PRS[0:r, 6 * (b % 2) + g, 0:q * L].rearrange("p (a b) -> p a b", b=L), sc,
                                    amx[0:r, k:k + q].unsqueeze(2).to_broadcast([r, q, L]), ALU.subtract).then_inc(S["s_sub"], 1)

            def sums(b, w):
                for g in (2 * w, 2 * w + 1):
                    r, q = GROUPS[g]
                    k = 18 * (b % 2) + 3 * g
                    dve.wait_ge(S["s_exp"], 6 * b + g + 1)
                    st.add(v.tensor_reduce(asm[0:r, k:k + q], PRS[0:r, 6 * (b % 2) + g, 0:q * L].rearrange("p (a b) -> p a b", b=L), AX.X, ALU.add))
                st.wait()
                if b >= 2:
                    dve.wait_ge(S["p_norm"], 6 * (b - 1))
                for g in (2 * w, 2 * w + 1):
                    r, q = GROUPS[g]
                    k = 18 * (b % 2) + 3 * g
                    v.reciprocal(arc[0:r, k:k + q], asm[0:r, k:k + q]).then_inc(S["s_sum"], 1)

            def last_keys_out(b, g):
                dve.wait_ge(S["p_turned"], 4 * b + g + 1)
                if b:
                    dve.wait_ge(S["av_mm"], 2 * b)
                v.tensor_copy(PTr[:, 3 * g:3 * g + 3, :], bank[5][0:R, 0:3 * L].rearrange("p (a b) -> p a b", b=L)).then_inc(S["pt_dve"], 1)

            for i in range(NB + 1):
                if i < NB:
                    subtract_maxima(i, 0)
                if i:
                    last_keys_out(i - 1, 0)
                if i < NB:
                    subtract_maxima(i, 1)
                if i:
                    last_keys_out(i - 1, 1)
                if i < NB:
                    sums(i, 0)
                    subtract_maxima(i, 2)
                if i:
                    last_keys_out(i - 1, 2)
                if i < NB:
                    sums(i, 1)
                if i:
                    last_keys_out(i - 1, 3)
                if i < NB:
                    sums(i, 2)
            for t in range(TT):
                dve.wait_ge(S["wo_mm"], t + 1)
                v.tensor_tensor(H[0:rows(t), t, :], H[0:rows(t), t, :], bank[t % 4][0:rows(t), 0:D], ALU.add).then_inc(S["h_att"], 1)
            dve.wait_ge(S["h_att"], TT)

            def clip(g, m):
                w, n = TOK(*ITEMS[g]), g * KH + m
                if n + 2 < STEPS:
                    rest_w(n + 2)
                dve.wait_ge(S["gu_mm"], 2 * n + 1)
                if n >= 3:
                    dve.wait_ge(S["g_silu"], n - 2)
                v.tensor_scalar(GM[:, n % 3, 0:w], bank[2 * (n % 2)][:, 0:w], 10.0, None, ALU.min).then_inc(S["g_min"], 1)
                dve.wait_ge(S["gu_mm"], 2 * n + 2)
                if n >= 3:
                    dve.wait_ge(S["hh_ready"], n - 2)
                v.tensor_scalar(UM[:, n % 3, 0:w], bank[2 * (n % 2) + 1][:, 0:w], 10.0, -10.0, ALU.min, ALU.max).then_inc(S["u_clip"], 1)

            def product(g, m):
                w, n = TOK(*ITEMS[g]), g * KH + m
                dve.wait_ge(S["g_silu"], n + 1)
                dve.wait_ge(S["u_clip"], n + 1)
                if m == 0:
                    dve.wait_ge(S["hh_ready"], n)
                    if g >= 2:
                        dve.wait_ge(S["e_mm"], g - 1)
                v.tensor_tensor(HH[:, g % 2, m * SLOTS:m * SLOTS + w], GS[:, n % 3, 0:w], UM[:, n % 3, 0:w], ALU.mult)\
                    .then_inc(S["hh_ready"], 1)

            def rest_x(g):
                kind, c = ITEMS[g]
                w = TOK(kind, c)
                if kind == "shared":
                    a, b = XTa[:, c * SLOTS:c * SLOTS + w], XTb[0:DB, c * SLOTS:c * SLOTS + w]
                else:
                    o = bank[6 + c % 2]
                    a, b = o[:, 0:SLOTS], o[0:DB, SLOTS:2 * SLOTS]
                dve.wait_ge(S["x_lead"], 2 * (g + 1))
                v.tensor_tensor(XR[g % 2][:, 0:w], a, XH[g % 2][:, 0:w], ALU.subtract).then_inc(S["x_rest"], 1)
                v.tensor_tensor(XB[g % 2][DB:P, 0:w], b, XB[g % 2][0:DB, 0:w], ALU.subtract).then_inc(S["x_rest"], 1)

            def rest_w(n):
                g, m = divmod(n, KH)
                dve.wait_ge(S["w_lead"], n + 1)
                v.tensor_tensor(WL[n % 4][:, :], weights(g)[:, m * BLK:(m + 1) * BLK], WH[n % 4][:, :], ALU.subtract)\
                    .then_inc(S["w_rest"], 1)

            ln(3)
            dve.wait_ge(S["g_mm"], 1)
            st.add(v.tensor_copy(gv[:, :], bank[4][:, 0:TT * NE]))
            st.wait()
            v.scalar_tensor_tensor(out=gn[:, :], in0=gv[:, :], scalar=-1.0, in1=gv[:, :], op0=ALU.mult, op1=ALU.min).then_inc(S["g_dve"], 1)
            rest_x(0)
            rest_w(0)
            rest_w(1)
            clip(0, 0)
            dve.wait_ge(S["g_act"], 1)
            log1p_series(ge[:, :], gt[:, :], gq[:, :], gp[:, :], gs[:, :])
            v.scalar_tensor_tensor(out=gs[:, :], in0=gv[:, :], scalar=0.0, in1=gp[:, :], op0=ALU.max, op1=ALU.add).then_inc(S["g_dve"], 1)
            clip(0, 1)
            dve.wait_ge(S["g_act"], 2)
            dve.wait_ge(S["ld_small"], 96)
            gs3 = gs[:, :].rearrange("p (t e) -> p t e", e=NE)
            st.add(v.tensor_tensor(gr[:, :, :], gs3, gateb[:, :].unsqueeze(1).to_broadcast([P, TT, NE]), ALU.add))
            st.wait()
            for t in range(TT):
                st.add(v.max(top[:, t, :], gr[:, t, :]))
            st.wait()
            for t in range(TT):
                st.add(v.max_index(topi[:, t, :], top[:, t, :], gr[:, t, :]))
            st.wait()
            st.add(v.tensor_copy(topf[:, :, :], topi[:, :, :]))
            st.wait()
            it3 = iota8[:, :].unsqueeze(1).to_broadcast([P, TT, NE])
            st.add(v.tensor_tensor(M1[:, :, :], it3, topf[:, :, 0:1].to_broadcast([P, TT, NE]), ALU.is_equal))
            st.add(v.tensor_tensor(M2[:, :, :], it3, topf[:, :, 1:2].to_broadcast([P, TT, NE]), ALU.is_equal))
            dve.wait_ge(S["const_ready"], 14)
            st.add(v.tensor_scalar(before[:, :], column[:, :], qcol[:, :], None, ALU.is_gt))
            st.add(v.tensor_scalar(valid[:, :], qcol[:, :], float(LAST), None, ALU.is_lt))
            st.add(v.memset(seg[:, :, 1:TT], 1.0))
            st.add(v.memset(seg[:, :, 0:1], 0.0))
            st.wait()
            st.add(v.tensor_tensor(MB[:, :, :], M1[:, :, :], M2[:, :, :], ALU.add))
            st.wait()
            v.tensor_scalar(MB[:, TT - 1, :], MB[:, TT - 1, :], valid[:, 0:1], None, ALU.mult).then_inc(S["picked"], 1)
            clip(0, 2)
            dve.wait_ge(S["picked"], 1)
            st.add(v.tensor_tensor(comb[:, :, :], MB[:, :, :], gs3, ALU.mult))
            st.wait()
            st.add(v.tensor_reduce(csum[:, :], comb[:, :, :], AX.X, ALU.add))
            st.wait()
            st.add(v.tensor_scalar(csum[:, :], csum[:, :], 1e-6, None, ALU.max))
            st.wait()
            st.add(v.reciprocal(csum[:, :], csum[:, :]))
            st.wait()
            st.add(v.tensor_tensor(comb[:, :, :], comb[:, :, :], csum[:, :].unsqueeze(2).to_broadcast([P, TT, NE]), ALU.mult))
            st.wait()
            for k, M in enumerate((M1, M2)):
                st.add(v.tensor_tensor(pk[:, :, :], M[:, :, :], comb[:, :, :], ALU.mult))
                st.wait()
                st.add(v.tensor_reduce(wt[:, k * TT:(k + 1) * TT], pk[:, :, :], AX.X, ALU.add))
                st.wait()

            def assign_slots():
                dve.wait_ge(S["counted"], 1)
                et = lambda x: x.rearrange("p (t e) -> p e t", e=NE)
                flat = lambda x: x.rearrange("p a b -> p (a b)")
                st.add(v.tensor_copy(tot[:, :, :], et(bank[7][:, RT:2 * RT])))
                st.wait()
                st.add(v.tensor_tensor_scan(flat(inc[:, :, :]), flat(seg[:, :, :]), flat(tot[:, :, :]), 0.0, ALU.mult, ALU.add))
                st.wait()
                st.add(v.tensor_scalar(tiles[:, :], inc[:, :, TT - 1], 1.0 / SLOTS, 0.5 - 0.5 / SLOTS, ALU.mult, ALU.add))
                st.add(v.tensor_tensor(slot[:, :, :], inc[:, :, :], tot[:, :, :], ALU.subtract))
                st.wait()
                st.add(v.tensor_scalar(tiles[:, :], tiles[:, :], ROUNDER, None, ALU.add))
                st.add(v.tensor_tensor(slot[:, :, :], slot[:, :, :], et(bank[7][:, 0:RT]), ALU.add))
                st.wait()
                st.add(v.tensor_scalar(tiles[:, :], tiles[:, :], -ROUNDER, None, ALU.add))
                st.wait()
                st.add(v.tensor_tensor_scan(upto[:, :], ones[:, 0:NE], tiles[:, :], 0.0, ALU.mult, ALU.add))
                st.wait()
                st.add(v.tensor_tensor(tiles[:, :], upto[:, :], tiles[:, :], ALU.subtract))
                st.wait()
                st.add(v.scalar_tensor_tensor(out=slot[:, :, :], in0=tiles[:, :].unsqueeze(2).to_broadcast([P, NE, TT]),
                                              scalar=float(SLOTS), in1=slot[:, :, :], op0=ALU.mult, op1=ALU.add))
                st.wait()
                for k, M in enumerate((M1, M2)):
                    st.add(v.tensor_tensor(pk[:, :, :], M[:, :, :], slot[:, :, :].rearrange("p e t -> p t e"), ALU.mult))
                    st.wait()
                    st.add(v.tensor_reduce(slotf[:, k * TT:(k + 1) * TT], pk[:, :, :], AX.X, ALU.add))
                    st.wait()
                v.tensor_copy(slots[:, :], slotf[:, :]).then_inc(S["slots_ready"], 1)
                st.add(v.tensor_tensor(past[:, :, :], column[:, 0:NTILE].unsqueeze(2).to_broadcast([P, NTILE, NE]),
                                       upto[:, :].unsqueeze(1).to_broadcast([P, NTILE, NE]), ALU.is_ge))
                st.wait()
                st.add(v.tensor_reduce(expf[:, :], past[:, :, :], AX.X, ALU.add))
                st.wait()
                st.add(v.tensor_scalar(expf[:, :], expf[:, :], float(NE - 1), float(P), ALU.min, ALU.mult))
                st.wait()
                st.add(v.tensor_scalar(expf[:, :], expf[:, :], qcol[:, :], None, ALU.add))
                st.wait()
                v.tensor_copy(expert[:, :], expf[:, :]).then_inc(S["slots_ready"], 1)

            for g, (kind, c) in enumerate(ITEMS + [(None, 0)]):
                if kind:
                    for m in range(0 if g else 3, KH):
                        clip(g, m)
                        if on_dve(g) and m:
                            product(g, m - 1)
                        if g == AFTER and m == OUT_AT:
                            rest_x(g + 1)
                    if on_dve(g):
                        product(g, KH - 1)
                    if g != AFTER and g + 1 < len(ITEMS):
                        rest_x(g + 1)
                if g == 0:
                    assign_slots()
                if g and ITEMS[g - 1][0] == "shared":
                    c, k = ITEMS[g - 1][1], SHARED[ITEMS[g - 1][1]]
                    dve.wait_ge(S["e_mm"], g)
                    h = H[:, GCH * c:GCH * c + k, :]
                    v.tensor_tensor(h, h, bank[4 + (g - 1) % 2][:, 0:k * D].rearrange("p (k d) -> p k d", d=D), ALU.add).then_inc(S["s_acc"], 1)
            dve.wait_ge(S["s_acc"], len(SHARED))
            for t in range(TT):
                if t % 3 == 0:
                    dve.wait_ge(y_back[t // 3], 16 * 2 * 3)
                for k in range(2):
                    if k:
                        dve.wait_ge(S["h_moe"], 2 * t + 1)
                    v.scalar_tensor_tensor(out=H[0:rows(t), t, :], in0=YG[0:rows(t), k * TT + t, :], scalar=wt[0:rows(t), k * TT + t:k * TT + t + 1],
                                           in1=H[0:rows(t), t, :], op0=ALU.mult, op1=ALU.add).then_inc(S["h_moe"], 1)


def kernel(**inputs):
    import numpy as np
    import concourse.bacc as bacc
    from concourse.bass_utils import run_bass_kernel_spmd

    a = {k: np.asarray(x) for k, x in inputs.items()}
    f = np.float32

    def both(name):
        return np.stack([a[f"L0_attn_f_{name}"], a[f"L0_attn_b_{name}"]])

    def packed(w):
        gap = np.zeros((D, 16), f)
        return np.concatenate([w[:, 0:784], gap, w[:, 784:800], w[:, 800:806]], 1)

    def taps(w):
        z = np.zeros((16,) + w.shape[1:], f)
        z2 = np.zeros((80,) + w.shape[1:], f)
        return np.concatenate([w[0:400], z, w[400:416], z2]).reshape((4, P) + w.shape[1:])

    dt_bias, a_log = both("dt_bias"), both("A_log")
    heads = lambda x: np.tile(np.repeat(x[:, None, :], NB, 1).reshape(1, -1), (1, 2))
    tiles = lambda w: w.reshape(-1, P, KH, P)
    twice = lambda w: tiles(np.concatenate([w[:, DA:D], w[:, DA:D]], 1))
    w1, w2, w3 = (np.concatenate([a[f"L1_ffn_{n}"], a[f"L1_ffn_{n}s"][None]]) for n in ("w1", "w2", "w3"))
    arrays = {
        "patches": a["x"].reshape(NB, 3, 8, 16, 8, 16).transpose(3, 5, 1, 0, 2, 4).reshape(IN, NB * NI),
        "tok": np.pad(a["x_txt"], ((0, 0), (76, 0)), constant_values=-1),
        "tok_w": a["L0_tok_W"].T, "tok_b": a["L0_tok_b"][None], "emb": a["L0_txt_emb"],
        "ln1": np.stack([a["L0_attn_ln1_w"], a["L0_attn_ln1_b"]], 1),
        "ln2_w": a["L0_attn_ln2_w"][None], "ln2_b": a["L0_attn_ln2_b"][None],
        "in_w": np.stack([packed(a["L0_attn_f_in_w"]), packed(a["L0_attn_b_in_w"])]),
        "dt_bias": heads(dt_bias), "a_log": heads(a_log),
        "conv_w": np.stack([taps(a["L0_attn_f_conv_w"]), taps(a["L0_attn_b_conv_w"])]).transpose(2, 0, 1, 3),
        "conv_b": np.stack([taps(a["L0_attn_f_conv_b"]), taps(a["L0_attn_b_conv_b"])]).transpose(2, 0, 1),
        "skip_d": np.repeat(both("D"), 64, axis=1).reshape(2, KD, P).transpose(2, 0, 1),
        "norm_w": both("norm_w").reshape(2 * KD, P).T, "out_w": both("out_w"),
        "ffn_w1": a["L0_attn_ffn_w1"], "ffn_b1": a["L0_attn_ffn_b1"].reshape(KH, P).T,
        "ffn_w2": a["L0_attn_ffn_w2"], "ffn_b2": a["L0_attn_ffn_b2"][None],
        "q_w1": a["L0_ffn_w1"], "q_w1t": a["L0_ffn_w1"].T, "q_w2": a["L0_ffn_w2"],
        "q_b1": a["L0_ffn_b1"].reshape(KH, P).T, "q_b2": a["L0_ffn_b2"][:, None],
        "w_q": a["L1_attn_w_q"], "w_k": a["L1_attn_w_k"], "w_v": a["L1_attn_w_v"],
        "w_o": a["L1_attn_w_o"], "b_o": a["L1_attn_b_o"][None],
        "gate_w": a["L1_ffn_gate_w"], "gate_b": a["L1_ffn_gate_bias"][None],
        "e_gate_up": np.stack([tiles(w1[:, 0:DA]), tiles(w3[:, 0:DA]), twice(w1), twice(w3)], 3).reshape(-1, 4 * HID),
        "e_down": w2.reshape(-1, KH, P, D).transpose(0, 2, 1, 3).reshape(-1, KH * D),
    }
    nc = bacc.Bacc("TRN2", target_bir_lowering=False, num_devices=1)
    feed, aps = {}, {}
    for name, x in arrays.items():
        x = np.ascontiguousarray(x)
        feed[f"in_{name}"] = x
        aps[name] = nc.dram_tensor(f"in_{name}", x.shape, mybir.dt.from_np(x.dtype), kind="ExternalInput").ap()
    out = nc.dram_tensor("out_0", (NB, L, D), F32, kind="ExternalOutput").ap()
    build(nc, aps, out)
    r = run_bass_kernel_spmd(nc, [feed], core_ids=[0])
    return r.results[0]["out_0"]
```
